# Optimizing a Trainium2 kernel written in Bass

```python
import numpy as np
import jax
import jax.numpy as jnp

def _softmax(x, axis=-1):
    return jax.nn.softmax(x, axis=axis)

def _gelu(x):
    return jax.nn.gelu(x, approximate=True)

def _silu(x):
    return jax.nn.silu(x)

def _sigmoid(x):
    return jax.nn.sigmoid(x)

def _layernorm(x, axis=-1, eps=1e-05):
    m = jnp.mean(x, axis=axis, keepdims=True)
    v = jnp.var(x, axis=axis, keepdims=True)
    return (x - m) / jnp.sqrt(v + eps)

def _scatter_add(tgt, idx, src, axis=0):
    return tgt.at[idx].add(src)

def _segment_sum(src, seg, n):
    return jax.ops.segment_sum(src, seg, n)
kernel_name = 'mk_vit_tower_d1_tok_img256_r4_a0360a'

def setup_inputs(seed: int=0):
    np.random.seed(seed)
    _w = jnp.asarray

    def _rec_inputs():
        import jax
        import jax.numpy as jnp
        _rk = jax.random.key(seed)
        x = -0.000125008 + 0.999885 * jax.random.normal(jax.random.fold_in(_rk, 1), (32, 64, 128, 128), jnp.float32)
        return x
    x = _rec_inputs()

    def _L0_tok_setup():
        import jax, jax.numpy as jnp
        import numpy as np
        D_MODEL = 64
        NHEAD = 8
        DS = 4
        OFFSET_SCALE = 4.0

        def bilinear_sample(fm, pts):
            B, C, H, W = fm.shape
            x = (pts[..., 0] + 1.0) * 0.5 * (W - 1)
            y = (pts[..., 1] + 1.0) * 0.5 * (H - 1)
            x0 = jnp.clip(jnp.floor(x), 0.0, W - 2)
            y0 = jnp.clip(jnp.floor(y), 0.0, H - 2)
            wx = jnp.clip(x - x0, 0.0, 1.0)
            wy = jnp.clip(y - y0, 0.0, 1.0)
            x0i = x0.astype(jnp.int32)
            y0i = y0.astype(jnp.int32)
            fm2 = fm.reshape(B, C, H * W)
            N, P = (pts.shape[1], pts.shape[2])

            def gather(yi, xi):
                idx = (yi * W + xi).reshape(B, N * P)
                g = jnp.take_along_axis(fm2, idx[:, None, :], axis=2)
                return g.reshape(B, C, N, P)
            v00 = gather(y0i, x0i)
            v01 = gather(y0i, x0i + 1)
            v10 = gather(y0i + 1, x0i)
            v11 = gather(y0i + 1, x0i + 1)
            wx_ = wx[:, None]
            wy_ = wy[:, None]
            out = v00 * (1 - wx_) * (1 - wy_) + v01 * wx_ * (1 - wy_) + v10 * (1 - wx_) * wy_ + v11 * wx_ * wy_
            return jnp.moveaxis(out, 1, -1)

        def layer_norm(x, g, b, eps=1e-05):
            mu = jnp.mean(x, axis=-1, keepdims=True)
            var = jnp.var(x, axis=-1, keepdims=True)
            return (x - mu) * jax.lax.rsqrt(var + eps) * g + b

        def reference_points(B, H, W):
            yc = jnp.linspace(-1.0, 1.0, H // DS)
            xc = jnp.linspace(-1.0, 1.0, W // DS)
            yg, xg = jnp.meshgrid(yc, xc, indexing='ij')
            ref = jnp.stack([xg.reshape(-1), yg.reshape(-1)], axis=-1)
            return jnp.broadcast_to(ref[None], (B,) + ref.shape)
        key = jax.random.key(seed)
        ks = jax.random.split(key, 6)
        B, C, H, W = (8, D_MODEL, 128, 128)
        s = 0.05
        return {'feature_map': jax.random.normal(ks[0], (B, C, H, W), jnp.float32), 'W_q': jax.random.normal(ks[1], (C, C), jnp.float32) * s, 'W_k': jax.random.normal(ks[2], (C, C), jnp.float32) * s, 'W_v': jax.random.normal(ks[3], (C, C), jnp.float32) * s, 'W_o1': jax.random.normal(ks[4], (C, C // DS), jnp.float32) * s, 'b_o1': jnp.zeros((C // DS,), jnp.float32), 'ln_g': jnp.ones((C // DS,), jnp.float32), 'ln_b': jnp.zeros((C // DS,), jnp.float32), 'W_o2': jax.random.normal(ks[5], (C // DS, NHEAD * 2), jnp.float32) * s, 'b_o2': jnp.zeros((NHEAD * 2,), jnp.float32)}
    _L0_tok_all = _L0_tok_setup()
    _L0_tok_in = {k: v for k, v in _L0_tok_all.items() if k in ('W_q', 'W_k', 'W_v', 'W_o1', 'b_o1', 'ln_g', 'ln_b', 'W_o2', 'b_o2')}
    del _L0_tok_all

    def _L0_attn_setup():
        import jax, jax.numpy as jnp
        import numpy as np
        DIM = 64
        HEADS = 4
        DIM_HEAD = 32
        NUM_MEM = 4
        HIDDEN = HEADS * DIM_HEAD
        SCALE = DIM_HEAD ** (-0.5)

        def rmsnorm(x, g):
            n = jnp.linalg.norm(x, axis=-1, keepdims=True)
            return x / jnp.maximum(n, 1e-12) * g * x.shape[-1] ** 0.5
        key = jax.random.key(seed)
        ks = jax.random.split(key, 8)
        B, N = (4, 4096)
        return {'x': jax.random.normal(ks[0], (B, N, DIM), jnp.float32), 't': jax.random.normal(ks[1], (B,), jnp.float32), 'w_qkv': jax.random.normal(ks[2], (DIM, 3 * HIDDEN), jnp.float32) * 0.02, 'mem_kv': jax.random.normal(ks[3], (2, HEADS, DIM_HEAD, NUM_MEM), jnp.float32), 'w_out': jax.random.normal(ks[4], (HIDDEN, DIM), jnp.float32) * 0.02, 'b_out': jnp.zeros((DIM,), jnp.float32), 'g_out': jnp.ones((DIM,), jnp.float32), 'g_pre': jnp.ones((DIM,), jnp.float32)}
    _L0_attn_all = _L0_attn_setup()
    _L0_attn_in = {k: v for k, v in _L0_attn_all.items() if k in ('t', 'w_qkv', 'mem_kv', 'w_out', 'b_out', 'g_out', 'g_pre')}
    del _L0_attn_all

    def _L0_ffn_setup():
        import jax, jax.numpy as jnp
        import numpy as np
        B, S, H, F, E, K = (8, 1024, 64, 128, 16, 2)
        EPS = 1e-05
        key = jax.random.key(seed)
        ks = jax.random.split(key, 9)
        sc = 0.02
        return {'x': jax.random.normal(ks[0], (B, S, H), dtype=jnp.float32), 'gate_w': jax.random.normal(ks[1], (H, E), dtype=jnp.float32) * sc, 'gate_b': jnp.zeros((E,), dtype=jnp.float32), 'w1': jax.random.normal(ks[2], (E, H, F), dtype=jnp.float32) * sc, 'b1': jnp.zeros((E, F), dtype=jnp.float32), 'w2': jax.random.normal(ks[3], (E, F, H), dtype=jnp.float32) * sc, 'b2': jnp.zeros((E, H), dtype=jnp.float32), 'gamma': jnp.ones((H,), dtype=jnp.float32), 'beta': jnp.zeros((H,), dtype=jnp.float32)}
    _L0_ffn_all = _L0_ffn_setup()
    _L0_ffn_in = {k: v for k, v in _L0_ffn_all.items() if k in ('gate_w', 'gate_b', 'w1', 'b1', 'w2', 'b2', 'gamma', 'beta')}
    del _L0_ffn_all
    return {'x': x, 'L0_tok_W_q': _L0_tok_in['W_q'], 'L0_tok_W_k': _L0_tok_in['W_k'], 'L0_tok_W_v': _L0_tok_in['W_v'], 'L0_tok_W_o1': _L0_tok_in['W_o1'], 'L0_tok_b_o1': _L0_tok_in['b_o1'], 'L0_tok_ln_g': _L0_tok_in['ln_g'], 'L0_tok_ln_b': _L0_tok_in['ln_b'], 'L0_tok_W_o2': _L0_tok_in['W_o2'], 'L0_tok_b_o2': _L0_tok_in['b_o2'], 'L0_attn_t': _L0_attn_in['t'], 'L0_attn_w_qkv': _L0_attn_in['w_qkv'], 'L0_attn_mem_kv': _L0_attn_in['mem_kv'], 'L0_attn_w_out': _L0_attn_in['w_out'], 'L0_attn_b_out': _L0_attn_in['b_out'], 'L0_attn_g_out': _L0_attn_in['g_out'], 'L0_attn_g_pre': _L0_attn_in['g_pre'], 'L0_ffn_gate_w': _L0_ffn_in['gate_w'], 'L0_ffn_gate_b': _L0_ffn_in['gate_b'], 'L0_ffn_w1': _L0_ffn_in['w1'], 'L0_ffn_b1': _L0_ffn_in['b1'], 'L0_ffn_w2': _L0_ffn_in['w2'], 'L0_ffn_b2': _L0_ffn_in['b2'], 'L0_ffn_gamma': _L0_ffn_in['gamma'], 'L0_ffn_beta': _L0_ffn_in['beta']}

def reference(x, L0_tok_W_q, L0_tok_W_k, L0_tok_W_v, L0_tok_W_o1, L0_tok_b_o1, L0_tok_ln_g, L0_tok_ln_b, L0_tok_W_o2, L0_tok_b_o2, L0_attn_t, L0_attn_w_qkv, L0_attn_mem_kv, L0_attn_w_out, L0_attn_b_out, L0_attn_g_out, L0_attn_g_pre, L0_ffn_gate_w, L0_ffn_gate_b, L0_ffn_w1, L0_ffn_b1, L0_ffn_w2, L0_ffn_b2, L0_ffn_gamma, L0_ffn_beta):
    import jax
    import jax.numpy as jnp

    def _L0_tok_ref(feature_map, W_q, W_k, W_v, W_o1, b_o1, ln_g, ln_b, W_o2, b_o2):
        import jax, jax.numpy as jnp
        import numpy as np
        D_MODEL = 64
        NHEAD = 8
        DS = 4
        OFFSET_SCALE = 4.0

        def bilinear_sample(fm, pts):
            B, C, H, W = fm.shape
            x = (pts[..., 0] + 1.0) * 0.5 * (W - 1)
            y = (pts[..., 1] + 1.0) * 0.5 * (H - 1)
            x0 = jnp.clip(jnp.floor(x), 0.0, W - 2)
            y0 = jnp.clip(jnp.floor(y), 0.0, H - 2)
            wx = jnp.clip(x - x0, 0.0, 1.0)
            wy = jnp.clip(y - y0, 0.0, 1.0)
            x0i = x0.astype(jnp.int32)
            y0i = y0.astype(jnp.int32)
            fm2 = fm.reshape(B, C, H * W)
            N, P = (pts.shape[1], pts.shape[2])

            def gather(yi, xi):
                idx = (yi * W + xi).reshape(B, N * P)
                g = jnp.take_along_axis(fm2, idx[:, None, :], axis=2)
                return g.reshape(B, C, N, P)
            v00 = gather(y0i, x0i)
            v01 = gather(y0i, x0i + 1)
            v10 = gather(y0i + 1, x0i)
            v11 = gather(y0i + 1, x0i + 1)
            wx_ = wx[:, None]
            wy_ = wy[:, None]
            out = v00 * (1 - wx_) * (1 - wy_) + v01 * wx_ * (1 - wy_) + v10 * (1 - wx_) * wy_ + v11 * wx_ * wy_
            return jnp.moveaxis(out, 1, -1)

        def layer_norm(x, g, b, eps=1e-05):
            mu = jnp.mean(x, axis=-1, keepdims=True)
            var = jnp.var(x, axis=-1, keepdims=True)
            return (x - mu) * jax.lax.rsqrt(var + eps) * g + b

        def reference_points(B, H, W):
            yc = jnp.linspace(-1.0, 1.0, H // DS)
            xc = jnp.linspace(-1.0, 1.0, W // DS)
            yg, xg = jnp.meshgrid(yc, xc, indexing='ij')
            ref = jnp.stack([xg.reshape(-1), yg.reshape(-1)], axis=-1)
            return jnp.broadcast_to(ref[None], (B,) + ref.shape)
        B, C, H, W = feature_map.shape
        dh = C // NHEAD
        ref = reference_points(B, H, W)
        Nq = ref.shape[1]
        q_feat = bilinear_sample(feature_map, ref[:, :, None, :])[:, :, 0]
        queries = q_feat @ W_q.T
        h = jax.nn.gelu(layer_norm(q_feat @ W_o1 + b_o1, ln_g, ln_b))
        off = (h @ W_o2 + b_o2).reshape(B, Nq, NHEAD, 2) * OFFSET_SCALE
        scale = jnp.array([2.0 / (W - 1), 2.0 / (H - 1)], jnp.float32)
        sampling_points = ref[:, :, None, :] + off * scale
        sampled = bilinear_sample(feature_map, sampling_points)
        keys = jnp.einsum('bnpc,dc->bnpd', sampled, W_k)
        values = jnp.einsum('bnpc,dc->bnpd', sampled, W_v)
        q = queries.reshape(B, Nq, NHEAD, dh)
        k = keys.reshape(B, Nq, NHEAD, NHEAD, dh)
        v = values.reshape(B, Nq, NHEAD, NHEAD, dh)
        scores = jnp.einsum('bnhd,bnphd->bnhp', q, k) / jnp.sqrt(jnp.float32(dh))
        attn = jax.nn.softmax(scores, axis=-1)
        out = jnp.einsum('bnhp,bnphd->bnhd', attn, v).reshape(B, Nq, C)
        return out

    def _L0_attn_ref(x, t, w_qkv, mem_kv, w_out, b_out, g_out, g_pre):
        import jax, jax.numpy as jnp
        import numpy as np
        DIM = 64
        HEADS = 4
        DIM_HEAD = 32
        NUM_MEM = 4
        HIDDEN = HEADS * DIM_HEAD
        SCALE = DIM_HEAD ** (-0.5)

        def rmsnorm(x, g):
            n = jnp.linalg.norm(x, axis=-1, keepdims=True)
            return x / jnp.maximum(n, 1e-12) * g * x.shape[-1] ** 0.5
        b, n, c = x.shape
        xn = rmsnorm(x, g_pre)
        qkv = xn @ w_qkv
        q, k, v = jnp.split(qkv, 3, axis=-1)

        def to_heads(z):
            return z.reshape(b, n, HEADS, DIM_HEAD).transpose(0, 2, 3, 1)
        q, k, v = map(to_heads, (q, k, v))
        mk = jnp.broadcast_to(mem_kv[0], (b, HEADS, DIM_HEAD, NUM_MEM))
        mv = jnp.broadcast_to(mem_kv[1], (b, HEADS, DIM_HEAD, NUM_MEM))
        k = jnp.concatenate([mk, k], axis=-1)
        v = jnp.concatenate([mv, v], axis=-1)
        q = jax.nn.softmax(q, axis=-2) * SCALE
        k = jax.nn.softmax(k, axis=-1)
        context = jnp.einsum('bhdn,bhen->bhde', k, v)
        out = jnp.einsum('bhde,bhdn->bhen', context, q)
        out = out.transpose(0, 3, 1, 2).reshape(b, n, HIDDEN)
        out = rmsnorm(out @ w_out + b_out, g_out)
        return out + x

    def _L0_ffn_ref(x, gate_w, gate_b, w1, b1, w2, b2, gamma, beta):
        import jax, jax.numpy as jnp
        import numpy as np
        B, S, H, F, E, K = (8, 1024, 64, 128, 16, 2)
        EPS = 1e-05
        gate_logits = x @ gate_w + gate_b
        topk_vals, topk_idx = jax.lax.top_k(gate_logits, K)
        topk_w = jax.nn.softmax(topk_vals, axis=-1)
        h = jax.nn.relu(jnp.einsum('bsh,ehf->bsef', x, w1) + b1)
        expert_out = jnp.einsum('bsef,efh->bseh', h, w2) + b2
        sel = jnp.take_along_axis(expert_out, topk_idx[:, :, :, None], axis=2)
        moe = jnp.sum(topk_w[..., None] * sel, axis=2)
        y = x + moe
        mu = jnp.mean(y, axis=-1, keepdims=True)
        var = jnp.var(y, axis=-1, keepdims=True)
        return (y - mu) / jnp.sqrt(var + EPS) * gamma + beta
    h = _L0_tok_ref(x, L0_tok_W_q, L0_tok_W_k, L0_tok_W_v, L0_tok_W_o1, L0_tok_b_o1, L0_tok_ln_g, L0_tok_ln_b, L0_tok_W_o2, L0_tok_b_o2)
    h = h + _L0_attn_ref(_layernorm(h, axis=-1), L0_attn_t, L0_attn_w_qkv, L0_attn_mem_kv, L0_attn_w_out, L0_attn_b_out, L0_attn_g_out, L0_attn_g_pre)
    h = h + _L0_ffn_ref(_layernorm(h, axis=-1), L0_ffn_gate_w, L0_ffn_gate_b, L0_ffn_w1, L0_ffn_b1, L0_ffn_w2, L0_ffn_b2, L0_ffn_gamma, L0_ffn_beta)
    return h

_drawn_inputs = setup_inputs


def setup_inputs(seed=0):
    import zlib

    import numpy as np

    out = dict(_drawn_inputs(seed))
    spreads = {'L0_tok_b_o1': (0.0, 0.1),
     'L0_tok_ln_g': (1.0, 0.2),
     'L0_tok_ln_b': (0.0, 0.1),
     'L0_tok_b_o2': (0.0, 0.1),
     'L0_attn_b_out': (0.0, 0.1),
     'L0_attn_g_out': (1.0, 0.2),
     'L0_attn_g_pre': (1.0, 0.6),
     'L0_ffn_gate_b': (0.0, 0.267),
     'L0_ffn_b1': (0.0, 0.8),
     'L0_ffn_b2': (0.0, 0.289),
     'L0_ffn_gamma': (1.0, 0.2),
     'L0_ffn_beta': (0.0, 0.1)}
    factors = {'L0_attn_w_qkv': 8.0,
     'L0_attn_mem_kv': 8.0,
     'L0_attn_w_out': 8.0,
     'L0_ffn_w1': 8.0,
     'L0_ffn_w2': 7.022}
    for name, (base, spread) in spreads.items():
        noise = np.random.default_rng([zlib.crc32(name.encode()), seed]).standard_normal(out[name].shape)
        drawn = base * np.exp(spread * noise) if base else spread * noise
        out[name] = jnp.asarray(drawn.astype(out[name].dtype))
    for name, factor in factors.items():
        out[name] = (out[name] * factor).astype(out[name].dtype)
    return out
```

```python
import math
from contextlib import ExitStack

import numpy as np
import concourse.bass as bass
from concourse import mybir
from concourse.alu_op_type import AluOpType as ALU

FP32 = mybir.dt.float32
I32 = mybir.dt.int32
ACT = mybir.ActivationFunctionType
AX = mybir.AxisListType.X

B, C, H, W = 32, 64, 128, 128
PAIRS = B // 2
DS = 4
QR = H // DS
NQ = QR * QR
TILES = NQ // 128
PT, DH = 8, 8
O1 = C // DS
CHUNKS, CROWS = 8, H // 8
QCOLS = NQ // CHUNKS
GROUPS = CROWS // 4
XA_USES = CHUNKS * (GROUPS + 1)
HEADS, HD, MEM = 4, 32, 4
HID = HEADS * HD
E, F = 16, 128
MAPROWS = H - 1
IMGROWS = MAPROWS * W
STORES = 16 * CHUNKS
EPS = 1e-5
LN_SCALE = float(2 ** 18)
FLOOR = float(3 * 2 ** 22)
GSLOTS = 4
BIG = 3.0e38


def build(nc, x, interp, ref, ident, headmask, descend, wqT, wkT, wvT, wo1, bo1, lng, lnb, wo2, bo2,
          wqkv_in, mk_in, mvT_in, wout_in, bout_in, gout_in, gpre_in, gatew, gateb, w1_in, b1_in, w2_in, b2_in,
          gamma_in, beta_in, corner_maps, out):
    ctx = ExitStack()
    with ctx:
        def sb(name, shape, dt=FP32):
            return ctx.enter_context(nc.sbuf_tensor(name, shape, dt))

        def pb(name, cols):
            return ctx.enter_context(nc.psum_tensor(name, [128, cols], FP32))

        def sem(name):
            return ctx.enter_context(nc.semaphore(name))

        interp_sb = sb("interp_sb", [128, 2 * QR * QR])
        ref_sb = sb("ref_sb", [128, TILES * 2])
        id_sb = sb("id_sb", [128, 128])
        mask_sb = sb("mask_sb", [128, 128])
        desc_sb = sb("desc_sb", [128, E])
        wqo = sb("wqo", [128, 160])
        wkv = sb("wkv", [128, 256])
        wo2bd = sb("wo2bd", [128, 128])
        bo1_sb = sb("bo1_sb", [128, O1])
        lng_sb = sb("lng_sb", [128, O1])
        lnb_sb = sb("lnb_sb", [128, O1])
        bo2_sb = sb("bo2_sb", [128, 2 * PT])
        base = sb("base", [128, 2 * TILES, 2 * PT])
        gbase = sb("gbase", [128, 2 * TILES])
        wqkv = sb("wqkv", [C + 1, 3 * HID])
        gpre = sb("gpre", [C, 1])
        mk_sb = sb("mk_sb", [128, MEM])
        mkmax = sb("mkmax", [128, 1])
        mvT = sb("mvT", [MEM, HID])
        wout = sb("wout", [HID, C])
        bout = sb("bout", [128, C])
        gout = sb("gout", [128, C])
        gate_aug = sb("gate_aug", [C + 1, E])
        w1 = sb("w1", [C + 1, E * F])
        w2 = sb("w2", [F, E * C])
        b2bd = sb("b2bd", [128, TILES * C])
        gamma = sb("gamma", [128, C])
        beta = sb("beta", [128, C])
        ones = sb("ones", [128, 1])

        img = [sb(f"img{b}", [128, CROWS * W]) for b in range(2)]
        rows = [sb(f"rows{b}", [128, 2, CROWS + 1, C]) for b in range(2)]
        qfT = sb("qfT", [128, NQ])

        q_sb = sb("q_sb", [128, 2, TILES, C])
        o1 = sb("o1", [128, 2 * TILES, O1])
        oc = sb("oc", [128, 2 * TILES, O1])
        os_ = sb("os_", [128, 2 * TILES, O1])
        st16 = sb("st16", [128, 6, 2 * TILES])
        hT = sb("hT", [128, 256])
        px = sb("px", [128, 2 * TILES * PT, 2])
        fl = sb("fl", [128, 2 * TILES * PT, 2])
        wt = sb("wt", [128, 2, 2 * TILES * PT, 2])
        idxf = sb("idxf", [128, 2 * TILES, PT])
        idx = sb("idx", [128, 2 * TILES, PT], I32)
        w4 = sb("w4", [128, 2 * TILES * PT, 2, 2])
        gath = [sb(f"gath{s}", [128, PT, 4 * C]) for s in range(GSLOTS)]
        samp = [sb(f"samp{b}", [128, PT * C]) for b in range(2)]
        sampT = [sb(f"sampT{b}", [128, PT * C]) for b in range(2)]
        prod = sb("prod", [128, PT * C])
        v_sb = [sb(f"v_sb{b}", [128, 4, PT * C]) for b in range(2)]
        sc = sb("sc", [128, 4, PT, DH])
        scm = sb("scm", [128, 4, 2, DH])
        h0 = sb("h0", [128, TILES, C])

        cen = sb("cen", [128, TILES, C])
        sq = sb("sq", [128, TILES, C])
        xln = sb("xln", [128, TILES, C])
        xn = sb("xn", [128, TILES, C])
        st8 = sb("st8", [128, 8, 2, TILES])
        xnT = sb("xnT", [C + 1, NQ])
        mx = sb("mx", [128, 4])
        d33 = sb("d33", [128, 33])
        emem = sb("emem", [MEM, HID])
        ek = sb("ek", [128, TILES, HID])
        va = sb("va", [128, TILES, HID])
        qs = sb("qs", [128, TILES * HEADS, HD])
        qst = sb("qst", [128, 3, TILES * HEADS])
        qnT = sb("qnT", [128, NQ])
        cm = sb("cm", [128, 128])
        rs = sb("rs", [128, 2])
        ms = sb("ms", [128, C])
        h1 = [sb(f"h1_{j}", [128, TILES, C]) for j in range(2)]
        x2 = xn
        x2T = [sb(f"x2T{j}", [C + 1, NQ]) for j in range(2)]
        lg = sb("lg", [128, 4, TILES, E])
        tk = sb("tk", [128, 8, TILES])
        gates = [sb(f"gates{j}", [128, TILES, E]) for j in range(2)]
        gT = sb("gT", [128, 128])
        ybase = [sb(f"ybase{j}", [128, TILES, C]) for j in range(2)]

        hid = [sb(f"hid{b}", [128, 4 * F]) for b in range(2)]
        yprod = sb("yprod", [128, E, C])
        moe = sb("moe", [128, TILES, C])
        fst = sb("fst", [128, 6, TILES])
        fc, fsq = cen, sq
        outb = sb("outb", [128, TILES, C])

        xa = [pb(f"xa{b}", 512) for b in range(2)]
        kp = pb("kp", 512)
        vp = pb("vp", 512)
        st = pb("st", 512)
        wb = [pb(f"wb{b}", 512) for b in range(3)]

        consts_in = sem("consts_in")
        consts_ready = sem("consts_ready")
        xa_filled = sem("xa_filled")
        xa_emptied = sem("xa_emptied")
        seam_copied = sem("seam_copied")
        qo_filled = sem("qo_filled")
        q_taken = sem("q_taken")
        o1_taken = sem("o1_taken")
        o1_var = sem("o1_var")
        o1_seed = sem("o1_seed")
        gelu_in = sem("gelu_in")
        gelu_exp = sem("gelu_exp")
        h_ready = sem("h_ready")
        hT_filled = sem("hT_filled")
        hT_taken = sem("hT_taken")
        off_filled = sem("off_filled")
        off_read = sem("off_read")
        idx_ready = sem("idx_ready")
        summed = sem("summed")
        st_filled = sem("st_filled")
        st_taken = sem("st_taken")
        k_filled = sem("k_filled")
        v_filled = sem("v_filled")
        k_used = sem("k_used")
        v_copied = sem("v_copied")
        score_ready = sem("score_ready")
        score_exp = sem("score_exp")
        av_read = sem("av_read")
        pool_step = sem("pool_step")
        xn_ready = sem("xn_ready")
        xnT_filled = sem("xnT_filled")
        xnT_taken = sem("xnT_taken")
        kt_filled = sem("kt_filled")
        d33_ready = sem("d33_ready")
        d33T_filled = sem("d33T_filled")
        em_done = sem("em_done")
        krow_done = sem("krow_done")
        q_filled = sem("q_filled")
        kva_filled = sem("kva_filled")
        ek_done = sem("ek_done")
        va_done = sem("va_done")
        qmax_done = sem("qmax_done")
        eq_done = sem("eq_done")
        qn_ready = sem("qn_ready")
        qnT_filled = sem("qnT_filled")
        qnT_taken = sem("qnT_taken")
        ctx_filled = sem("ctx_filled")
        cm_ready = sem("cm_ready")
        m_filled = sem("m_filled")
        ms_ready = sem("ms_ready")
        o_filled = sem("o_filled")
        c_var = sem("c_var")
        c_seed = sem("c_seed")
        o_var = sem("o_var")
        o_seed = sem("o_seed")
        l_var = sem("l_var")
        l_seed = sem("l_seed")
        x2_ready = sem("x2_ready")
        x2T_filled = sem("x2T_filled")
        x2T_taken = sem("x2T_taken")
        gate_filled = sem("gate_filled")
        top_exp_in = sem("top_exp_in")
        top_exp = sem("top_exp")
        gates_ready = sem("gates_ready")
        gT_filled = sem("gT_filled")
        gT_taken = sem("gT_taken")
        b2_filled = sem("b2_filled")
        c_done = sem("c_done")
        h_filled = sem("h_filled")
        h_relu = sem("h_relu")
        y_filled = sem("y_filled")
        quad_used = sem("quad_used")
        y_taken = sem("y_taken")
        f_var = sem("f_var")
        f_seed = sem("f_seed")
        out_ready = sem("out_ready")
        out_stored = sem("out_stored")
        dve_chain = sem("dve_chain")
        act_chain = sem("act_chain")
        sp_step = sem("sp_step")
        dve_step = sem("dve_step")
        stored = [sem(f"stored{b}") for b in range(2)]
        img_loaded = [sem(f"img_loaded{b}") for b in range(2)]
        gathered = [sem(f"gathered{s}") for s in range(GSLOTS)]
        block = ctx.enter_context(nc.Block())


        def past(n, per, c):
            return not isinstance(n, int) or n * per + c > 0


        @block.sync
        def _(sp):
            count = [0]

            def const(dst, src):
                sp.dma_start(dst, src).then_inc(consts_in, 16)
                count[0] += 1

            sp.wait_ge(consts_ready, 1)
            const(id_sb[:, :], ident)
            const(interp_sb[:, :], interp)
            const(ref_sb[:, :], ref)
            const(mask_sb[:, :], headmask)
            const(desc_sb[:, :], descend)
            for j in range(2):
                const(wqo[j * C:(j + 1) * C, j * C:(j + 1) * C], wqT)
                const(wqo[j * C:(j + 1) * C, 2 * C + j * O1:2 * C + (j + 1) * O1], wo1)
                const(wkv[j * C:(j + 1) * C, j * C:(j + 1) * C], wkT)
                const(wkv[j * C:(j + 1) * C, (2 + j) * C:(3 + j) * C], wvT)
            for t in range(TILES):
                const(wo2bd[t * O1:(t + 1) * O1, t * 16:(t + 1) * 16], wo2)
                const(b2bd[t * E:(t + 1) * E, t * C:(t + 1) * C], b2_in)
            for dst, src, n in ((bo1_sb, bo1, O1), (lng_sb, lng, O1), (lnb_sb, lnb, O1), (bo2_sb, bo2, 2 * PT),
                                (bout, bout_in, C), (gout, gout_in, C), (gamma, gamma_in, C), (beta, beta_in, C)):
                const(dst[:, :], src.rearrange("(a n) -> a n", a=1).to_broadcast([128, n]))
            const(wqkv[0:C, :], wqkv_in)
            const(gpre[:, :], gpre_in.rearrange("(n a) -> n a", a=1))
            const(mk_sb[:, :], mk_in)
            const(mvT[:, :], mvT_in)
            const(wout[:, :], wout_in)
            const(gate_aug[0:C, :], gatew)
            const(gate_aug[C:C + 1, :], gateb.rearrange("(a n) -> a n", a=1))
            const(w1[0:C, :], w1_in)
            const(w1[C:C + 1, :], b1_in.rearrange("(a n) -> a n", a=1))
            const(w2[:, :], w2_in)
            assert 16 * count[0] == NCONST_INC[0], count[0]

            def load(n, k):
                if past(n, XA_USES, (GROUPS + 1) * (k - 2) + GROUPS):
                    sp.wait_ge(xa_filled, n * XA_USES + (GROUPS + 1) * (k - 2) + GROUPS)
                    sp.sem_inc(sp_step, 1)
                sp.dma_start(img[k % 2][:, :],
                             x[bass.ds(n * 128, 128), k * CROWS * W:(k + 1) * CROWS * W]).then_inc(img_loaded[k % 2], 16)

            def store(n, par, k):
                sp.wait_ge(xa_emptied, n * XA_USES + (GROUPS + 1) * k + GROUPS)
                sp.sem_inc(sp_step, 1)
                if past(n, CHUNKS - 1, k):
                    sp.wait_ge(seam_copied, n * (CHUNKS - 1) + k)
                    sp.sem_inc(sp_step, 1)
                if k == 0:
                    if past(n, 2 * TILES, -2 * TILES):
                        sp.wait_ge(summed, n * (2 * TILES) - 2 * TILES)
                        sp.sem_inc(sp_step, 1)
                first = 1 if k == 0 else 0
                for j in range(2):
                    src = rows[k % 2][:, j, first:CROWS + 1, :]
                    src = bass.AP(tensor=src.tensor, offset=(j * (CROWS + 1) + first) * C,
                                  ap=[[2 * (CROWS + 1) * C, 128], [C, CROWS - first], [1, 2 * C]])
                    y0 = k * CROWS - 1 + first
                    dst = corner_maps[par][j * MAPROWS + y0:j * MAPROWS + y0 + CROWS - first]
                    sp.dma_start(dst.rearrange("y x c -> x y c"), src).then_inc(stored[k % 2], 16)

            def map_stage(n, par):
                for k in range(CHUNKS):
                    load(n, k)
                    if k:
                        store(n, par, k - 1)
                store(n, par, CHUNKS - 1)

            def store_out(i, j):
                sp.wait_ge(out_ready, i * 2 + j + 1)
                sp.sem_inc(sp_step, 1)
                sp.dma_start(out[bass.ds(i * 2 + j, 1)].rearrange("a (t p) c -> p (a t) c", p=128),
                             outb[:, :, :]).then_inc(out_stored, 16)

            map_stage(0, 0)
            map_stage(1, 1)
            with sp.Fori(0, PAIRS // 2 - 1) as half:
                for b in range(2):
                    map_stage(half * 2 + (b + 2), b)
                    store_out(half * 2 + b, 0)
                    store_out(half * 2 + b, 1)
            for n in (PAIRS - 2, PAIRS - 1):
                for j in range(2):
                    store_out(n, j)
            sp.wait_ge(out_stored, 16 * 2 * PAIRS)
            for s in stored:
                sp.wait_ge(s, STORES * PAIRS)

        @block.gpsimd
        def _(pool):
            def gather(i, par, g):
                s = g % GSLOTS
                if past(i, 2 * TILES, g + 1 - GSLOTS):
                    pool.wait_ge(summed, i * (2 * TILES) + g + 1 - GSLOTS)
                    pool.sem_inc(pool_step, 1)
                for p in range(PT):
                    pool.indirect_dma_start(
                        gath[s][:, p, :], None, corner_maps[par].rearrange("y x c -> (y x) c"),
                        bass.IndirectOffsetOnAxis(idx[:, g, p:p + 1], 0)).then_inc(gathered[s], 16)

            def body(i, par):
                for s in stored:
                    pool.wait_ge(s, i * STORES + STORES)
                    pool.sem_inc(pool_step, 1)
                pool.wait_ge(idx_ready, i + 1)
                pool.sem_inc(pool_step, 1)
                for g in range(2 * TILES):
                    gather(i, par, g)

            body(0, 0)
            with pool.Fori(0, PAIRS // 2 - 1) as half:
                body(half * 2 + 1, 1)
                body(half * 2 + 2, 0)
            body(PAIRS - 1, 1)

        @block.tensor
        def _(pe):
            mm = nc.tensor.matmul

            def transpose(dst, src):
                return nc.tensor.transpose(dst, src, id_sb[:, :])

            def chunk(n, k):
                pe.wait_ge(img_loaded[k % 2], n * (8 * CHUNKS) + 16 * (k // 2 + 1))
                for g in range(GROUPS + 1):
                    u = (GROUPS + 1) * k + g
                    if past(n, XA_USES, u - 1):
                        pe.wait_ge(xa_emptied, n * XA_USES + u - 1)
                    if g < GROUPS:
                        for r in range(4):
                            y = 4 * g + r
                            last = transpose(xa[u % 2][:, r * 128:(r + 1) * 128], img[k % 2][:, y * W:(y + 1) * W])
                    else:
                        if past(n, XA_USES, u):
                            pe.wait_ge(xa_emptied, n * XA_USES + u)
                        for q in range(CROWS // DS):
                            qy = k * (CROWS // DS) + q
                            y0 = QUERY_ROW[qy] - k * CROWS
                            for j in range(2):
                                for r in range(2):
                                    last = mm(xa[u % 2][j * C:(j + 1) * C, q * QR:(q + 1) * QR],
                                              rows[k % 2][:, j, 1 + y0 + r, :],
                                              interp_sb[:, (2 * qy + r) * QR:(2 * qy + r + 1) * QR],
                                              start=(r == 0), stop=(r == 1))
                    last.then_inc(xa_filled, 1)

            QO = [(kp, 0, 3), (vp, 3, 3), (st, 6, 2)]

            def project_queries(i):
                pe.wait_ge(xa_emptied, i * XA_USES + XA_USES)
                if past(i, 2 * TILES, 0):
                    pe.wait_ge(k_used, i * (2 * TILES))
                if past(i, 2 * TILES, 0):
                    pe.wait_ge(v_copied, i * (2 * TILES))
                if past(i, 2 * TILES, 0):
                    pe.wait_ge(st_taken, i * (2 * TILES))
                for bank, t0, nt in QO:
                    for t in range(nt):
                        last = mm(bank[:, t * 160:(t + 1) * 160], qfT[:, (t0 + t) * 128:(t0 + t + 1) * 128],
                                  wqo[:, :], start=True, stop=True)
                    last.then_inc(qo_filled, 1)
                pe.wait_ge(h_ready, i + 1)
                pe.wait_ge(q_taken, i * 3 + 3)
                for j in range(2):
                    last = transpose(st[:, j * 128:(j + 1) * 128],
                                     os_[:, j * TILES:(j + 1) * TILES, :].rearrange("p t c -> p (t c)"))
                last.then_inc(hT_filled, 1)
                pe.wait_ge(hT_taken, i + 1)
                for j in range(2):
                    last = mm(kp[:, j * 128:(j + 1) * 128], hT[:, j * 128:(j + 1) * 128], wo2bd[:, :], start=True, stop=True)
                last.then_inc(off_filled, 1)
                pe.wait_ge(off_read, i + 1)

            def sample_T(i, g):
                pe.wait_ge(summed, i * (2 * TILES) + g + 1)
                if past(i, 2 * TILES, g):
                    pe.wait_ge(st_taken, i * (2 * TILES) + g)
                for q in range(4):
                    last = transpose(st[:, q * 128:(q + 1) * 128], samp[g % 2][:, q * 128:(q + 1) * 128])
                last.then_inc(st_filled, 1)

            def sample_kv(i, g):
                pe.wait_ge(st_taken, i * (2 * TILES) + g + 1)
                if past(i, 2 * TILES, g):
                    pe.wait_ge(k_used, i * (2 * TILES) + g)
                if past(i, 2 * TILES, g):
                    pe.wait_ge(v_copied, i * (2 * TILES) + g)
                for bank, part, filled in ((kp, 0, k_filled), (vp, 1, v_filled)):
                    for q in range(4):
                        last = mm(bank[:, q * 128:(q + 1) * 128], sampT[g % 2][:, q * 128:(q + 1) * 128],
                                  wkv[:, part * 128:(part + 1) * 128], start=True, stop=True)
                    last.then_inc(filled, 1)

            def attention(i, j):
                pe.wait_ge(xn_ready, i * 2 + j + 1)
                for q in range(4):
                    last = transpose(wb[0][:, q * 128:(q + 1) * 128], xn[:, 2 * q:2 * q + 2, :].rearrange("p t c -> p (t c)"))
                last.then_inc(xnT_filled, 1)
                pe.wait_ge(xnT_taken, i * 4 + 2 * j + 2)
                for h in range(2):
                    mm(wb[1 + h][:, :], wqkv[0:C, HID:2 * HID], xnT[0:C, h * 512:(h + 1) * 512],
                       start=True, stop=True).then_inc(kt_filled, 1)
                pe.wait_ge(d33_ready, i * 2 + j + 1)
                mm(wb[0][0:33, 0:128], d33[:, :], id_sb[:, :], start=True, stop=True).then_inc(d33T_filled, 1)
                pe.wait_ge(krow_done, i * 2 + j + 1)
                pe.wait_ge(em_done, i * 2 + j + 1)
                for h in range(2):
                    if h:
                        if past(i, 4, 2 * j + h):
                            pe.wait_ge(qmax_done, i * 4 + 2 * j + h)
                    for t in range(4 * h, 4 * h + 4):
                        last = mm(wb[0][:, (t % 4) * HID:(t % 4 + 1) * HID], xnT[:, t * 128:(t + 1) * 128], wqkv[:, 0:HID],
                                  start=True, stop=True)
                    last.then_inc(q_filled, 1)
                    for u in range(2 * h, 2 * h + 2):
                        if h:
                            if past(i, 8, 4 * j + u - 1):
                                pe.wait_ge(va_done, i * 8 + 4 * j + u - 1)
                        for t in range(2 * u, 2 * u + 2):
                            last = mm(wb[1 + u % 2][:, (t % 2) * 256:(t % 2 + 1) * 256], xnT[:, t * 128:(t + 1) * 128],
                                      wqkv[:, HID:3 * HID], start=True, stop=True)
                        last.then_inc(kva_filled, 1)
                pe.wait_ge(va_done, i * 8 + 4 * j + 4)
                pe.wait_ge(qmax_done, i * 4 + 2 * j + 2)
                pe.wait_ge(ek_done, i * 8 + 4 * j + 4)
                for t in range(TILES):
                    mm(wb[2][:, 128:129], ek[:, t, :], ones[:, :], start=(t == 0), stop=False)
                mm(wb[2][:, 128:129], emem[:, :], ones[0:MEM, :], start=False, stop=True)
                for t in range(TILES):
                    mm(wb[2][:, 0:128], va[:, t, :], ek[:, t, :], start=(t == 0), stop=False)
                mm(wb[2][:, 0:128], mvT[:, :], emem[:, :], start=False, stop=True).then_inc(ctx_filled, 1)
                pe.wait_ge(qn_ready, i * 2 + j + 1)
                for h in range(2):
                    for q in range(4):
                        t = 4 * h + q
                        last = transpose(wb[h][:, q * 128:(q + 1) * 128],
                                         qs[:, t * HEADS:(t + 1) * HEADS, :].rearrange("p h d -> p (h d)"))
                    last.then_inc(qnT_filled, 1)
                pe.wait_ge(cm_ready, i * 2 + j + 1)
                mm(wb[2][:, 256:256 + C], cm[:, :], wout[:, :], start=True, stop=True).then_inc(m_filled, 1)
                pe.wait_ge(ms_ready, i * 2 + j + 1)
                pe.wait_ge(qnT_taken, i * 4 + 2 * j + 2)
                for t in range(TILES):
                    last = mm(wb[2][:, t * C:(t + 1) * C], qnT[:, t * 128:(t + 1) * 128], ms[:, :], start=True, stop=True)
                last.then_inc(o_filled, 1)
                pe.wait_ge(x2_ready, i * 2 + j + 1)
                for q in range(4):
                    last = transpose(wb[0][:, q * 128:(q + 1) * 128], x2[:, 2 * q:2 * q + 2, :].rearrange("p t c -> p (t c)"))
                last.then_inc(x2T_filled, 1)
                pe.wait_ge(x2T_taken, i * 4 + 2 * j + 2)
                for t in range(TILES):
                    last = mm(wb[1][:, t * E:(t + 1) * E], x2T[j][:, t * 128:(t + 1) * 128], gate_aug[:, :], start=True, stop=True)
                last.then_inc(gate_filled, 1)
                pe.wait_ge(gates_ready, i * 2 + j + 1)
                transpose(wb[2][:, 0:128], gates[j][:, :, :].rearrange("p t e -> p (t e)")).then_inc(gT_filled, 1)
                pe.wait_ge(gT_taken, i * 2 + j + 1)
                mm(wb[0][:, :], gT[:, :], b2bd[:, :], start=True, stop=True).then_inc(b2_filled, 1)
                pe.wait_ge(c_done, i * 2 + j + 1)

            def experts(i, g):
                j, t = g // TILES, g % TILES

                def up(q):
                    u = 4 * g + q
                    if u >= 2:
                        pe.wait_ge(h_relu, i * (8 * TILES) + u - 1)
                    for e in range(4 * q, 4 * q + 4):
                        last = mm(wb[q % 2][:, (e % 4) * F:(e % 4 + 1) * F], w1[:, e * F:(e + 1) * F],
                                  x2T[j][:, t * 128:(t + 1) * 128], start=True, stop=True)
                    last.then_inc(h_filled, 1)

                def down(q):
                    u = 4 * g + q
                    pe.wait_ge(h_relu, i * (8 * TILES) + u + 1)
                    if u >= 2 and q % 2 == 0:
                        pe.wait_ge(y_taken, i * (4 * TILES) + 2 * g + q // 2)
                    for e in range(4 * q, 4 * q + 4):
                        last = mm(wb[2][:, (e % 8) * C:(e % 8 + 1) * C], hid[q % 2][:, (e % 4) * F:(e % 4 + 1) * F],
                                  w2[:, e * C:(e + 1) * C], start=True, stop=True)
                    last.then_inc(quad_used, 1)

                up(0)
                up(1)
                down(0)
                up(2)
                down(1)
                up(3)
                down(2)
                down(3)

            def body(i, first=False, last=False):
                project_queries(i)
                for g in range(2 * TILES):
                    sample_T(i, g)
                    if not first:
                        experts(i - 1, g)
                    sample_kv(i, g)
                    if not last and g % 2 == 1:
                        chunk(i + 1, g // 2)
                    if g % TILES == TILES - 1:
                        attention(i, g // TILES)

            pe.wait_ge(consts_in, NCONST_INC[0])
            pe.wait_ge(consts_ready, 2)
            for k in range(CHUNKS):
                chunk(0, k)
            body(0, first=True)
            with pe.Fori(1, PAIRS - 1) as i:
                body(i)
            body(PAIRS - 1, last=True)
            for g in range(2 * TILES):
                experts(PAIRS - 1, g)

        @block.scalar
        def _(act):
            chain = [0]

            def link(ins):
                chain[0] += 1
                ins.then_inc(act_chain, 1)
                act.wait_ge(act_chain, chain[0])

            def copy(dst, src):
                return nc.scalar.activation(dst, src, ACT.Copy)

            def chunk(n, k):
                if past(n, STORES, 32 * (k // 2)):
                    act.wait_ge(stored[k % 2], n * STORES + 32 * (k // 2))
                if k:
                    if past(n, XA_USES, (GROUPS + 1) * k - 1):
                        act.wait_ge(xa_emptied, n * XA_USES + (GROUPS + 1) * k - 1)
                    copy(rows[k % 2][:, :, 0, :], rows[(k + 1) % 2][:, :, CROWS, :]).then_inc(seam_copied, 1)
                for g in range(GROUPS + 1):
                    u = (GROUPS + 1) * k + g
                    act.wait_ge(xa_filled, n * XA_USES + u + 1)
                    if g < GROUPS:
                        copy(rows[k % 2][:, :, 1 + 4 * g:5 + 4 * g, :].rearrange("p j r c -> p r j c"),
                             xa[u % 2][:, :].rearrange("p (r j c) -> p r j c", r=4, j=2)).then_inc(xa_emptied, 1)
                    else:
                        if past(n, 3, 0):
                            act.wait_ge(qo_filled, n * 3)
                        copy(qfT[:, k * QCOLS:(k + 1) * QCOLS], xa[u % 2][:, 0:QCOLS]).then_inc(xa_emptied, 1)

            def rsqrt_seed(var, seed, src, tmp, dst, per, i, c, scale):
                act.wait_ge(var, i * per + c)
                link(nc.scalar.activation(tmp, src, ACT.Ln, scale=scale))
                nc.scalar.activation(dst, tmp, ACT.Exp, scale=-0.5).then_inc(seed, 1)

            QO = [(kp, 0, 3), (vp, 3, 3), (st, 6, 2)]

            def project_queries(i):
                for n, (bank, t0, nt) in enumerate(QO):
                    act.wait_ge(qo_filled, i * 3 + n + 1)
                    nc.scalar.activation(
                        q_sb[:, :, t0:t0 + nt, :].rearrange("p j t c -> p t j c"),
                        bank[:, 0:nt * 160].rearrange("p (t c) -> p t c", c=160)[:, :, 0:2 * C]
                        .rearrange("p t (j c) -> p t j c", j=2),
                        ACT.Copy, scale=float(DH) ** -0.5).then_inc(q_taken, 1)
                rsqrt_seed(o1_var, o1_seed, st16[:, 2, :], st16[:, 3, :], st16[:, 4, :], 1, i, 1, 1.0)
                act.wait_ge(gelu_in, i + 1)
                nc.scalar.activation(os_[:, :, :], os_[:, :, :], ACT.Exp,
                                     scale=-2.0 * math.sqrt(2.0 / math.pi)).then_inc(gelu_exp, 1)
                act.wait_ge(hT_filled, i + 1)
                copy(hT[:, :], st[:, 0:256]).then_inc(hT_taken, 1)

            def sample_T(i, g):
                act.wait_ge(st_filled, i * (2 * TILES) + g + 1)
                if past(i, 2 * TILES, g - 1):
                    act.wait_ge(v_filled, i * (2 * TILES) + g - 1)
                copy(sampT[g % 2][:, :], st[:, :]).then_inc(st_taken, 1)

            def sample_v(i, g):
                act.wait_ge(v_filled, i * (2 * TILES) + g + 1)
                if past(i, 4, g // 4 - 1):
                    act.wait_ge(av_read, i * 4 + g // 4 - 1)
                copy(v_sb[(g // 4) % 2][:, g % 4, :], vp[:, :]).then_inc(v_copied, 1)

            def softmax_exp(i, q):
                act.wait_ge(score_ready, i * 4 + q + 1)
                nc.scalar.activation(sc[:, :, :, :], sc[:, :, :, :], ACT.Exp).then_inc(score_exp, 1)

            def attention(i, j):
                rsqrt_seed(c_var, c_seed, st8[:, 0, :, :], st8[:, 1, :, :], st8[:, 2, :, :], 2, i, j + 1, LN_SCALE)
                act.wait_ge(xnT_filled, i * 2 + j + 1)
                for par in range(2):
                    copy(xnT[0:C, :].rearrange("c (q a n) -> c q a n", a=2, n=128)[:, :, par, :],
                         wb[0][par * C:(par + 1) * C, :].rearrange("c (q n) -> c q n", n=128)).then_inc(xnT_taken, 1)
                act.wait_ge(d33T_filled, i * 2 + j + 1)
                nc.scalar.activation(emem[:, :], wb[0][0:MEM, 0:128], ACT.Exp).then_inc(em_done, 1)
                copy(wqkv[C:C + 1, HID:2 * HID], wb[0][32:33, 0:128]).then_inc(krow_done, 1)
                for u in range(4):
                    act.wait_ge(kva_filled, i * 8 + 4 * j + u + 1)
                    two = wb[1 + u % 2][:, :].rearrange("p (t a c) -> p t a c", a=2, c=HID)
                    nc.scalar.activation(ek[:, 2 * u:2 * u + 2, :], two[:, :, 0, :], ACT.Exp).then_inc(ek_done, 1)
                    copy(va[:, 2 * u:2 * u + 2, :], two[:, :, 1, :]).then_inc(va_done, 1)
                act.wait_ge(qmax_done, i * 4 + 2 * j + 2)
                nc.scalar.activation(qs[:, :, :], qs[:, :, :], ACT.Exp).then_inc(eq_done, 1)
                for h in range(2):
                    act.wait_ge(qnT_filled, i * 4 + 2 * j + h + 1)
                    copy(qnT[:, h * 512:(h + 1) * 512], wb[h][:, :]).then_inc(qnT_taken, 1)
                rsqrt_seed(o_var, o_seed, st8[:, 3, 0, :], st8[:, 4, 0, :], st8[:, 5, 0, :], 2, i, j + 1, LN_SCALE)
                rsqrt_seed(l_var, l_seed, st8[:, 3, 1, :], st8[:, 4, 1, :], st8[:, 5, 1, :], 2, i, j + 1, LN_SCALE)
                act.wait_ge(x2T_filled, i * 2 + j + 1)
                for par in range(2):
                    copy(x2T[j][0:C, :].rearrange("c (q a n) -> c q a n", a=2, n=128)[:, :, par, :],
                         wb[0][par * C:(par + 1) * C, :].rearrange("c (q n) -> c q n", n=128)).then_inc(x2T_taken, 1)
                act.wait_ge(top_exp_in, i * 2 + j + 1)
                nc.scalar.activation(tk[:, 5, :], tk[:, 4, :], ACT.Exp).then_inc(top_exp, 1)
                act.wait_ge(gT_filled, i * 2 + j + 1)
                copy(gT[:, :], wb[2][:, 0:128]).then_inc(gT_taken, 1)

            def experts(i, g):
                for q in range(4):
                    u = 4 * g + q
                    act.wait_ge(h_filled, i * (8 * TILES) + u + 1)
                    if u >= 2:
                        act.wait_ge(quad_used, i * (8 * TILES) + u - 1)
                    nc.scalar.activation(hid[q % 2][:, :], wb[q % 2][:, :], ACT.Relu).then_inc(h_relu, 1)

            def final_seed(i, j):
                rsqrt_seed(f_var, f_seed, fst[:, 2, :], fst[:, 3, :], fst[:, 4, :], 2, i, j + 1, LN_SCALE)

            def body(i, first=False, last=False):
                project_queries(i)
                for g in range(2 * TILES):
                    sample_T(i, g)
                    if not first:
                        experts(i - 1, g)
                    sample_v(i, g)
                    if not last and g % 2 == 1:
                        chunk(i + 1, g // 2)
                    if g % 4 == 3:
                        softmax_exp(i, g // 4)
                    if g % TILES == TILES - 1:
                        if not first:
                            final_seed(i - 1, g // TILES)
                        attention(i, g // TILES)
                act.sem_clear(act_chain)
                chain[0] = 0

            nc.scalar.preload_act_table_set("natural_log_exp_and_others")
            for k in range(CHUNKS):
                chunk(0, k)
            body(0, first=True)
            with act.Fori(1, PAIRS - 1) as i:
                body(i)
            body(PAIRS - 1, last=True)
            for g in range(2 * TILES):
                experts(PAIRS - 1, g)
                if g % TILES == TILES - 1:
                    final_seed(PAIRS - 1, g // TILES)

        @block.vector
        def _(dve):
            V = nc.vector
            chain = [0]

            def link(ins):
                chain[0] += 1
                ins.then_inc(dve_chain, 1)
                dve.wait_ge(dve_chain, chain[0])

            def tt(out_, a, b, op):
                return V.tensor_tensor(out_, a, b, op)

            def refine(r, seed, h, u, a, scale):
                link(V.tensor_scalar(h, a, -0.5, None, ALU.mult))
                link(V.tensor_scalar(r, seed, scale ** 0.5, None, ALU.mult))
                link(tt(u, r, r, ALU.mult))
                link(tt(u, u, h, ALU.mult))
                link(V.scalar_tensor_tensor(r, u, 1.5, r, ALU.add, ALU.mult))

            def bc(ap, n):
                return ap.unsqueeze(2).to_broadcast([ap.shape[0], ap.shape[1], n])

            def bc_mid(ap, n):
                return ap.unsqueeze(1).to_broadcast([ap.shape[0], n, ap.shape[1]])

            def centred(src, cen_, sq_, s, v, n):
                link(V.reduce_sum(s, src, AX))
                link(V.scalar_tensor_tensor(cen_, bc(s, n), -1.0 / n, src, ALU.mult, ALU.add))
                link(tt(sq_, cen_, cen_, ALU.mult))
                link(V.reduce_sum(v, sq_, AX))

            QO = [(kp, 0, 3), (vp, 3, 3), (st, 6, 2)]

            def project_queries(i):
                for n, (bank, t0, nt) in enumerate(QO):
                    dve.wait_ge(q_taken, i * 3 + n + 1)
                    link(tt(o1[:, :, :].rearrange("p (j t) c -> p t j c", j=2)[:, t0:t0 + nt, :, :],
                            bank[:, 0:nt * 160].rearrange("p (t c) -> p t c", c=160)[:, :, 2 * C:160]
                            .rearrange("p t (j c) -> p t j c", j=2),
                            bo1_sb[:, :].unsqueeze(1).unsqueeze(1).to_broadcast([128, nt, 2, O1]), ALU.add))
                centred(o1[:, :, :], oc[:, :, :], os_[:, :, :], st16[:, 0, :], st16[:, 1, :], O1)
                V.tensor_scalar(st16[:, 2, :], st16[:, 1, :], 1.0 / O1, EPS, ALU.mult, ALU.add).then_inc(o1_var, 1)
                dve.wait_ge(o1_seed, i + 1)
                refine(st16[:, 5, :], st16[:, 4, :], st16[:, 0, :], st16[:, 1, :], st16[:, 2, :], 1.0)
                link(tt(oc[:, :, :], oc[:, :, :], bc(st16[:, 5, :], O1), ALU.mult))
                link(tt(oc[:, :, :], oc[:, :, :], bc_mid(lng_sb[:, :], 2 * TILES), ALU.mult))
                link(tt(oc[:, :, :], oc[:, :, :], bc_mid(lnb_sb[:, :], 2 * TILES), ALU.add))
                link(tt(os_[:, :, :], oc[:, :, :], oc[:, :, :], ALU.mult))
                link(V.tensor_scalar(os_[:, :, :], os_[:, :, :], 0.044715, 1.0, ALU.mult, ALU.add))
                tt(os_[:, :, :], os_[:, :, :], oc[:, :, :], ALU.mult).then_inc(gelu_in, 1)
                dve.wait_ge(gelu_exp, i + 1)
                link(V.tensor_scalar(os_[:, :, :], os_[:, :, :], 1.0, None, ALU.add))
                link(V.reciprocal(os_[:, :, :], os_[:, :, :]))
                tt(os_[:, :, :], os_[:, :, :], oc[:, :, :], ALU.mult).then_inc(h_ready, 1)
                dve.wait_ge(off_filled, i + 1)
                V.scalar_tensor_tensor(px[:, :, :].rearrange("p n a -> p (n a)"), kp[:, 0:256], 4.0,
                                       base[:, :, :].rearrange("p g c -> p (g c)"),
                                       ALU.mult, ALU.add).then_inc(off_read, 1)
                dve.wait_ge(off_read, i + 1)
                link(V.tensor_scalar(px[:, :, :], px[:, :, :], 0.0, float(W - 1), ALU.max, ALU.min))
                link(V.tensor_scalar(fl[:, :, :], px[:, :, :], -0.5, FLOOR, ALU.add, ALU.add))
                link(V.tensor_scalar(fl[:, :, :], fl[:, :, :], FLOOR, None, ALU.subtract))
                link(tt(wt[:, 1, :, :], px[:, :, :], fl[:, :, :], ALU.subtract))
                link(V.tensor_scalar(wt[:, 0, :, :], wt[:, 1, :, :], -1.0, 1.0, ALU.mult, ALU.add))
                link(V.scalar_tensor_tensor(idxf[:, :, :].rearrange("p g s -> p (g s)"), fl[:, :, 1], float(W), fl[:, :, 0],
                                            ALU.mult, ALU.add))
                tt(idx[:, :, :], idxf[:, :, :], bc(gbase[:, :], PT), ALU.add).then_inc(idx_ready, 1)
                for a in range(2):
                    for b in range(2):
                        link(tt(w4[:, :, a, b], wt[:, a, :, 0], wt[:, b, :, 1], ALU.mult))

            def sample(i, g):
                G = gath[g % GSLOTS]
                dve.wait_ge(gathered[g % GSLOTS], i * (16 * PT * 2 * TILES // GSLOTS) + 16 * PT * (g // GSLOTS + 1))
                Gc = G[:, :, :].rearrange("p s (k c) -> p (s k) c", c=C)
                wg = w4[:, g * PT:(g + 1) * PT, :, :].rearrange("p s a b -> p (s a b)")
                link(tt(Gc, Gc, bc(wg, C), ALU.mult))
                link(tt(G[:, :, 0:2 * C], G[:, :, 0:2 * C], G[:, :, 2 * C:4 * C], ALU.add))
                if past(i, 2 * TILES, g - 1):
                    dve.wait_ge(st_filled, i * (2 * TILES) + g - 1)
                tt(samp[g % 2][:, :].rearrange("p (s c) -> p s c", c=C), G[:, :, 0:C], G[:, :, C:2 * C],
                   ALU.add).then_inc(summed, 1)

            def scores(i, g):
                dve.wait_ge(k_filled, i * (2 * TILES) + g + 1)
                j, t = g // TILES, g % TILES
                tt(prod[:, :].rearrange("p (s c) -> p s c", c=C),
                   kp[:, :].rearrange("p (s c) -> p s c", c=C),
                   bc_mid(q_sb[:, j, t, :], PT), ALU.mult).then_inc(k_used, 1)
                dve.wait_ge(k_used, i * (2 * TILES) + g + 1)
                link(V.reduce_sum(sc[:, g % 4, :, :].rearrange("p s h -> p (s h)"),
                                  prod[:, :].rearrange("p (n d) -> p n d", d=DH), AX))

            def attend(i, q):
                by_point = lambda a: a.rearrange("p t s h -> p t h s")
                link(V.reduce_max(scm[:, :, 0, :], by_point(sc[:, :, :, :]), AX))
                tt(sc[:, :, :, :], sc[:, :, :, :], scm[:, :, 0, :].unsqueeze(2).to_broadcast([128, 4, PT, DH]),
                   ALU.subtract).then_inc(score_ready, 1)
                dve.wait_ge(score_exp, i * 4 + q + 1)
                link(V.reduce_sum(scm[:, :, 1, :], by_point(sc[:, :, :, :]), AX))
                link(V.reciprocal(scm[:, :, 0, :], scm[:, :, 1, :]))
                link(tt(sc[:, :, :, :], sc[:, :, :, :], scm[:, :, 0, :].unsqueeze(2).to_broadcast([128, 4, PT, DH]), ALU.mult))
                dve.wait_ge(v_copied, i * (2 * TILES) + 4 * (q + 1))
                v = v_sb[q % 2][:, :, :].rearrange("p t (n d) -> p (t n) d", d=DH)
                link(tt(v, v, bc(sc[:, :, :, :].rearrange("p t s h -> p (t s h)"), DH), ALU.mult))
                V.reduce_sum(h0[:, (q % 2) * 4:(q % 2) * 4 + 4, :],
                             v_sb[q % 2][:, :, :].rearrange("p t (s c) -> p t c s", s=PT), AX).then_inc(av_read, 1)
                dve.wait_ge(av_read, i * 4 + q + 1)

            def attention(i, j):
                hj, h1j = h0[:, :, :], h1[j][:, :, :]
                centred(hj, cen[:, :, :], sq[:, :, :], st8[:, 6, 0, :], st8[:, 6, 1, :], C)
                link(V.tensor_scalar(st8[:, 0, 0, :], st8[:, 6, 1, :], 1.0 / C, EPS, ALU.mult, ALU.add))
                link(V.reciprocal(st8[:, 7, 0, :], st8[:, 0, 0, :]))
                link(tt(st8[:, 7, 0, :], st8[:, 7, 0, :], st8[:, 6, 1, :], ALU.mult))
                V.tensor_scalar(st8[:, 0, 1, :], st8[:, 7, 0, :], 1e-24, None, ALU.max).then_inc(c_var, 1)
                dve.wait_ge(c_seed, i * 2 + j + 1)
                refine(st8[:, 3, :, :], st8[:, 2, :, :], st8[:, 6, :, :], st8[:, 7, :, :], st8[:, 0, :, :], LN_SCALE)
                link(tt(xln[:, :, :], cen[:, :, :], bc(st8[:, 3, 0, :], C), ALU.mult))
                tt(xn[:, :, :], xln[:, :, :], bc(st8[:, 3, 1, :], C), ALU.mult).then_inc(xn_ready, 1)
                for h in range(2):
                    dve.wait_ge(kt_filled, i * 4 + 2 * j + h + 1)
                    link(V.reduce_max(mx[:, h:h + 1], wb[1 + h][:, :], AX))
                link(tt(mx[:, 2:3], mx[:, 0:1], mx[:, 1:2], ALU.max))
                link(tt(mx[:, 2:3], mx[:, 2:3], mkmax[:, :], ALU.max))
                link(V.tensor_scalar(d33[:, 0:MEM], mk_sb[:, :], mx[:, 2:3], None, ALU.subtract))
                V.tensor_scalar(d33[:, 32:33], mx[:, 2:3], -1.0, None, ALU.mult).then_inc(d33_ready, 1)
                for h in range(2):
                    dve.wait_ge(q_filled, i * 4 + 2 * j + h + 1)
                    q = wb[0][:, :].rearrange("p (n d) -> p n d", d=HD)
                    m = qst[:, 0, h * 4 * HEADS:(h + 1) * 4 * HEADS]
                    link(V.reduce_max(m, q, AX))
                    tt(qs[:, h * 4 * HEADS:(h + 1) * 4 * HEADS, :], q, bc(m, HD), ALU.subtract).then_inc(qmax_done, 1)
                dve.wait_ge(eq_done, i * 2 + j + 1)
                link(V.reduce_sum(qst[:, 1, :], qs[:, :, :], AX))
                link(V.reciprocal(qst[:, 2, :], qst[:, 1, :]))
                tt(qs[:, :, :], qs[:, :, :], bc(qst[:, 2, :], HD), ALU.mult).then_inc(qn_ready, 1)
                dve.wait_ge(ctx_filled, i * 2 + j + 1)
                link(V.reciprocal(rs[:, 0:1], wb[2][:, 128:129]))
                link(V.tensor_scalar(rs[:, 1:2], rs[:, 0:1], float(HD) ** -0.5, None, ALU.mult))
                tt(cm[:, :], wb[2][:, 0:128], mask_sb[:, :], ALU.mult).then_inc(cm_ready, 1)
                dve.wait_ge(m_filled, i * 2 + j + 1)
                V.tensor_scalar(ms[:, :], wb[2][:, 256:256 + C], rs[:, 1:2], None, ALU.mult).then_inc(ms_ready, 1)
                dve.wait_ge(o_filled, i * 2 + j + 1)
                link(tt(cen[:, :, :], wb[2][:, :].rearrange("p (t c) -> p t c", c=C), bc_mid(bout[:, :], TILES), ALU.add))
                link(tt(sq[:, :, :], cen[:, :, :], cen[:, :, :], ALU.mult))
                link(V.reduce_sum(st8[:, 6, 0, :], sq[:, :, :], AX))
                V.tensor_scalar(st8[:, 3, 0, :], st8[:, 6, 0, :], 1e-24, None, ALU.max).then_inc(o_var, 1)
                dve.wait_ge(o_seed, i * 2 + j + 1)
                refine(st8[:, 6, 1, :], st8[:, 5, 0, :], st8[:, 7, 0, :], st8[:, 7, 1, :], st8[:, 3, 0, :], LN_SCALE)
                link(tt(cen[:, :, :], cen[:, :, :], bc(st8[:, 6, 1, :], C), ALU.mult))
                link(tt(cen[:, :, :], cen[:, :, :], bc_mid(gout[:, :], TILES), ALU.mult))
                link(tt(xln[:, :, :], xln[:, :, :], hj, ALU.add))
                link(tt(h1j, cen[:, :, :], xln[:, :, :], ALU.add))
                centred(h1j, cen[:, :, :], sq[:, :, :], st8[:, 6, 0, :], st8[:, 6, 1, :], C)
                V.tensor_scalar(st8[:, 3, 1, :], st8[:, 6, 1, :], 1.0 / C, EPS, ALU.mult, ALU.add).then_inc(l_var, 1)
                dve.wait_ge(l_seed, i * 2 + j + 1)
                refine(st8[:, 6, 1, :], st8[:, 5, 1, :], st8[:, 7, 0, :], st8[:, 7, 1, :], st8[:, 3, 1, :], LN_SCALE)
                tt(x2[:, :, :], cen[:, :, :], bc(st8[:, 6, 1, :], C), ALU.mult).then_inc(x2_ready, 1)
                dve.wait_ge(gate_filled, i * 2 + j + 1)
                logit = wb[1][:, 0:TILES * E].rearrange("p (t e) -> p t e", e=E)
                desc = bc_mid(desc_sb[:, :], TILES)

                def best(src, onehot, val, key):
                    link(V.reduce_max(val, src, AX))
                    link(tt(lg[:, 0, :, :], src, bc(val, E), ALU.is_equal))
                    link(tt(lg[:, 0, :, :], lg[:, 0, :, :], desc, ALU.mult))
                    link(V.reduce_max(key, lg[:, 0, :, :], AX))
                    link(tt(onehot, lg[:, 0, :, :], bc(key, E), ALU.is_equal))

                best(logit, lg[:, 1, :, :], tk[:, 0, :], tk[:, 1, :])
                link(V.scalar_tensor_tensor(lg[:, 2, :, :], lg[:, 1, :, :], -BIG, logit, ALU.mult, ALU.add))
                best(lg[:, 2, :, :], lg[:, 3, :, :], tk[:, 2, :], tk[:, 3, :])
                tt(tk[:, 4, :], tk[:, 2, :], tk[:, 0, :], ALU.subtract).then_inc(top_exp_in, 1)
                dve.wait_ge(top_exp, i * 2 + j + 1)
                link(V.tensor_scalar(tk[:, 6, :], tk[:, 5, :], 1.0, None, ALU.add))
                link(V.reciprocal(tk[:, 6, :], tk[:, 6, :]))
                link(tt(tk[:, 7, :], tk[:, 5, :], tk[:, 6, :], ALU.mult))
                link(tt(lg[:, 1, :, :], lg[:, 1, :, :], bc(tk[:, 6, :], E), ALU.mult))
                link(tt(lg[:, 3, :, :], lg[:, 3, :, :], bc(tk[:, 7, :], E), ALU.mult))
                tt(gates[j][:, :, :], lg[:, 1, :, :], lg[:, 3, :, :], ALU.add).then_inc(gates_ready, 1)
                dve.wait_ge(b2_filled, i * 2 + j + 1)
                tt(ybase[j][:, :, :], x2[:, :, :], wb[0][:, :].rearrange("p (t c) -> p t c", c=C),
                   ALU.add).then_inc(c_done, 1)

            def experts(i, g):
                j, t = g // TILES, g % TILES
                for h in range(2):
                    dve.wait_ge(quad_used, i * (8 * TILES) + 4 * g + 2 * h + 2)
                    tt(yprod[:, 8 * h:8 * h + 8, :], wb[2][:, :].rearrange("p (e c) -> p e c", c=C),
                       bc(gates[j][:, t, 8 * h:8 * h + 8], C), ALU.mult).then_inc(y_taken, 1)
                dve.wait_ge(y_taken, i * (4 * TILES) + 2 * g + 2)
                link(V.reduce_sum(moe[:, t, :], yprod[:, :, :].rearrange("p e c -> p c e"), AX))

            def finish(i, j):
                link(tt(moe[:, :, :], moe[:, :, :], ybase[j][:, :, :], ALU.add))
                centred(moe[:, :, :], fc[:, :, :], fsq[:, :, :], fst[:, 0, :], fst[:, 1, :], C)
                V.tensor_scalar(fst[:, 2, :], fst[:, 1, :], 1.0 / C, EPS, ALU.mult, ALU.add).then_inc(f_var, 1)
                dve.wait_ge(f_seed, i * 2 + j + 1)
                refine(fst[:, 5, :], fst[:, 4, :], fst[:, 0, :], fst[:, 1, :], fst[:, 2, :], LN_SCALE)
                link(tt(fc[:, :, :], fc[:, :, :], bc(fst[:, 5, :], C), ALU.mult))
                link(tt(fc[:, :, :], fc[:, :, :], bc_mid(gamma[:, :], TILES), ALU.mult))
                link(tt(fc[:, :, :], fc[:, :, :], bc_mid(beta[:, :], TILES), ALU.add))
                if j:
                    dve.wait_ge(out_stored, i * 32 + 16)
                tt(outb[:, :, :], fc[:, :, :], h1[j][:, :, :], ALU.add).then_inc(out_ready, 1)

            def body(i, first=False, last=False):
                project_queries(i)
                for g in range(2 * TILES):
                    sample(i, g)
                    if not first:
                        experts(i - 1, g)
                    scores(i, g)
                    if g % 4 == 3:
                        attend(i, g // 4)
                    if g % TILES == TILES - 1:
                        if not first:
                            finish(i - 1, g // TILES)
                        attention(i, g // TILES)
                if not first:
                    dve.wait_ge(out_stored, (i - 1) * 32 + 32)
                    dve.sem_inc(dve_step, 1)
                dve.sem_clear(dve_chain)
                chain[0] = 0

            for z in (wqo, wkv, wo2bd, b2bd, d33):
                V.memset(z[:, :], 0.0)
            V.memset(wqkv[:, :], 0.0)
            V.memset(ones[:, :], 1.0)
            for z in (xnT, x2T[0], x2T[1]):
                V.memset(z[C:C + 1, :], 1.0)
            for j in range(2):
                V.memset(gbase[:, j * TILES:(j + 1) * TILES], float(j * IMGROWS))
            link(V.memset(lg[:, :, :, :], 0.0))
            V.memset(moe[:, :, :], 0.0).then_inc(consts_ready, 1)
            dve.wait_ge(consts_in, NCONST_INC[0])
            for h in range(3):
                link(V.tensor_scalar(wqkv[0:C, h * HID:(h + 1) * HID], wqkv[0:C, h * HID:(h + 1) * HID],
                                     gpre[:, 0:1], float(C) ** 0.5, ALU.mult, ALU.mult))
            link(V.tensor_scalar(gout[:, :], gout[:, :], float(C) ** 0.5, None, ALU.mult))
            link(V.reduce_max(mkmax[:, :], mk_sb[:, :], AX))
            link(V.tensor_scalar(bo2_sb[:, :], bo2_sb[:, :], 4.0, None, ALU.mult))
            for g in range(2 * TILES):
                t = g % TILES
                link(tt(base[:, g, :].rearrange("p (s a) -> p s a", a=2),
                        bo2_sb[:, :].rearrange("p (s a) -> p s a", a=2),
                        bc_mid(ref_sb[:, 2 * t:2 * t + 2], PT), ALU.add))
            V.memset(moe[:, :, :], 0.0).then_inc(consts_ready, 1)
            dve.wait_ge(consts_ready, 2)
            body(0, first=True)
            with dve.Fori(1, PAIRS - 1) as i:
                body(i)
            body(PAIRS - 1, last=True)
            for g in range(2 * TILES):
                experts(PAIRS - 1, g)
                if g % TILES == TILES - 1:
                    finish(PAIRS - 1, g // TILES)


POINT = np.linspace(-1.0, 1.0, QR, dtype=np.float32)
PIXEL = (POINT + np.float32(1)) * np.float32(0.5) * np.float32(W - 1)
QUERY_ROW = [int(min(math.floor(v), H - 2)) for v in PIXEL]
NCONST_INC = [16 * (5 + 8 + 16 + 8 + 10)]


def shape_constants():
    frac = PIXEL - np.array(QUERY_ROW, np.float32)
    cols = np.zeros((W, QR), np.float32)
    for q in range(QR):
        cols[QUERY_ROW[q], q] = 1 - frac[q]
        cols[QUERY_ROW[q] + 1, q] = frac[q]
    interp = np.zeros((W, QR, 2, QR), np.float32)
    for q in range(QR):
        interp[:, q, 0] = cols * (1 - frac[q])
        interp[:, q, 1] = cols * frac[q]
    p = np.arange(128)
    ref = np.zeros((128, TILES, 2), np.float32)
    for t in range(TILES):
        ref[:, t, 0] = PIXEL[p % QR]
        ref[:, t, 1] = PIXEL[(128 // QR) * t + p // QR]
    return {
        "interp": interp.reshape(W, -1),
        "ref": ref.reshape(128, -1),
        "ident": np.eye(128, dtype=np.float32),
        "headmask": np.kron(np.eye(HEADS), np.ones((HD, HD))).astype(np.float32),
        "descend": np.broadcast_to(np.arange(E, 0, -1, dtype=np.float32), (128, E)).copy(),
    }


def kernel(**inputs):
    import concourse.bacc as bacc
    from concourse.bass_utils import run_bass_kernel_spmd

    a = {k: np.asarray(v) for k, v in inputs.items()}
    c = np.ascontiguousarray
    arrays = {"x": c(a["x"]).reshape(B * C, H * W)}
    arrays.update(shape_constants())
    arrays.update({
        "wqT": c(a["L0_tok_W_q"].T), "wkT": c(a["L0_tok_W_k"].T), "wvT": c(a["L0_tok_W_v"].T),
        "wo1": a["L0_tok_W_o1"], "bo1": a["L0_tok_b_o1"], "lng": a["L0_tok_ln_g"], "lnb": a["L0_tok_ln_b"],
        "wo2": a["L0_tok_W_o2"], "bo2": a["L0_tok_b_o2"],
        "wqkv": a["L0_attn_w_qkv"], "mk": c(a["L0_attn_mem_kv"][0]).reshape(HID, MEM),
        "mvT": c(a["L0_attn_mem_kv"][1].reshape(HID, MEM).T),
        "wout": a["L0_attn_w_out"], "bout": a["L0_attn_b_out"], "gout": a["L0_attn_g_out"], "gpre": a["L0_attn_g_pre"],
        "gatew": a["L0_ffn_gate_w"], "gateb": a["L0_ffn_gate_b"],
        "w1": c(a["L0_ffn_w1"].transpose(1, 0, 2)).reshape(C, E * F), "b1": c(a["L0_ffn_b1"]).reshape(E * F),
        "w2": c(a["L0_ffn_w2"].transpose(1, 0, 2)).reshape(F, E * C), "b2": a["L0_ffn_b2"],
        "gamma": a["L0_ffn_gamma"], "beta": a["L0_ffn_beta"],
    })
    nc = bacc.Bacc("TRN2", target_bir_lowering=False, num_devices=1)
    args = [nc.dram_tensor(f"{n}_dram", v.shape, mybir.dt.from_np(v.dtype), kind="ExternalInput").ap()
            for n, v in arrays.items()]
    corner_maps = [nc.dram_tensor(f"corner_map{b}", (2 * MAPROWS, W, 2 * C), FP32).ap() for b in range(2)]
    out = nc.dram_tensor("out_dram", (B, NQ, C), FP32, kind="ExternalOutput").ap()
    build(nc, *args, corner_maps, out)
    r = run_bass_kernel_spmd(nc, [{f"{n}_dram": c(v) for n, v in arrays.items()}], core_ids=[0])
    return r.results[0]["out_dram"]
```

```python
import math
from contextlib import ExitStack

import numpy as np
import concourse.bass as bass
from concourse import mybir
from concourse.alu_op_type import AluOpType as ALU

FP32 = mybir.dt.float32
I32 = mybir.dt.int32
ACT = mybir.ActivationFunctionType
AX = mybir.AxisListType.X

B, C, H, W = 32, 64, 128, 128
PAIRS = B // 2
DS = 4
QR = H // DS
NQ = QR * QR
TILES = NQ // 128
PT, DH = 8, 8
O1 = C // DS
CHUNKS, CROWS = 8, H // 8
QCOLS = NQ // CHUNKS
GROUPS = CROWS // 4
XA_USES = CHUNKS * (GROUPS + 1) + 5
CB_USES = 18
HEADS, HD, MEM = 4, 32, 4
HID = HEADS * HD
E, F = 16, 128
MAPROWS = H - 1
IMGROWS = MAPROWS * W
STORES = 16 * CHUNKS
QO = ((0, 3), (3, 3), (6, 2))
EPS = 1e-5
LN_SCALE = float(2 ** 18)
FLOOR = float(3 * 2 ** 22)
GSLOTS = 4
BIG = 3.0e38


def build(nc, x, interp, ref, ident, headmask, descend, wqT, wkT, wvT, wo1, bo1, lng, lnb, wo2, bo2,
          wqkv_in, mk_in, mvT_in, wout_in, bout_in, gout_in, gpre_in, gatew, gateb, w1_in, b1_in, w2_in, b2_in,
          gamma_in, beta_in, corner_maps, out):
    ctx = ExitStack()
    with ctx:
        def sb(name, shape, dt=FP32):
            return ctx.enter_context(nc.sbuf_tensor(name, shape, dt))

        def pb(name, cols):
            return ctx.enter_context(nc.psum_tensor(name, [128, cols], FP32))

        def sem(name):
            return ctx.enter_context(nc.semaphore(name))

        interp_sb = sb("interp_sb", [128, 2 * QR * QR])
        ref_sb = sb("ref_sb", [128, TILES * 2])
        id_sb = sb("id_sb", [128, 128])
        mask_sb = sb("mask_sb", [128, 128])
        desc_sb = sb("desc_sb", [128, E])
        wqo = sb("wqo", [128, 160])
        wkv = sb("wkv", [128, 256])
        wo2bd = sb("wo2bd", [128, 128])
        bo1_sb = sb("bo1_sb", [128, O1])
        lng_sb = sb("lng_sb", [128, O1])
        lnb_sb = sb("lnb_sb", [128, O1])
        bo2_sb = sb("bo2_sb", [128, 2 * PT])
        base = sb("base", [128, 2 * TILES, 2 * PT])
        gbase = sb("gbase", [128, 2 * TILES])
        wqkv = sb("wqkv", [C + 1, 3 * HID])
        gpre = sb("gpre", [C, 1])
        mk_sb = sb("mk_sb", [128, MEM])
        mkmax = sb("mkmax", [128, 1])
        mvT = sb("mvT", [MEM, HID])
        wout = sb("wout", [HID, C])
        bout = sb("bout", [128, C])
        gout = sb("gout", [128, C])
        gate_aug = sb("gate_aug", [C + 1, E])
        w1 = sb("w1", [128, E // 2, F])
        w2 = sb("w2", [F, E * C])
        b2bd = sb("b2bd", [128, TILES * C])
        gamma = sb("gamma", [128, C])
        beta = sb("beta", [128, C])
        ones = sb("ones", [128, 1])

        img = [sb(f"img{b}", [128, CROWS * W]) for b in range(2)]
        rows = [sb(f"rows{b}", [128, 2, CROWS + 1, C]) for b in range(2)]
        qfT = sb("qfT", [128, NQ])

        q_sb = [sb(f"q_sb{b}", [128, 2, TILES, C]) for b in range(2)]
        o1 = sb("o1", [128, 2 * TILES, O1])
        oc = sb("oc", [128, 2 * TILES, O1])
        os_ = sb("os_", [128, 2 * TILES, O1])
        st16 = sb("st16", [128, 6, 2 * TILES])
        hT = sb("hT", [128, 256])
        px = sb("px", [128, 2 * TILES * PT, 2])
        fl = sb("fl", [128, 2 * TILES * PT, 2])
        wt = sb("wt", [128, 2, 2 * TILES * PT, 2])
        idxf = sb("idxf", [128, 2 * TILES, PT])
        idx = [sb(f"idx{b}", [128, 2 * TILES, PT], I32) for b in range(2)]
        w4 = [sb(f"w4_{b}", [128, 2 * TILES * PT, 2, 2]) for b in range(2)]
        gath = [sb(f"gath{s}", [128, PT, 4 * C]) for s in range(GSLOTS)]
        samp = [sb(f"samp{b}", [128, PT * C]) for b in range(2)]
        sampT = [sb(f"sampT{b}", [128, PT * C]) for b in range(2)]
        prod = sb("prod", [128, PT * C])
        v_sb = [sb(f"v_sb{b}", [128, 4, PT * C]) for b in range(2)]
        sc = sb("sc", [128, 4, PT, DH])
        scm = sb("scm", [128, 4, 2, DH])
        h0 = [sb(f"h0_{j}", [128, TILES, C]) for j in range(2)]

        cen = sb("cen", [128, TILES, C])
        xln = sb("xln", [128, TILES, C])
        st8 = sb("st8", [128, 8, 2, TILES])
        xnT = sb("xnT", [C + 1, NQ])
        mx = sb("mx", [128, 4])
        d33 = sb("d33", [128, 33])
        emem = sb("emem", [MEM, HID])
        ek = sb("ek", [128, TILES, HID])
        va = sb("va", [128, TILES, HID])
        qs = sb("qs", [128, TILES * HEADS, HD])
        xn = qs[:, 0:TILES * HEADS // 2, :].rearrange("p (t a) d -> p t (a d)", a=2)
        sq = qs[:, TILES * HEADS // 2:TILES * HEADS, :].rearrange("p (t a) d -> p t (a d)", a=2)
        qst = sb("qst", [128, 3, TILES * HEADS])
        qnT = sb("qnT", [128, NQ])
        cm = sb("cm", [128, 128])
        rs = sb("rs", [128, 2])
        ms = sb("ms", [128, C])
        lg = sb("lg", [128, 4, TILES, E])
        tk = sb("tk", [128, 8, TILES])
        h1 = [sb(f"h1_{j}", [128, TILES, C]) for j in range(2)]
        x2 = [sb(f"x2_{j}", [128, TILES, C]) for j in range(2)]
        x2one = [sb(f"x2one{j}", [128, TILES, C]) for j in range(2)]
        gates = [sb(f"gates{j}", [128, TILES, E]) for j in range(2)]
        gT = [sb(f"gT{j}", [128, 128]) for j in range(2)]

        xg = sb("xg", [128, E, C])
        xgT = sb("xgT", [128, E // 2, 128])
        hid = [sb(f"hid{b}", [128, 4 * F]) for b in range(2)]
        fst = sb("fst", [128, 6, TILES])
        fsq = sb("fsq", [128, TILES, C])
        outb = sb("outb", [128, TILES, C])

        xa = pb("xa", 512)
        st = pb("st", 512)
        kp = pb("kp", 512)
        vp = pb("vp", 512)
        cb = pb("cb", 512)
        hb = [pb(f"hb{b}", 512) for b in range(2)]
        yb = pb("yb", 512)

        consts_in = sem("consts_in")
        consts_ready = sem("consts_ready")
        xa_filled = sem("xa_filled")
        xa_emptied = sem("xa_emptied")
        seam_copied = sem("seam_copied")
        o1_sum = sem("o1_sum")
        o1_sq = sem("o1_sq")
        o1_var = sem("o1_var")
        o1_seed = sem("o1_seed")
        gelu_in = sem("gelu_in")
        gelu_exp = sem("gelu_exp")
        h_ready = sem("h_ready")
        idx_ready = sem("idx_ready")
        corners_weighed = sem("corners_weighed")
        summed = sem("summed")
        sT_filled = sem("sT_filled")
        sT_taken = sem("sT_taken")
        k_filled = sem("k_filled")
        v_filled = sem("v_filled")
        k_used = sem("k_used")
        v_copied = sem("v_copied")
        score_ready = sem("score_ready")
        score_exp = sem("score_exp")
        av_read = sem("av_read")
        pool_step = sem("pool_step")
        cb_filled = sem("cb_filled")
        cb_emptied = sem("cb_emptied")
        cen_ready = sem("cen_ready")
        sq_done = sem("sq_done")
        var_ready = sem("var_ready")
        seed_ready = sem("seed_ready")
        xn_ready = sem("xn_ready")
        d33_ready = sem("d33_ready")
        qmax_done = sem("qmax_done")
        eq_done = sem("eq_done")
        qn_ready = sem("qn_ready")
        ms_ready = sem("ms_ready")
        x2_ready = sem("x2_ready")
        x2one_ready = sem("x2one_ready")
        top_exp_in = sem("top_exp_in")
        top_exp = sem("top_exp")
        gates_ready = sem("gates_ready")
        xg_ready = sem("xg_ready")
        x_filled = sem("x_filled")
        x_taken = sem("x_taken")
        h_filled = sem("h_filled")
        h_relu = sem("h_relu")
        quad_used = sem("quad_used")
        y_read = sem("y_read")
        f_cen = sem("f_cen")
        f_sq = sem("f_sq")
        f_var = sem("f_var")
        f_seed = sem("f_seed")
        out_ready = sem("out_ready")
        out_stored = sem("out_stored")
        dve_chain = sem("dve_chain")
        act_chain = sem("act_chain")
        sp_step = sem("sp_step")
        dve_step = sem("dve_step")
        stored = [sem(f"stored{b}") for b in range(2)]
        img_loaded = [sem(f"img_loaded{b}") for b in range(2)]
        gathered = [sem(f"gathered{s}") for s in range(GSLOTS)]
        block = ctx.enter_context(nc.Block())

        S2 = 2 * TILES

        def past(n, per, c):
            return not isinstance(n, int) or n * per + c > 0

        @block.sync
        def _(sp):
            count = [0]

            def const(dst, src):
                sp.dma_start(dst, src).then_inc(consts_in, 16)
                count[0] += 1

            sp.wait_ge(consts_ready, 1)
            const(id_sb[:, :], ident)
            const(interp_sb[:, :], interp)
            const(ref_sb[:, :], ref)
            const(mask_sb[:, :], headmask)
            const(desc_sb[:, :], descend)
            for j in range(2):
                const(wqo[j * C:(j + 1) * C, j * C:(j + 1) * C], wqT)
                const(wqo[j * C:(j + 1) * C, 2 * C + j * O1:2 * C + (j + 1) * O1], wo1)
                const(wkv[j * C:(j + 1) * C, j * C:(j + 1) * C], wkT)
                const(wkv[j * C:(j + 1) * C, (2 + j) * C:(3 + j) * C], wvT)
            for t in range(TILES):
                const(wo2bd[t * O1:(t + 1) * O1, t * 16:(t + 1) * 16], wo2)
                const(b2bd[t * E:(t + 1) * E, t * C:(t + 1) * C], b2_in)
            for dst, src, n in ((bo1_sb, bo1, O1), (lng_sb, lng, O1), (lnb_sb, lnb, O1), (bo2_sb, bo2, 2 * PT),
                                (bout, bout_in, C), (gout, gout_in, C), (gamma, gamma_in, C), (beta, beta_in, C)):
                const(dst[:, :], src.rearrange("(a n) -> a n", a=1).to_broadcast([128, n]))
            for a in range(2):
                of = w1_in.rearrange("c (q a f) -> c q a f", a=2, f=F)
                const(w1[a * C:(a + 1) * C - 1, :, :], of[0:C - 1, :, a, :])
                const(w1[(a + 1) * C - 1:(a + 1) * C, :, :],
                      b1_in.rearrange("(o q a f) -> o q a f", o=1, a=2, f=F)[:, :, a, :])
                const(ek[a * C:(a + 1) * C - 1, :, :], of[C - 1:C, :, a, :].to_broadcast([C - 1, E // 2, F]))
            const(wqkv[0:C, :], wqkv_in)
            const(gpre[:, :], gpre_in.rearrange("(n a) -> n a", a=1))
            const(mk_sb[:, :], mk_in)
            const(mvT[:, :], mvT_in)
            const(wout[:, :], wout_in)
            const(gate_aug[0:C, :], gatew)
            const(gate_aug[C:C + 1, :], gateb.rearrange("(a n) -> a n", a=1))
            const(w2[:, :], w2_in)
            assert 16 * count[0] == NCONST_INC, count[0]

            def load(n, k):
                fill = (GROUPS + 1) * (k - 2) + GROUPS - (5 if k < 2 else 0)
                if past(n, XA_USES, fill):
                    sp.wait_ge(xa_filled, n * XA_USES + fill)
                    sp.sem_inc(sp_step, 1)
                sp.dma_start(img[k % 2][:, :],
                             x[bass.ds(n * 128, 128), k * CROWS * W:(k + 1) * CROWS * W]).then_inc(img_loaded[k % 2], 16)

            def store(n, par, k):
                sp.wait_ge(xa_emptied, n * XA_USES + (GROUPS + 1) * k + GROUPS)
                sp.sem_inc(sp_step, 1)
                if past(n, CHUNKS - 1, k):
                    sp.wait_ge(seam_copied, n * (CHUNKS - 1) + k)
                    sp.sem_inc(sp_step, 1)
                if k == 0:
                    if past(n, S2, -S2):
                        sp.wait_ge(corners_weighed, n * S2 - S2)
                        sp.sem_inc(sp_step, 1)
                first = 1 if k == 0 else 0
                for j in range(2):
                    src = rows[k % 2][:, j, first:CROWS + 1, :]
                    src = bass.AP(tensor=src.tensor, offset=(j * (CROWS + 1) + first) * C,
                                  ap=[[2 * (CROWS + 1) * C, 128], [C, CROWS - first], [1, 2 * C]])
                    y0 = k * CROWS - 1 + first
                    dst = corner_maps[par][j * MAPROWS + y0:j * MAPROWS + y0 + CROWS - first]
                    sp.dma_start(dst.rearrange("y x c -> x y c"), src).then_inc(stored[k % 2], 16)

            def store_out(i, j):
                sp.wait_ge(out_ready, i * 2 + j + 1)
                sp.sem_inc(sp_step, 1)
                sp.dma_start(out[bass.ds(i * 2 + j, 1)].rearrange("a (t p) c -> p (a t) c", p=128),
                             outb[:, :, :]).then_inc(out_stored, 16)

            def body(n, par, out1=True, out0=True):
                for k in range(CHUNKS):
                    load(n, k)
                    if k:
                        store(n, par, k - 1)
                    if k == 5 and out1:
                        store_out(n - 3, 1)
                store(n, par, CHUNKS - 1)
                if out0:
                    store_out(n - 2, 0)

            body(0, 0, out1=False, out0=False)
            body(1, 1, out1=False, out0=False)
            body(2, 0, out1=False)
            with sp.Fori(0, (PAIRS - 4) // 2) as half:
                body(half * 2 + 3, 1)
                body(half * 2 + 4, 0)
            body(PAIRS - 1, 1)
            for n, j in ((PAIRS - 3, 1), (PAIRS - 2, 0), (PAIRS - 2, 1), (PAIRS - 1, 0), (PAIRS - 1, 1)):
                store_out(n, j)
            sp.wait_ge(out_stored, 16 * 2 * PAIRS)
            for s in stored:
                sp.wait_ge(s, STORES * PAIRS)

        @block.gpsimd
        def _(pool):
            def gather(i, par, g):
                s = g % GSLOTS
                if past(i, S2, g + 1 - GSLOTS):
                    pool.wait_ge(summed, i * S2 + g + 1 - GSLOTS)
                    pool.sem_inc(pool_step, 1)
                for p in range(PT):
                    pool.indirect_dma_start(
                        gath[s][:, p, :], None, corner_maps[par].rearrange("y x c -> (y x) c"),
                        bass.IndirectOffsetOnAxis(idx[par][:, g, p:p + 1], 0)).then_inc(gathered[s], 16)

            def body(i, par):
                for s in stored:
                    pool.wait_ge(s, i * STORES + STORES)
                    pool.sem_inc(pool_step, 1)
                pool.wait_ge(idx_ready, i + 1)
                pool.sem_inc(pool_step, 1)
                for g in range(S2):
                    gather(i, par, g)

            body(0, 0)
            with pool.Fori(0, PAIRS // 2 - 1) as half:
                body(half * 2 + 1, 1)
                body(half * 2 + 2, 0)
            body(PAIRS - 1, 1)

        @block.tensor
        def _(pe):
            mm = nc.tensor.matmul

            def transpose(dst, src):
                return nc.tensor.transpose(dst, src, id_sb[:, :])

            def chunk(n, k):
                pe.wait_ge(img_loaded[k % 2], n * (8 * CHUNKS) + 16 * (k // 2 + 1))
                for g in range(GROUPS + 1):
                    u = (GROUPS + 1) * k + g
                    if past(n, XA_USES, u):
                        pe.wait_ge(xa_emptied, n * XA_USES + u)
                    if g < GROUPS:
                        for r in range(4):
                            y = 4 * g + r
                            last = transpose(xa[:, r * 128:(r + 1) * 128], img[k % 2][:, y * W:(y + 1) * W])
                    else:
                        for q in range(CROWS // DS):
                            qy = k * (CROWS // DS) + q
                            y0 = QUERY_ROW[qy] - k * CROWS
                            for j in range(2):
                                for r in range(2):
                                    last = mm(xa[j * C:(j + 1) * C, q * QR:(q + 1) * QR],
                                              rows[k % 2][:, j, 1 + y0 + r, :],
                                              interp_sb[:, (2 * qy + r) * QR:(2 * qy + r + 1) * QR],
                                              start=(r == 0), stop=(r == 1))
                    last.then_inc(xa_filled, 1)
                    yield

            def queries(n):
                u = XA_USES - 5
                for t0, nt in QO:
                    pe.wait_ge(xa_emptied, n * XA_USES + u)
                    for t in range(nt):
                        last = mm(xa[:, t * 160:(t + 1) * 160], qfT[:, (t0 + t) * 128:(t0 + t + 1) * 128],
                                  wqo[:, :], start=True, stop=True)
                    last.then_inc(xa_filled, 1)
                    u += 1
                    yield
                yield
                yield
                yield
                pe.wait_ge(h_ready, n + 1)
                for j in range(2):
                    last = transpose(xa[:, j * 128:(j + 1) * 128],
                                     os_[:, j * TILES:(j + 1) * TILES, :].rearrange("p t c -> p (t c)"))
                last.then_inc(xa_filled, 1)
                yield
                pe.wait_ge(xa_emptied, n * XA_USES + XA_USES - 1)
                for j in range(2):
                    last = mm(xa[:, j * 128:(j + 1) * 128], hT[:, j * 128:(j + 1) * 128], wo2bd[:, :], start=True, stop=True)
                last.then_inc(xa_filled, 1)

            def sample_T(i, g, gated):
                pe.wait_ge(summed, i * S2 + g + 1)
                if gated and past(i, 2 * S2, 2 * (g - S2) + 2):
                    pe.wait_ge(x_taken, i * (2 * S2) + 2 * (g - S2) + 2)
                if past(i, S2, g):
                    pe.wait_ge(sT_taken, i * S2 + g)
                for q in range(4):
                    last = transpose(st[:, q * 128:(q + 1) * 128], samp[g % 2][:, q * 128:(q + 1) * 128])
                last.then_inc(sT_filled, 1)

            def sample_k(i, g):
                pe.wait_ge(sT_taken, i * S2 + g + 1)
                if past(i, S2, g):
                    pe.wait_ge(k_used, i * S2 + g)
                for q in range(4):
                    last = mm(kp[:, q * 128:(q + 1) * 128], sampT[g % 2][:, q * 128:(q + 1) * 128],
                              wkv[:, 0:128], start=True, stop=True)
                last.then_inc(k_filled, 1)

            def sample_v(i, g):
                if past(i, S2, g):
                    pe.wait_ge(v_copied, i * S2 + g)
                for q in range(4):
                    last = mm(vp[:, q * 128:(q + 1) * 128], sampT[g % 2][:, q * 128:(q + 1) * 128],
                              wkv[:, 128:256], start=True, stop=True)
                last.then_inc(v_filled, 1)

            def attention(i, j):
                f0 = i * (2 * CB_USES) + j * CB_USES
                yield
                yield
                yield
                pe.wait_ge(xn_ready, i * 2 + j + 1)
                if past(i, 2 * CB_USES, j * CB_USES):
                    pe.wait_ge(cb_emptied, f0)
                for q in range(4):
                    last = transpose(cb[:, q * 128:(q + 1) * 128], xn[:, 2 * q:2 * q + 2, :].rearrange("p t c -> p (t c)"))
                last.then_inc(cb_filled, 1)
                yield
                for h in range(2):
                    pe.wait_ge(cb_emptied, f0 + 1 + h)
                    mm(cb[:, :], wqkv[0:C, HID:2 * HID], xnT[0:C, h * 512:(h + 1) * 512],
                       start=True, stop=True).then_inc(cb_filled, 1)
                    yield
                pe.wait_ge(d33_ready, i * 2 + j + 1)
                pe.wait_ge(cb_emptied, f0 + 3)
                mm(cb[0:33, 0:128], d33[:, :], id_sb[:, :], start=True, stop=True).then_inc(cb_filled, 1)
                yield
                for u in range(4):
                    pe.wait_ge(cb_emptied, f0 + 4 + u)
                    for t in range(2 * u, 2 * u + 2):
                        last = mm(cb[:, (t % 2) * 256:(t % 2 + 1) * 256], xnT[:, t * 128:(t + 1) * 128],
                                  wqkv[:, HID:3 * HID], start=True, stop=True)
                    last.then_inc(cb_filled, 1)
                    yield
                for h in range(2):
                    pe.wait_ge(cb_emptied, f0 + 8 + h)
                    for t in range(4 * h, 4 * h + 4):
                        last = mm(cb[:, (t % 4) * HID:(t % 4 + 1) * HID], xnT[:, t * 128:(t + 1) * 128], wqkv[:, 0:HID],
                                  start=True, stop=True)
                    last.then_inc(cb_filled, 1)
                    yield
                pe.wait_ge(cb_emptied, f0 + 10)
                for t in range(TILES):
                    mm(cb[:, 128:129], ek[:, t, :], ones[:, :], start=(t == 0), stop=False)
                mm(cb[:, 128:129], emem[:, :], ones[0:MEM, :], start=False, stop=True)
                for t in range(TILES):
                    mm(cb[:, 0:128], va[:, t, :], ek[:, t, :], start=(t == 0), stop=False)
                mm(cb[:, 0:128], mvT[:, :], emem[:, :], start=False, stop=True).then_inc(cb_filled, 1)
                yield
                pe.wait_ge(cb_emptied, f0 + 11)
                mm(cb[:, 0:C], cm[:, :], wout[:, :], start=True, stop=True).then_inc(cb_filled, 1)
                yield
                pe.wait_ge(qn_ready, i * 2 + j + 1)
                for h in range(2):
                    pe.wait_ge(cb_emptied, f0 + 12 + h)
                    for q in range(4):
                        t = 4 * h + q
                        last = transpose(cb[:, q * 128:(q + 1) * 128],
                                         qs[:, t * HEADS:(t + 1) * HEADS, :].rearrange("p h d -> p (h d)"))
                    last.then_inc(cb_filled, 1)
                    yield
                pe.wait_ge(ms_ready, i * 2 + j + 1)
                pe.wait_ge(cb_emptied, f0 + 14)
                for t in range(TILES):
                    last = mm(cb[:, t * C:(t + 1) * C], qnT[:, t * 128:(t + 1) * 128], ms[:, :], start=True, stop=True)
                last.then_inc(cb_filled, 1)
                yield
                yield
                yield
                yield
                yield
                pe.wait_ge(x2_ready, i * 2 + j + 1)
                pe.wait_ge(cb_emptied, f0 + 15)
                for q in range(4):
                    last = transpose(cb[:, q * 128:(q + 1) * 128],
                                     x2[j][:, 2 * q:2 * q + 2, :].rearrange("p t c -> p (t c)"))
                last.then_inc(cb_filled, 1)
                yield
                pe.wait_ge(cb_emptied, f0 + 16)
                for t in range(TILES):
                    last = mm(cb[:, t * E:(t + 1) * E], xnT[:, t * 128:(t + 1) * 128], gate_aug[:, :], start=True, stop=True)
                last.then_inc(cb_filled, 1)
                yield
                yield
                pe.wait_ge(gates_ready, i * 2 + j + 1)
                pe.wait_ge(cb_emptied, f0 + 17)
                transpose(cb[:, 0:128], gates[j][:, :, :].rearrange("p t e -> p (t e)")).then_inc(cb_filled, 1)

            def inputs_T(n, h):
                pe.wait_ge(xg_ready, n * 2 + h + 1)
                if past(n, 2, h):
                    pe.wait_ge(x_taken, n * 2 + h)
                for q in range(4):
                    last = transpose(st[:, q * 128:(q + 1) * 128],
                                     xg[:, 8 * h + 2 * q:8 * h + 2 * q + 2, :].rearrange("p e c -> p (e c)"))
                last.then_inc(x_filled, 1)

            def experts_of(q):
                return range(8 * (q // 2) + q % 2, 8 * (q // 2) + 8, 2)

            def up(i, g, q):
                pe.wait_ge(x_taken, i * (2 * S2) + 2 * g + q // 2 + 1)
                if past(i, 4 * S2, 4 * g + q - 1):
                    pe.wait_ge(h_relu, i * (4 * S2) + 4 * g + q - 1)
                half = slice((q % 2) * C, (q % 2 + 1) * C)
                for n, e in enumerate(experts_of(q)):
                    last = mm(hb[q % 2][:, n * F:(n + 1) * F], w1[half, e // 2, :], xgT[half, e // 2, :],
                              start=True, stop=True)
                last.then_inc(h_filled, 1)

            def output_bias(i, g):
                j, t = g // TILES, g % TILES
                if t == 0:
                    pe.wait_ge(cb_emptied, i * (2 * CB_USES) + (j + 1) * CB_USES)
                    if past(i, 2, j):
                        pe.wait_ge(y_read, i * 2 + j)
                mm(yb[:, t * C:(t + 1) * C], gT[j][:, :], b2bd[:, t * C:(t + 1) * C], start=True, stop=False)

            def down(i, g, q):
                t = g % TILES
                pe.wait_ge(h_relu, i * (4 * S2) + 4 * g + q + 1)
                for n, e in enumerate(experts_of(q)):
                    last = mm(yb[:, t * C:(t + 1) * C], hid[q % 2][:, n * F:(n + 1) * F],
                              w2[:, e * C:(e + 1) * C], start=False, stop=(e == E - 1))
                last.then_inc(quad_used, 1)

            def body(i, first=False, maps=True, last=False):
                work = experts = None
                for g in range(S2):
                    if g == 0:
                        attn = iter(()) if first else attention(i - 1, 1)
                    if g == TILES:
                        attn = iter(()) if last else attention(i, 0)
                        side = queries(i + 1) if maps else iter(())
                    if g < TILES:
                        side = chunk(i + 1, g) if maps else iter(())
                    gated = not last or g < S2 - 1
                    gated = gated and (not first or g == S2 - 1)
                    before = not first

                    if not last:
                        sample_T(i, g, before)
                    if g < TILES:
                        next(side, None)
                    if not first:
                        up(i - 1, g, 0)
                    next(attn, None)
                    if not first:
                        up(i - 1, g, 1)
                    next(side, None)
                    if not last:
                        sample_k(i, g)
                    if gated:
                        inputs_T(i * S2 + (g + 1 - S2), 0)
                    if not first:
                        output_bias(i - 1, g)
                        down(i - 1, g, 0)
                    next(attn, None)
                    if g < TILES:
                        next(side, None)
                    if not first:
                        up(i - 1, g, 2)
                    if not last:
                        sample_v(i, g)
                    if not first:
                        down(i - 1, g, 1)
                        up(i - 1, g, 3)
                    next(attn, None)
                    next(side, None)
                    if gated:
                        inputs_T(i * S2 + (g + 1 - S2), 1)
                    if not first:
                        down(i - 1, g, 2)
                    next(attn, None)
                    if g < TILES:
                        next(side, None)
                    if not first:
                        down(i - 1, g, 3)
                    if g % TILES == TILES - 1:
                        for _ in attn:
                            pass
                        for _ in side:
                            pass

            pe.wait_ge(consts_in, NCONST_INC)
            pe.wait_ge(consts_ready, 2)
            for k in range(CHUNKS):
                for _ in chunk(0, k):
                    pass
            for _ in queries(0):
                pass
            body(0, first=True)
            body(1)
            with pe.Fori(2, PAIRS - 1) as i:
                body(i)
            body(PAIRS - 1, maps=False)
            body(PAIRS, maps=False, last=True)

        @block.scalar
        def _(act):
            chain = [0]

            def link(ins):
                chain[0] += 1
                ins.then_inc(act_chain, 1)
                act.wait_ge(act_chain, chain[0])

            def copy(dst, src):
                return nc.scalar.activation(dst, src, ACT.Copy)

            def square(dst, src):
                return nc.scalar.activation(dst, src, ACT.Square)

            def chunk(n, k):
                for g in range(GROUPS + 1):
                    u = (GROUPS + 1) * k + g
                    if g == 0:
                        if past(n, STORES, 32 * (k // 2)):
                            act.wait_ge(stored[k % 2], n * STORES + 32 * (k // 2))
                        if k:
                            act.wait_ge(xa_emptied, n * XA_USES + (GROUPS + 1) * k - 1)
                            copy(rows[k % 2][:, :, 0, :], rows[(k + 1) % 2][:, :, CROWS, :]).then_inc(seam_copied, 1)
                    act.wait_ge(xa_filled, n * XA_USES + u + 1)
                    if g < GROUPS:
                        copy(rows[k % 2][:, :, 1 + 4 * g:5 + 4 * g, :].rearrange("p j r c -> p r j c"),
                             xa[:, :].rearrange("p (r j c) -> p r j c", r=4, j=2)).then_inc(xa_emptied, 1)
                    else:
                        copy(qfT[:, k * QCOLS:(k + 1) * QCOLS], xa[:, 0:QCOLS]).then_inc(xa_emptied, 1)
                    yield

            def rsqrt_seed(src, tmp, dst, scale):
                link(nc.scalar.activation(tmp, src, ACT.Ln, scale=scale))
                return nc.scalar.activation(dst, tmp, ACT.Exp, scale=-0.5)

            def queries(n, par):
                u = XA_USES - 5
                if past(n, S2, -S2):
                    act.wait_ge(k_used, n * S2 - S2)
                for t0, nt in QO:
                    act.wait_ge(xa_filled, n * XA_USES + u + 1)
                    two = xa[:, 0:nt * 160].rearrange("p (t c) -> p t c", c=160)
                    nc.scalar.activation(q_sb[par][:, :, t0:t0 + nt, :].rearrange("p j t c -> p t j c"),
                                         two[:, :, 0:2 * C].rearrange("p t (j c) -> p t j c", j=2),
                                         ACT.Copy, scale=float(DH) ** -0.5)
                    copy(o1[:, :, :].rearrange("p (j t) c -> p t j c", j=2)[:, t0:t0 + nt, :, :],
                         two[:, :, 2 * C:160].rearrange("p t (j c) -> p t j c", j=2)).then_inc(xa_emptied, 1)
                    u += 1
                    yield
                act.wait_ge(o1_sum, n + 1)
                square(os_[:, :, :], oc[:, :, :]).then_inc(o1_sq, 1)
                yield
                act.wait_ge(o1_var, n + 1)
                rsqrt_seed(st16[:, 2, :], st16[:, 3, :], st16[:, 4, :], 1.0).then_inc(o1_seed, 1)
                yield
                act.wait_ge(gelu_in, n + 1)
                nc.scalar.activation(os_[:, :, :], os_[:, :, :], ACT.Exp,
                                     scale=-2.0 * math.sqrt(2.0 / math.pi)).then_inc(gelu_exp, 1)
                yield
                act.wait_ge(xa_filled, n * XA_USES + XA_USES - 1)
                copy(hT[:, :], xa[:, 0:256]).then_inc(xa_emptied, 1)
                yield
                act.wait_ge(xa_filled, n * XA_USES + XA_USES)
                nc.scalar.activation(px[:, :, :].rearrange("p n a -> p (n a)"), xa[:, 0:256],
                                     ACT.Copy, scale=4.0).then_inc(xa_emptied, 1)

            def sample_T(i, g):
                act.wait_ge(sT_filled, i * S2 + g + 1)
                if past(i, S2, g - 1):
                    act.wait_ge(v_filled, i * S2 + g - 1)
                copy(sampT[g % 2][:, :], st[:, :]).then_inc(sT_taken, 1)

            def sample_v(i, g):
                act.wait_ge(v_filled, i * S2 + g + 1)
                if past(i, 4, g // 4 - 1):
                    act.wait_ge(av_read, i * 4 + g // 4 - 1)
                copy(v_sb[(g // 4) % 2][:, g % 4, :], vp[:, :]).then_inc(v_copied, 1)

            def softmax_exp(i, q):
                act.wait_ge(score_ready, i * 4 + q + 1)
                nc.scalar.activation(sc[:, :, :, :], sc[:, :, :, :], ACT.Exp).then_inc(score_exp, 1)

            def attention(i, j):
                f0 = i * (2 * CB_USES) + j * CB_USES
                n3 = i * 6 + 3 * j
                yield
                act.wait_ge(cen_ready, n3 + 1)
                square(sq[:, :, :], cen[:, :, :]).then_inc(sq_done, 1)
                yield
                act.wait_ge(var_ready, n3 + 1)
                rsqrt_seed(st8[:, 0, :, :], st8[:, 1, :, :], st8[:, 2, :, :], LN_SCALE).then_inc(seed_ready, 1)
                yield
                act.wait_ge(cb_filled, f0 + 1)
                for par in range(2):
                    last = copy(xnT[0:C, :].rearrange("c (q a n) -> c q a n", a=2, n=128)[:, :, par, :],
                                cb[par * C:(par + 1) * C, :].rearrange("c (q n) -> c q n", n=128))
                last.then_inc(cb_emptied, 1)
                yield
                yield
                yield
                act.wait_ge(cb_filled, f0 + 4)
                nc.scalar.activation(emem[:, :], cb[0:MEM, 0:128], ACT.Exp)
                copy(wqkv[C:C + 1, HID:2 * HID], cb[32:33, 0:128]).then_inc(cb_emptied, 1)
                yield
                for u in range(4):
                    act.wait_ge(cb_filled, f0 + 5 + u)
                    two = cb[:, :].rearrange("p (t a c) -> p t a c", a=2, c=HID)
                    nc.scalar.activation(ek[:, 2 * u:2 * u + 2, :], two[:, :, 0, :], ACT.Exp)
                    copy(va[:, 2 * u:2 * u + 2, :], two[:, :, 1, :]).then_inc(cb_emptied, 1)
                    yield
                yield
                yield
                act.wait_ge(qmax_done, i * 2 + j + 1)
                nc.scalar.activation(qs[:, :, :], qs[:, :, :], ACT.Exp).then_inc(eq_done, 1)
                yield
                yield
                for h in range(2):
                    act.wait_ge(cb_filled, f0 + 13 + h)
                    copy(qnT[:, h * 512:(h + 1) * 512], cb[:, :]).then_inc(cb_emptied, 1)
                    yield
                yield
                act.wait_ge(cen_ready, n3 + 2)
                square(sq[:, :, :], cen[:, :, :]).then_inc(sq_done, 1)
                yield
                act.wait_ge(var_ready, n3 + 2)
                rsqrt_seed(st8[:, 3, 0, :], st8[:, 4, 0, :], st8[:, 5, 0, :], LN_SCALE).then_inc(seed_ready, 1)
                yield
                act.wait_ge(cen_ready, n3 + 3)
                square(sq[:, :, :], cen[:, :, :]).then_inc(sq_done, 1)
                yield
                act.wait_ge(var_ready, n3 + 3)
                rsqrt_seed(st8[:, 3, 1, :], st8[:, 4, 1, :], st8[:, 5, 1, :], LN_SCALE).then_inc(seed_ready, 1)
                yield
                act.wait_ge(cb_filled, f0 + 16)
                for par in range(2):
                    last = copy(xnT[0:C, :].rearrange("c (q a n) -> c q a n", a=2, n=128)[:, :, par, :],
                                cb[par * C:(par + 1) * C, :].rearrange("c (q n) -> c q n", n=128))
                last.then_inc(cb_emptied, 1)
                act.wait_ge(x2_ready, i * 2 + j + 1)
                copy(x2one[j][:, :, 0:C - 1], x2[j][:, :, 0:C - 1]).then_inc(x2one_ready, 1)
                yield
                yield
                act.wait_ge(top_exp_in, i * 2 + j + 1)
                nc.scalar.activation(tk[:, 5, :], tk[:, 4, :], ACT.Exp).then_inc(top_exp, 1)
                yield
                act.wait_ge(cb_filled, f0 + 18)
                copy(gT[j][:, :], cb[:, 0:128]).then_inc(cb_emptied, 1)

            def inputs_T(n, h):
                act.wait_ge(x_filled, n * 2 + h + 1)
                copy(xgT[:, 4 * h:4 * h + 4, :].rearrange("p e n -> p (e n)"), st[:, :]).then_inc(x_taken, 1)

            def relu(i, g, q):
                act.wait_ge(h_filled, i * (4 * S2) + 4 * g + q + 1)
                if past(i, 4 * S2, 4 * g + q - 1):
                    act.wait_ge(quad_used, i * (4 * S2) + 4 * g + q - 1)
                nc.scalar.activation(hid[q % 2][:, :], hb[q % 2][:, :], ACT.Relu).then_inc(h_relu, 1)

            def finish(i, j):
                yield
                act.wait_ge(f_cen, i * 2 + j + 1)
                square(fsq[:, :, :], outb[:, :, :]).then_inc(f_sq, 1)
                yield
                act.wait_ge(f_var, i * 2 + j + 1)
                rsqrt_seed(fst[:, 2, :], fst[:, 3, :], fst[:, 4, :], LN_SCALE).then_inc(f_seed, 1)

            def body(i, par, first=False, second=False, maps=True, last=False):
                for g in range(S2):
                    if g == 0:
                        attn = iter(()) if first else attention(i - 1, 1)
                        fin = iter(()) if first or second else finish(i - 2, 1)
                    if g == TILES:
                        attn = iter(()) if last else attention(i, 0)
                        side = queries(i + 1, 1 - par) if maps else iter(())
                        fin = iter(()) if first else finish(i - 1, 0)
                    if g < TILES:
                        side = chunk(i + 1, g) if maps else iter(())
                    gated = not last or g < S2 - 1
                    gated = gated and (not first or g == S2 - 1)

                    if not last:
                        sample_T(i, g)
                    if g < TILES:
                        next(side, None)
                    if not first:
                        relu(i - 1, g, 0)
                    if g % 4 == 0:
                        if g and not last:
                            softmax_exp(i, g // 4 - 1)
                        if not g and not first:
                            softmax_exp(i - 1, 3)
                    next(attn, None)
                    if not first:
                        relu(i - 1, g, 1)
                    next(side, None)
                    next(fin, None)
                    if gated:
                        inputs_T(i * S2 + (g + 1 - S2), 0)
                    next(attn, None)
                    if g < TILES:
                        next(side, None)
                    if not first:
                        relu(i - 1, g, 2)
                    if not last:
                        sample_v(i, g)
                    if not first:
                        relu(i - 1, g, 3)
                    next(attn, None)
                    next(side, None)
                    next(fin, None)
                    if gated:
                        inputs_T(i * S2 + (g + 1 - S2), 1)
                    next(attn, None)
                    if g < TILES:
                        next(side, None)
                    if g % TILES == TILES - 1:
                        for spread in (attn, side, fin):
                            for _ in spread:
                                pass
                act.sem_clear(act_chain)
                chain[0] = 0

            nc.scalar.preload_act_table_set("natural_log_exp_and_others")
            for k in range(CHUNKS):
                for _ in chunk(0, k):
                    pass
            for _ in queries(0, 0):
                pass
            body(0, 0, first=True)
            body(1, 1, second=True)
            with act.Fori(0, (PAIRS - 4) // 2) as half:
                body(half * 2 + 2, 0)
                body(half * 2 + 3, 1)
            body(PAIRS - 2, 0)
            body(PAIRS - 1, 1, maps=False)
            body(PAIRS, 0, maps=False, last=True)
            for _ in finish(PAIRS - 1, 1):
                pass

        @block.vector
        def _(dve):
            V = nc.vector
            chain = [0]

            def mark(ins):
                chain[0] += 1
                ins.then_inc(dve_chain, 1)
                return chain[0]

            def link(ins):
                dve.wait_ge(dve_chain, mark(ins))

            def tt(out_, a, b, op):
                return V.tensor_tensor(out_, a, b, op)

            def bc(ap, n):
                return ap.unsqueeze(2).to_broadcast([ap.shape[0], ap.shape[1], n])

            def bc_mid(ap, n):
                return ap.unsqueeze(1).to_broadcast([ap.shape[0], n, ap.shape[1]])

            def centre(src, cen_, s, n):
                link(V.reduce_sum(s, src, AX))
                return V.scalar_tensor_tensor(cen_, bc(s, n), -1.0 / n, src, ALU.mult, ALU.add)

            def newton(r, seed, h, u, scale):
                link(V.tensor_scalar(r, seed, scale ** 0.5, None, ALU.mult))
                link(tt(u, r, r, ALU.mult))
                link(tt(u, u, h, ALU.mult))
                link(V.scalar_tensor_tensor(r, u, 1.5, r, ALU.add, ALU.mult))

            def queries(n, par):
                yield
                yield
                dve.wait_ge(xa_emptied, n * XA_USES + XA_USES - 2)
                link(tt(o1[:, :, :], o1[:, :, :], bc_mid(bo1_sb[:, :], S2), ALU.add))
                centre(o1[:, :, :], oc[:, :, :], st16[:, 0, :], O1).then_inc(o1_sum, 1)
                yield
                dve.wait_ge(o1_sq, n + 1)
                link(V.reduce_sum(st16[:, 1, :], os_[:, :, :], AX))
                V.tensor_scalar(st16[:, 2, :], st16[:, 1, :], 1.0 / O1, EPS, ALU.mult, ALU.add).then_inc(o1_var, 1)
                dve.wait_ge(o1_var, n + 1)
                link(V.tensor_scalar(st16[:, 0, :], st16[:, 2, :], -0.5, None, ALU.mult))
                yield
                dve.wait_ge(o1_seed, n + 1)
                newton(st16[:, 5, :], st16[:, 4, :], st16[:, 0, :], st16[:, 1, :], 1.0)
                link(tt(oc[:, :, :], oc[:, :, :], bc(st16[:, 5, :], O1), ALU.mult))
                link(tt(oc[:, :, :], oc[:, :, :], bc_mid(lng_sb[:, :], S2), ALU.mult))
                link(tt(oc[:, :, :], oc[:, :, :], bc_mid(lnb_sb[:, :], S2), ALU.add))
                link(tt(os_[:, :, :], oc[:, :, :], oc[:, :, :], ALU.mult))
                link(V.tensor_scalar(os_[:, :, :], os_[:, :, :], 0.044715, 1.0, ALU.mult, ALU.add))
                tt(os_[:, :, :], os_[:, :, :], oc[:, :, :], ALU.mult).then_inc(gelu_in, 1)
                yield
                dve.wait_ge(gelu_exp, n + 1)
                link(V.tensor_scalar(os_[:, :, :], os_[:, :, :], 1.0, None, ALU.add))
                link(V.reciprocal(os_[:, :, :], os_[:, :, :]))
                tt(os_[:, :, :], os_[:, :, :], oc[:, :, :], ALU.mult).then_inc(h_ready, 1)
                yield
                yield
                dve.wait_ge(xa_emptied, n * XA_USES + XA_USES)
                link(tt(px[:, :, :].rearrange("p n a -> p (n a)"), px[:, :, :].rearrange("p n a -> p (n a)"),
                        base[:, :, :].rearrange("p g c -> p (g c)"), ALU.add))
                link(V.tensor_scalar(px[:, :, :], px[:, :, :], 0.0, float(W - 1), ALU.max, ALU.min))
                link(V.tensor_scalar(fl[:, :, :], px[:, :, :], -0.5, FLOOR, ALU.add, ALU.add))
                link(V.tensor_scalar(fl[:, :, :], fl[:, :, :], FLOOR, None, ALU.subtract))
                link(V.scalar_tensor_tensor(idxf[:, :, :].rearrange("p g s -> p (g s)"), fl[:, :, 1], float(W), fl[:, :, 0],
                                            ALU.mult, ALU.add))
                tt(idx[par][:, :, :], idxf[:, :, :], bc(gbase[:, :], PT), ALU.add).then_inc(idx_ready, 1)
                yield
                link(tt(wt[:, 1, :, :], px[:, :, :], fl[:, :, :], ALU.subtract))
                link(V.tensor_scalar(wt[:, 0, :, :], wt[:, 1, :, :], -1.0, 1.0, ALU.mult, ALU.add))
                for a in range(2):
                    for b in range(2):
                        last = mark(tt(w4[par][:, :, a, b], wt[:, a, :, 0], wt[:, b, :, 1], ALU.mult))
                dve.wait_ge(dve_chain, last)

            def weigh(i, par, g):
                t = g % S2
                G = gath[g % GSLOTS]
                dve.wait_ge(gathered[g % GSLOTS], i * (16 * PT * S2 // GSLOTS) + 16 * PT * (g // GSLOTS + 1))
                Gc = G[:, :, :].rearrange("p s (k c) -> p (s k) c", c=C)
                wg = w4[par][:, t * PT:(t + 1) * PT, :, :].rearrange("p s a b -> p (s a b)")
                tt(Gc, Gc, bc(wg, C), ALU.mult).then_inc(corners_weighed, 1)

            def sum_columns(i, g):
                G = gath[g % GSLOTS]
                dve.wait_ge(corners_weighed, i * S2 + g + 1)
                return mark(tt(G[:, :, 0:2 * C], G[:, :, 0:2 * C], G[:, :, 2 * C:4 * C], ALU.add))

            def sum_rows(i, g, columns):
                G = gath[g % GSLOTS]
                if past(i, S2, g - 1):
                    dve.wait_ge(sT_filled, i * S2 + g - 1)
                dve.wait_ge(dve_chain, columns)
                tt(samp[g % 2][:, :].rearrange("p (s c) -> p s c", c=C), G[:, :, 0:C], G[:, :, C:2 * C],
                   ALU.add).then_inc(summed, 1)

            def scores(i, par, g):
                dve.wait_ge(k_filled, i * S2 + g + 1)
                j, t = g // TILES, g % TILES
                tt(prod[:, :].rearrange("p (s c) -> p s c", c=C),
                   kp[:, :].rearrange("p (s c) -> p s c", c=C),
                   bc_mid(q_sb[par][:, j, t, :], PT), ALU.mult).then_inc(k_used, 1)
                dve.wait_ge(k_used, i * S2 + g + 1)
                link(V.reduce_sum(sc[:, g % 4, :, :].rearrange("p s h -> p (s h)"),
                                  prod[:, :].rearrange("p (n d) -> p n d", d=DH), AX))

            def by_point(a):
                return a.rearrange("p t s h -> p t h s")

            def attend_max(i, q):
                link(V.reduce_max(scm[:, :, 0, :], by_point(sc[:, :, :, :]), AX))
                tt(sc[:, :, :, :], sc[:, :, :, :], scm[:, :, 0, :].unsqueeze(2).to_broadcast([128, 4, PT, DH]),
                   ALU.subtract).then_inc(score_ready, 1)

            def attend(i, q):
                dve.wait_ge(score_exp, i * 4 + q + 1)
                link(V.reduce_sum(scm[:, :, 1, :], by_point(sc[:, :, :, :]), AX))
                link(V.reciprocal(scm[:, :, 0, :], scm[:, :, 1, :]))
                link(tt(sc[:, :, :, :], sc[:, :, :, :], scm[:, :, 0, :].unsqueeze(2).to_broadcast([128, 4, PT, DH]), ALU.mult))
                dve.wait_ge(v_copied, i * S2 + 4 * (q + 1))
                v = v_sb[q % 2][:, :, :].rearrange("p t (n d) -> p (t n) d", d=DH)
                link(tt(v, v, bc(sc[:, :, :, :].rearrange("p t s h -> p (t s h)"), DH), ALU.mult))
                V.reduce_sum(h0[q // 2][:, (q % 2) * 4:(q % 2) * 4 + 4, :],
                             v_sb[q % 2][:, :, :].rearrange("p t (s c) -> p t c s", s=PT), AX).then_inc(av_read, 1)

            def attention(i, j):
                hj, h1j = h0[j][:, :, :], h1[j][:, :, :]
                f0 = i * (2 * CB_USES) + j * CB_USES
                n3 = i * 6 + 3 * j
                dve.wait_ge(av_read, i * 4 + 2 * j + 2)
                centre(hj, cen[:, :, :], st8[:, 6, 0, :], C).then_inc(cen_ready, 1)
                yield
                dve.wait_ge(sq_done, n3 + 1)
                link(V.reduce_sum(st8[:, 6, 1, :], sq[:, :, :], AX))
                link(V.tensor_scalar(st8[:, 0, 0, :], st8[:, 6, 1, :], 1.0 / C, EPS, ALU.mult, ALU.add))
                link(V.reciprocal(st8[:, 7, 0, :], st8[:, 0, 0, :]))
                link(tt(st8[:, 7, 0, :], st8[:, 7, 0, :], st8[:, 6, 1, :], ALU.mult))
                V.tensor_scalar(st8[:, 0, 1, :], st8[:, 7, 0, :], 1e-24, None, ALU.max).then_inc(var_ready, 1)
                dve.wait_ge(var_ready, n3 + 1)
                link(V.tensor_scalar(st8[:, 6, :, :], st8[:, 0, :, :], -0.5, None, ALU.mult))
                yield
                dve.wait_ge(seed_ready, n3 + 1)
                newton(st8[:, 3, :, :], st8[:, 2, :, :], st8[:, 6, :, :], st8[:, 7, :, :], LN_SCALE)
                link(tt(xln[:, :, :], cen[:, :, :], bc(st8[:, 3, 0, :], C), ALU.mult))
                tt(xn[:, :, :], xln[:, :, :], bc(st8[:, 3, 1, :], C), ALU.mult).then_inc(xn_ready, 1)
                yield
                yield
                for h in range(2):
                    dve.wait_ge(cb_filled, f0 + 2 + h)
                    V.reduce_max(mx[:, h:h + 1], cb[:, :], AX).then_inc(cb_emptied, 1)
                    if h == 0:
                        yield
                dve.wait_ge(cb_emptied, f0 + 3)
                link(tt(mx[:, 2:3], mx[:, 0:1], mx[:, 1:2], ALU.max))
                link(tt(mx[:, 2:3], mx[:, 2:3], mkmax[:, :], ALU.max))
                link(V.tensor_scalar(d33[:, 0:MEM], mk_sb[:, :], mx[:, 2:3], None, ALU.subtract))
                V.tensor_scalar(d33[:, 32:33], mx[:, 2:3], -1.0, None, ALU.mult).then_inc(d33_ready, 1)
                yield
                yield
                for u in range(4):
                    yield
                for h in range(2):
                    dve.wait_ge(cb_filled, f0 + 9 + h)
                    q = cb[:, :].rearrange("p (n d) -> p n d", d=HD)
                    m = qst[:, 0, h * 4 * HEADS:(h + 1) * 4 * HEADS]
                    link(V.reduce_max(m, q, AX))
                    tt(qs[:, h * 4 * HEADS:(h + 1) * 4 * HEADS, :], q, bc(m, HD), ALU.subtract).then_inc(cb_emptied, 1)
                    if h == 0:
                        yield
                dve.wait_ge(cb_emptied, f0 + 10)
                V.memset(rs[:, 0:1], 1.0).then_inc(qmax_done, 1)
                yield
                dve.wait_ge(cb_filled, f0 + 11)
                dve.wait_ge(qmax_done, i * 2 + j + 1)
                link(V.reciprocal(rs[:, 0:1], cb[:, 128:129]))
                tt(cm[:, :], cb[:, 0:128], mask_sb[:, :], ALU.mult).then_inc(cb_emptied, 1)
                link(V.tensor_scalar(rs[:, 1:2], rs[:, 0:1], float(HD) ** -0.5, None, ALU.mult))
                dve.wait_ge(eq_done, i * 2 + j + 1)
                link(V.reduce_sum(qst[:, 1, :], qs[:, :, :], AX))
                link(V.reciprocal(qst[:, 2, :], qst[:, 1, :]))
                tt(qs[:, :, :], qs[:, :, :], bc(qst[:, 2, :], HD), ALU.mult).then_inc(qn_ready, 1)
                yield
                dve.wait_ge(cb_filled, f0 + 12)
                V.tensor_scalar(ms[:, :], cb[:, 0:C], rs[:, 1:2], None, ALU.mult).then_inc(cb_emptied, 1)
                dve.wait_ge(cb_emptied, f0 + 12)
                V.memset(rs[:, 0:1], 1.0).then_inc(ms_ready, 1)
                yield
                yield
                yield
                dve.wait_ge(cb_filled, f0 + 15)
                tt(cen[:, :, :], cb[:, :].rearrange("p (t c) -> p t c", c=C), bc_mid(bout[:, :], TILES),
                   ALU.add).then_inc(cb_emptied, 1)
                dve.wait_ge(cb_emptied, f0 + 15)
                tt(xln[:, :, :], xln[:, :, :], hj, ALU.add).then_inc(cen_ready, 1)
                yield
                dve.wait_ge(sq_done, n3 + 2)
                link(V.reduce_sum(st8[:, 6, 0, :], sq[:, :, :], AX))
                V.tensor_scalar(st8[:, 3, 0, :], st8[:, 6, 0, :], 1e-24, None, ALU.max).then_inc(var_ready, 1)
                dve.wait_ge(var_ready, n3 + 2)
                link(V.tensor_scalar(st8[:, 7, 0, :], st8[:, 3, 0, :], -0.5, None, ALU.mult))
                yield
                link(tt(cen[:, :, :], cen[:, :, :], bc_mid(gout[:, :], TILES), ALU.mult))
                dve.wait_ge(seed_ready, n3 + 2)
                newton(st8[:, 6, 1, :], st8[:, 5, 0, :], st8[:, 7, 0, :], st8[:, 7, 1, :], LN_SCALE)
                link(tt(cen[:, :, :], cen[:, :, :], bc(st8[:, 6, 1, :], C), ALU.mult))
                link(tt(h1j, cen[:, :, :], xln[:, :, :], ALU.add))
                centre(h1j, cen[:, :, :], st8[:, 6, 0, :], C).then_inc(cen_ready, 1)
                yield
                dve.wait_ge(sq_done, n3 + 3)
                link(V.reduce_sum(st8[:, 6, 1, :], sq[:, :, :], AX))
                V.tensor_scalar(st8[:, 3, 1, :], st8[:, 6, 1, :], 1.0 / C, EPS, ALU.mult, ALU.add).then_inc(var_ready, 1)
                dve.wait_ge(var_ready, n3 + 3)
                link(V.tensor_scalar(st8[:, 7, 0, :], st8[:, 3, 1, :], -0.5, None, ALU.mult))
                yield
                dve.wait_ge(seed_ready, n3 + 3)
                newton(st8[:, 6, 1, :], st8[:, 5, 1, :], st8[:, 7, 0, :], st8[:, 7, 1, :], LN_SCALE)
                tt(x2[j][:, :, :], cen[:, :, :], bc(st8[:, 6, 1, :], C), ALU.mult).then_inc(x2_ready, 1)
                yield
                yield
                dve.wait_ge(cb_filled, f0 + 17)
                desc = bc_mid(desc_sb[:, :], TILES)
                link(V.tensor_scalar(lg[:, 2, :, :], cb[:, 0:TILES * E].rearrange("p (t e) -> p t e", e=E),
                                     0.0, None, ALU.add))

                def best(src, onehot, val, key):
                    link(V.reduce_max(val, src, AX))
                    link(tt(lg[:, 0, :, :], src, bc(val, E), ALU.is_equal))
                    link(tt(lg[:, 0, :, :], lg[:, 0, :, :], desc, ALU.mult))
                    link(V.reduce_max(key, lg[:, 0, :, :], AX))
                    link(tt(onehot, lg[:, 0, :, :], bc(key, E), ALU.is_equal))

                best(lg[:, 2, :, :], lg[:, 1, :, :], tk[:, 0, :], tk[:, 1, :])
                V.scalar_tensor_tensor(lg[:, 2, :, :], lg[:, 1, :, :], -BIG, lg[:, 2, :, :], ALU.mult,
                                       ALU.add).then_inc(cb_emptied, 1)
                dve.wait_ge(cb_emptied, f0 + 17)
                best(lg[:, 2, :, :], lg[:, 3, :, :], tk[:, 2, :], tk[:, 3, :])
                tt(tk[:, 4, :], tk[:, 2, :], tk[:, 0, :], ALU.subtract).then_inc(top_exp_in, 1)
                yield
                dve.wait_ge(top_exp, i * 2 + j + 1)
                link(V.tensor_scalar(tk[:, 6, :], tk[:, 5, :], 1.0, None, ALU.add))
                link(V.reciprocal(tk[:, 6, :], tk[:, 6, :]))
                link(tt(tk[:, 7, :], tk[:, 5, :], tk[:, 6, :], ALU.mult))
                link(tt(lg[:, 1, :, :], lg[:, 1, :, :], bc(tk[:, 6, :], E), ALU.mult))
                link(tt(lg[:, 3, :, :], lg[:, 3, :, :], bc(tk[:, 7, :], E), ALU.mult))
                tt(gates[j][:, :, :], lg[:, 1, :, :], lg[:, 3, :, :], ALU.add).then_inc(gates_ready, 1)
                dve.wait_ge(gates_ready, i * 2 + j + 1)
                yield

            def gate_inputs(i, g):
                j, t = (g % S2) // TILES, g % TILES
                n = i * S2 + g
                if t == 0:
                    dve.wait_ge(x2one_ready, i * 2 + g // TILES + 1)
                for h in range(2):
                    if past(i, 2 * S2, 2 * g + h - 1):
                        dve.wait_ge(x_filled, i * (2 * S2) + 2 * g + h - 1)
                    tt(xg[:, 8 * h:8 * h + 8, :], bc(gates[j][:, t, 8 * h:8 * h + 8], C), bc_mid(x2one[j][:, t, :], 8),
                       ALU.mult).then_inc(xg_ready, 1)

            def finish(i, j):
                dve.wait_ge(quad_used, i * (4 * S2) + 4 * TILES * (j + 1))
                if past(i, 32, 16 * j):
                    dve.wait_ge(out_stored, i * 32 + 16 * j)
                tt(outb[:, :, :], x2[j][:, :, :], yb[:, :].rearrange("p (t c) -> p t c", c=C), ALU.add).then_inc(y_read, 1)
                yield
                dve.wait_ge(y_read, i * 2 + j + 1)
                centre(outb[:, :, :], outb[:, :, :], fst[:, 0, :], C).then_inc(f_cen, 1)
                yield
                dve.wait_ge(f_sq, i * 2 + j + 1)
                link(V.reduce_sum(fst[:, 1, :], fsq[:, :, :], AX))
                V.tensor_scalar(fst[:, 2, :], fst[:, 1, :], 1.0 / C, EPS, ALU.mult, ALU.add).then_inc(f_var, 1)
                dve.wait_ge(f_var, i * 2 + j + 1)
                link(V.tensor_scalar(fst[:, 0, :], fst[:, 2, :], -0.5, None, ALU.mult))
                link(tt(outb[:, :, :], outb[:, :, :], bc_mid(gamma[:, :], TILES), ALU.mult))
                yield
                dve.wait_ge(f_seed, i * 2 + j + 1)
                newton(fst[:, 5, :], fst[:, 4, :], fst[:, 0, :], fst[:, 1, :], LN_SCALE)
                link(tt(outb[:, :, :], outb[:, :, :], bc(fst[:, 5, :], C), ALU.mult))
                yield
                link(tt(outb[:, :, :], outb[:, :, :], bc_mid(beta[:, :], TILES), ALU.add))
                tt(outb[:, :, :], outb[:, :, :], h1[j][:, :, :], ALU.add).then_inc(out_ready, 1)

            def body(i, par, first=False, second=False, maps=True, last=False):
                for g in range(S2):
                    if g == 0:
                        attn = iter(()) if first else attention(i - 1, 1)
                        side = iter(())
                        fin = iter(()) if first or second else finish(i - 2, 1)
                    if g == TILES:
                        attn = iter(()) if last else attention(i, 0)
                        side = queries(i + 1, 1 - par) if maps else iter(())
                        fin = iter(()) if first else finish(i - 1, 0)
                    gated = not last or g < S2 - 1
                    gated = gated and (not first or g == S2 - 1)
                    ahead = not last and (maps or g < S2 - 1)
                    npar = par if g < S2 - 1 else 1 - par

                    if g % TILES == 0:
                        next(fin, None)
                    if gated:
                        gate_inputs(i - 1, g + 1)
                    if ahead:
                        weigh(i, npar, g + 1)
                    if g % 4 == 0:
                        if g and not last:
                            attend(i, g // 4 - 1)
                        if not g and not first:
                            attend(i - 1, 3)
                    next(attn, None)
                    if ahead:
                        columns = sum_columns(i, g + 1)
                    next(side, None)
                    next(fin, None)
                    if ahead:
                        sum_rows(i, g + 1, columns)
                    next(attn, None)
                    next(attn, None)
                    if not last:
                        scores(i, par, g)
                        if g % 4 == 3:
                            attend_max(i, g // 4)
                    next(side, None)
                    next(fin, None)
                    next(attn, None)
                    if g % TILES == TILES - 1:
                        for spread in (attn, side, fin):
                            for _ in spread:
                                pass
                if first:
                    dve.sem_inc(dve_step, 1)
                dve.sem_clear(dve_chain)
                chain[0] = 0

            for z in (wqo, wkv, wo2bd, b2bd, d33, wqkv):
                V.memset(z[:, :], 0.0)
            V.memset(ek[:, :, :], 0.0)
            V.memset(ones[:, :], 1.0)
            V.memset(xnT[C:C + 1, :], 1.0)
            for j in range(2):
                V.memset(x2one[j][:, :, C - 1:C], 1.0)
                V.memset(gbase[:, j * TILES:(j + 1) * TILES], float(j * IMGROWS))
            link(V.memset(lg[:, :, :, :], 0.0))
            V.memset(outb[:, :, :], 0.0).then_inc(consts_ready, 1)
            dve.wait_ge(consts_in, NCONST_INC)
            for h in range(3):
                link(V.tensor_scalar(wqkv[0:C, h * HID:(h + 1) * HID], wqkv[0:C, h * HID:(h + 1) * HID],
                                     gpre[:, 0:1], float(C) ** 0.5, ALU.mult, ALU.mult))
            link(tt(w1[:, :, :], w1[:, :, :], ek[:, :, :], ALU.subtract))
            link(V.tensor_scalar(gout[:, :], gout[:, :], float(C) ** 0.5, None, ALU.mult))
            link(V.reduce_max(mkmax[:, :], mk_sb[:, :], AX))
            link(V.tensor_scalar(bo2_sb[:, :], bo2_sb[:, :], 4.0, None, ALU.mult))
            for g in range(S2):
                t = g % TILES
                link(tt(base[:, g, :].rearrange("p (s a) -> p s a", a=2),
                        bo2_sb[:, :].rearrange("p (s a) -> p s a", a=2),
                        bc_mid(ref_sb[:, 2 * t:2 * t + 2], PT), ALU.add))
            V.memset(outb[:, :, :], 0.0).then_inc(consts_ready, 1)
            dve.wait_ge(consts_ready, 2)
            for _ in queries(0, 0):
                pass
            weigh(0, 0, 0)
            sum_rows(0, 0, sum_columns(0, 0))
            body(0, 0, first=True)
            body(1, 1, second=True)
            with dve.Fori(0, (PAIRS - 4) // 2) as half:
                body(half * 2 + 2, 0)
                body(half * 2 + 3, 1)
            body(PAIRS - 2, 0)
            body(PAIRS - 1, 1, maps=False)
            body(PAIRS, 0, maps=False, last=True)
            for _ in finish(PAIRS - 1, 1):
                pass


POINT = np.linspace(-1.0, 1.0, QR, dtype=np.float32)
PIXEL = (POINT + np.float32(1)) * np.float32(0.5) * np.float32(W - 1)
QUERY_ROW = [int(min(math.floor(v), H - 2)) for v in PIXEL]
NCONST_INC = 16 * (5 + 8 + 16 + 8 + 6 + 8)


def shape_constants():
    frac = PIXEL - np.array(QUERY_ROW, np.float32)
    cols = np.zeros((W, QR), np.float32)
    for q in range(QR):
        cols[QUERY_ROW[q], q] = 1 - frac[q]
        cols[QUERY_ROW[q] + 1, q] = frac[q]
    interp = np.zeros((W, QR, 2, QR), np.float32)
    for q in range(QR):
        interp[:, q, 0] = cols * (1 - frac[q])
        interp[:, q, 1] = cols * frac[q]
    p = np.arange(128)
    ref = np.zeros((128, TILES, 2), np.float32)
    for t in range(TILES):
        ref[:, t, 0] = PIXEL[p % QR]
        ref[:, t, 1] = PIXEL[(128 // QR) * t + p // QR]
    return {
        "interp": interp.reshape(W, -1),
        "ref": ref.reshape(128, -1),
        "ident": np.eye(128, dtype=np.float32),
        "headmask": np.kron(np.eye(HEADS), np.ones((HD, HD))).astype(np.float32),
        "descend": np.broadcast_to(np.arange(E, 0, -1, dtype=np.float32), (128, E)).copy(),
    }


def kernel(**inputs):
    import concourse.bacc as bacc
    from concourse.bass_utils import run_bass_kernel_spmd

    a = {k: np.asarray(v) for k, v in inputs.items()}
    c = np.ascontiguousarray
    arrays = {"x": c(a["x"]).reshape(B * C, H * W)}
    arrays.update(shape_constants())
    arrays.update({
        "wqT": c(a["L0_tok_W_q"].T), "wkT": c(a["L0_tok_W_k"].T), "wvT": c(a["L0_tok_W_v"].T),
        "wo1": a["L0_tok_W_o1"], "bo1": a["L0_tok_b_o1"], "lng": a["L0_tok_ln_g"], "lnb": a["L0_tok_ln_b"],
        "wo2": a["L0_tok_W_o2"], "bo2": a["L0_tok_b_o2"],
        "wqkv": a["L0_attn_w_qkv"], "mk": c(a["L0_attn_mem_kv"][0]).reshape(HID, MEM),
        "mvT": c(a["L0_attn_mem_kv"][1].reshape(HID, MEM).T),
        "wout": a["L0_attn_w_out"], "bout": a["L0_attn_b_out"], "gout": a["L0_attn_g_out"], "gpre": a["L0_attn_g_pre"],
        "gatew": a["L0_ffn_gate_w"], "gateb": a["L0_ffn_gate_b"],
        "w1": c(a["L0_ffn_w1"].transpose(1, 0, 2)).reshape(C, E * F), "b1": c(a["L0_ffn_b1"]).reshape(E * F),
        "w2": c(a["L0_ffn_w2"].transpose(1, 0, 2)).reshape(F, E * C), "b2": a["L0_ffn_b2"],
        "gamma": a["L0_ffn_gamma"], "beta": a["L0_ffn_beta"],
    })
    nc = bacc.Bacc("TRN2", target_bir_lowering=False, num_devices=1)
    args = [nc.dram_tensor(f"{n}_dram", v.shape, mybir.dt.from_np(v.dtype), kind="ExternalInput").ap()
            for n, v in arrays.items()]
    corner_maps = [nc.dram_tensor(f"corner_map{b}", (2 * MAPROWS, W, 2 * C), FP32).ap() for b in range(2)]
    out = nc.dram_tensor("out_dram", (B, NQ, C), FP32, kind="ExternalOutput").ap()
    build(nc, *args, corner_maps, out)
    r = run_bass_kernel_spmd(nc, [{f"{n}_dram": c(v) for n, v in arrays.items()}], core_ids=[0])
    return r.results[0]["out_dram"]
```

```python
import math
from contextlib import ExitStack

import numpy as np
import concourse.bass as bass
from concourse import mybir
from concourse.alu_op_type import AluOpType as ALU

FP32 = mybir.dt.float32
I32 = mybir.dt.int32
ACT = mybir.ActivationFunctionType
AX = mybir.AxisListType.X

B, C, H, W = 32, 64, 128, 128
PAIRS = B // 2
DS = 4
QR = H // DS
NQ = QR * QR
TILES = NQ // 128
PT, DH = 8, 8
O1 = C // DS
CHUNKS, CROWS = 8, H // 8
QCOLS = NQ // CHUNKS
GROUPS = CROWS // 4
XA_USES = CHUNKS * (GROUPS + 1) + 5
CB_USES = 19
HEADS, HD, MEM = 4, 32, 4
HID = HEADS * HD
E, F = 16, 128
MAPROWS = H - 1
IMGROWS = MAPROWS * W
STORES = 16 * CHUNKS
QO = ((0, 3), (3, 3), (6, 2))
EPS = 1e-5
LN_SCALE = float(2 ** 18)
FLOOR = float(3 * 2 ** 22)
GSLOTS = 4
BIG = 3.0e38


def build(nc, x, interp, ref, ident, headmask, descend, wqT, wkT, wvT, wo1, bo1, lng, lnb, wo2, bo2,
          wqkv_in, mk_in, mvT_in, wout_in, bout_in, gout_in, gpre_in, gatew, gateb, w1_in, b1_in, w2_in, b2_in,
          gamma_in, beta_in, corner_maps, out):
    ctx = ExitStack()
    with ctx:
        def sb(name, shape, dt=FP32):
            return ctx.enter_context(nc.sbuf_tensor(name, shape, dt))

        def pb(name, cols):
            return ctx.enter_context(nc.psum_tensor(name, [128, cols], FP32))

        def sem(name):
            return ctx.enter_context(nc.semaphore(name))

        interp_sb = sb("interp_sb", [128, 2 * QR * QR])
        ref_sb = sb("ref_sb", [128, TILES * 2])
        id_sb = sb("id_sb", [128, 128])
        mask_sb = sb("mask_sb", [128, 128])
        desc_sb = sb("desc_sb", [128, E])
        wqo = sb("wqo", [128, 160])
        wkv = sb("wkv", [128, 256])
        wo2bd = sb("wo2bd", [128, 128])
        bo1_sb = sb("bo1_sb", [128, O1])
        lng_sb = sb("lng_sb", [128, O1])
        lnb_sb = sb("lnb_sb", [128, O1])
        bo2_sb = sb("bo2_sb", [128, 2 * PT])
        base = sb("base", [128, 2 * TILES, 2 * PT])
        gbase = sb("gbase", [128, 2 * TILES])
        wqkv = sb("wqkv", [C + 1, 3 * HID])
        gpre = sb("gpre", [C, 1])
        mk_sb = sb("mk_sb", [128, MEM])
        mkmax = sb("mkmax", [128, 1])
        mvT = sb("mvT", [MEM, HID + 1])
        wout = sb("wout", [HID, C])
        bout = sb("bout", [128, C])
        gout = sb("gout", [128, C])
        gate_aug = sb("gate_aug", [C + 1, E])
        w1 = sb("w1", [128, E // 2, F])
        w2 = sb("w2", [F, E * C])
        b2bd = sb("b2bd", [128, TILES * C])
        gamma = sb("gamma", [128, C])
        beta = sb("beta", [128, C])
        id2 = sb("id2", [128, C])

        img = [sb(f"img{b}", [128, CROWS * W]) for b in range(2)]
        rows = [sb(f"rows{b}", [128, 2, CROWS + 1, C]) for b in range(2)]
        qfT = sb("qfT", [128, NQ])

        q_sb = [sb(f"q_sb{b}", [128, 2, TILES, C]) for b in range(2)]
        o1 = sb("o1", [128, 2 * TILES, O1])
        oc = sb("oc", [128, 2 * TILES, O1])
        os_ = sb("os_", [128, 2 * TILES, O1])
        st16 = sb("st16", [128, 6, 2 * TILES])
        hT = sb("hT", [128, 256])
        px = o1[:, :, :].rearrange("p g (s a) -> p (g s) a", a=2)
        fl = oc[:, :, :].rearrange("p g (s a) -> p (g s) a", a=2)
        wt = sb("wt", [128, 2, 2 * TILES * PT, 2])
        idxf = sb("idxf", [128, 2 * TILES, PT])
        idx = [sb(f"idx{b}", [128, 2 * TILES, PT], I32) for b in range(2)]
        w4 = [sb(f"w4_{b}", [128, 2 * TILES * PT, 2, 2]) for b in range(2)]
        gath = [sb(f"gath{s}", [128, PT, 4 * C]) for s in range(GSLOTS)]
        samp = [sb(f"samp{b}", [128, PT * C]) for b in range(2)]
        sampT = [sb(f"sampT{b}", [128, PT * C]) for b in range(2)]
        prod = sb("prod", [128, PT * C])
        v_sb = [sb(f"v_sb{b}", [128, 4, PT * C]) for b in range(2)]
        sc = sb("sc", [128, 4, PT, DH])
        scm = sb("scm", [128, 4, 2, DH])
        h0 = [sb(f"h0_{j}", [128, TILES, C]) for j in range(2)]

        cen = sb("cen", [128, TILES, C])
        xln = sb("xln", [128, TILES, C])
        st8 = sb("st8", [128, 8, 2, TILES])
        xnT = sb("xnT", [C + 1, NQ])
        mx = sb("mx", [128, 2])
        d33 = sb("d33", [128, 33])
        emem = sb("emem", [MEM, HID])
        ek = sb("ek", [128, TILES, HID])
        va = sb("va", [128, TILES, HID + 1])
        qs = sb("qs", [128, TILES * HEADS, HD])
        xn = qs[:, 0:TILES * HEADS // 2, :].rearrange("p (t a) d -> p t (a d)", a=2)
        sq = qs[:, TILES * HEADS // 2:TILES * HEADS, :].rearrange("p (t a) d -> p t (a d)", a=2)
        qst = sb("qst", [128, 3, TILES * HEADS])
        qnT = sb("qnT", [128, NQ])
        cm = sb("cm", [128, 128])
        cmT = cen[:, 0:2, :].rearrange("p t c -> p (t c)")
        rs = sb("rs", [128, 1])
        ms = sb("ms", [128, C])
        lg = sb("lg", [128, 4, TILES, E])
        tk = sb("tk", [128, 8, TILES])
        h1 = [sb(f"h1_{j}", [128, TILES, C]) for j in range(2)]
        x2 = [sb(f"x2_{j}", [128, TILES, C]) for j in range(2)]
        x2one = [sb(f"x2one{j}", [128, TILES, C]) for j in range(2)]
        gates = [sb(f"gates{j}", [128, TILES, E]) for j in range(2)]
        gT = [sb(f"gT{j}", [128, 128]) for j in range(2)]

        xg = sb("xg", [128, E, C])
        xgT = sb("xgT", [128, E // 2, 128])
        hid = [sb(f"hid{b}", [128, 4, F]) for b in range(2)]
        yT = sb("yT", [128, 128])
        moe = sb("moe", [128, TILES, C])
        fst = sb("fst", [128, 6, TILES])
        fsq = sb("fsq", [128, TILES, C])
        outb = sb("outb", [128, TILES, C])

        xa = pb("xa", 512)
        st = pb("st", 512)
        kp = pb("kp", 512)
        vp = pb("vp", 512)
        cb = pb("cb", 512)
        hb = [pb(f"hb{b}", 512) for b in range(2)]
        yb = pb("yb", 512)

        consts_in = sem("consts_in")
        consts_ready = sem("consts_ready")
        xa_filled = sem("xa_filled")
        xa_emptied = sem("xa_emptied")
        seam_copied = sem("seam_copied")
        o1_sum = sem("o1_sum")
        o1_sq = sem("o1_sq")
        o1_var = sem("o1_var")
        o1_seed = sem("o1_seed")
        gelu_in = sem("gelu_in")
        gelu_exp = sem("gelu_exp")
        h_ready = sem("h_ready")
        idx_ready = sem("idx_ready")
        corners_weighed = sem("corners_weighed")
        columns_summed = sem("columns_summed")
        summed = sem("summed")
        sT_filled = sem("sT_filled")
        sT_taken = sem("sT_taken")
        k_filled = sem("k_filled")
        v_filled = sem("v_filled")
        k_used = sem("k_used")
        v_copied = sem("v_copied")
        score_ready = sem("score_ready")
        score_exp = sem("score_exp")
        av_read = sem("av_read")
        pool_step = sem("pool_step")
        cb_filled = sem("cb_filled")
        cb_emptied = sem("cb_emptied")
        cen_ready = sem("cen_ready")
        sq_done = sem("sq_done")
        var_ready = sem("var_ready")
        seed_ready = sem("seed_ready")
        xn_ready = sem("xn_ready")
        d33_ready = sem("d33_ready")
        qmax_done = sem("qmax_done")
        eq_done = sem("eq_done")
        qn_ready = sem("qn_ready")
        x2_ready = sem("x2_ready")
        x2one_ready = sem("x2one_ready")
        top_exp_in = sem("top_exp_in")
        top_exp = sem("top_exp")
        gates_ready = sem("gates_ready")
        xg_ready = sem("xg_ready")
        x_filled = sem("x_filled")
        x_taken = sem("x_taken")
        h_filled = sem("h_filled")
        h_relu = sem("h_relu")
        h_used = sem("h_used")
        yT_taken = sem("yT_taken")
        y_filled = sem("y_filled")
        y_taken = sem("y_taken")
        y_read = sem("y_read")
        f_cen = sem("f_cen")
        f_sq = sem("f_sq")
        f_var = sem("f_var")
        f_seed = sem("f_seed")
        out_ready = sem("out_ready")
        out_stored = sem("out_stored")
        dve_chain = sem("dve_chain")
        act_chain = sem("act_chain")
        sp_step = sem("sp_step")
        dve_step = sem("dve_step")
        stored = [sem(f"stored{b}") for b in range(2)]
        img_loaded = [sem(f"img_loaded{b}") for b in range(2)]
        gathered = [sem(f"gathered{s}") for s in range(GSLOTS)]
        block = ctx.enter_context(nc.Block())

        S2 = 2 * TILES

        def past(n, per, c):
            return not isinstance(n, int) or n * per + c > 0

        @block.sync
        def _(sp):
            count = [0]

            def const(dst, src):
                sp.dma_start(dst, src).then_inc(consts_in, 16)
                count[0] += 1

            sp.wait_ge(consts_ready, 1)
            const(id_sb[:, :], ident)
            for a in range(2):
                const(id2[a * C:(a + 1) * C, :], ident[0:C, 0:C])
            const(interp_sb[:, :], interp)
            const(ref_sb[:, :], ref)
            const(mask_sb[:, :], headmask)
            const(desc_sb[:, :], descend)
            for j in range(2):
                const(wqo[j * C:(j + 1) * C, j * C:(j + 1) * C], wqT)
                const(wqo[j * C:(j + 1) * C, 2 * C + j * O1:2 * C + (j + 1) * O1], wo1)
                const(wkv[j * C:(j + 1) * C, j * C:(j + 1) * C], wkT)
                const(wkv[j * C:(j + 1) * C, (2 + j) * C:(3 + j) * C], wvT)
            for t in range(TILES):
                const(wo2bd[t * O1:(t + 1) * O1, t * 16:(t + 1) * 16], wo2)
                const(b2bd[t * E:(t + 1) * E, t * C:(t + 1) * C], b2_in)
            for dst, src, n in ((bo1_sb, bo1, O1), (lng_sb, lng, O1), (lnb_sb, lnb, O1), (bo2_sb, bo2, 2 * PT),
                                (bout, bout_in, C), (gout, gout_in, C), (gamma, gamma_in, C), (beta, beta_in, C)):
                const(dst[:, :], src.rearrange("(a n) -> a n", a=1).to_broadcast([128, n]))
            for a in range(2):
                of = w1_in.rearrange("c (q a f) -> c q a f", a=2, f=F)
                const(w1[a * C:(a + 1) * C - 1, :, :], of[0:C - 1, :, a, :])
                const(w1[(a + 1) * C - 1:(a + 1) * C, :, :],
                      b1_in.rearrange("(o q a f) -> o q a f", o=1, a=2, f=F)[:, :, a, :])
                const(ek[a * C:(a + 1) * C - 1, :, :], of[C - 1:C, :, a, :].to_broadcast([C - 1, E // 2, F]))
            const(wqkv[0:C, :], wqkv_in)
            const(gpre[:, :], gpre_in.rearrange("(n a) -> n a", a=1))
            const(mk_sb[:, :], mk_in)
            const(mvT[:, 0:HID], mvT_in)
            const(wout[:, :], wout_in)
            const(gate_aug[0:C, :], gatew)
            const(gate_aug[C:C + 1, :], gateb.rearrange("(a n) -> a n", a=1))
            const(w2[:, :], w2_in)
            assert 16 * count[0] == NCONST_INC, count[0]

            def load(n, k):
                fill = (GROUPS + 1) * (k - 2) + GROUPS - (5 if k < 2 else 0)
                if past(n, XA_USES, fill):
                    sp.wait_ge(xa_filled, n * XA_USES + fill)
                    sp.sem_inc(sp_step, 1)
                sp.dma_start(img[k % 2][:, :],
                             x[bass.ds(n * 128, 128), k * CROWS * W:(k + 1) * CROWS * W]).then_inc(img_loaded[k % 2], 16)

            def store(n, par, k):
                sp.wait_ge(xa_emptied, n * XA_USES + (GROUPS + 1) * k + GROUPS)
                sp.sem_inc(sp_step, 1)
                if past(n, CHUNKS - 1, k):
                    sp.wait_ge(seam_copied, n * (CHUNKS - 1) + k)
                    sp.sem_inc(sp_step, 1)
                if k == 0:
                    if past(n, S2, -S2):
                        sp.wait_ge(summed, n * S2 - S2)
                        sp.sem_inc(sp_step, 1)
                first = 1 if k == 0 else 0
                for j in range(2):
                    src = rows[k % 2][:, j, first:CROWS + 1, :]
                    src = bass.AP(tensor=src.tensor, offset=(j * (CROWS + 1) + first) * C,
                                  ap=[[2 * (CROWS + 1) * C, 128], [C, CROWS - first], [1, 2 * C]])
                    y0 = k * CROWS - 1 + first
                    dst = corner_maps[par][j * MAPROWS + y0:j * MAPROWS + y0 + CROWS - first]
                    sp.dma_start(dst.rearrange("y x c -> x y c"), src).then_inc(stored[k % 2], 16)

            def store_out(i, j):
                sp.wait_ge(out_ready, i * 2 + j + 1)
                sp.sem_inc(sp_step, 1)
                sp.dma_start(out[bass.ds(i * 2 + j, 1)].rearrange("a (t p) c -> p (a t) c", p=128),
                             outb[:, :, :]).then_inc(out_stored, 16)

            def body(n, par, out1=True, out0=True):
                for k in range(CHUNKS):
                    load(n, k)
                    if k:
                        store(n, par, k - 1)
                    if k == 5 and out1:
                        store_out(n - 3, 1)
                store(n, par, CHUNKS - 1)
                if out0:
                    store_out(n - 2, 0)

            body(0, 0, out1=False, out0=False)
            body(1, 1, out1=False, out0=False)
            body(2, 0, out1=False)
            with sp.Fori(0, (PAIRS - 4) // 2) as half:
                body(half * 2 + 3, 1)
                body(half * 2 + 4, 0)
            body(PAIRS - 1, 1)
            for n, j in ((PAIRS - 3, 1), (PAIRS - 2, 0), (PAIRS - 2, 1), (PAIRS - 1, 0), (PAIRS - 1, 1)):
                store_out(n, j)
            sp.wait_ge(out_stored, 16 * 2 * PAIRS)
            for s in stored:
                sp.wait_ge(s, STORES * PAIRS)

        @block.gpsimd
        def _(pool):
            def gather(i, par, g):
                s = g % GSLOTS
                if past(i, S2, g + 1 - GSLOTS):
                    pool.wait_ge(summed, i * S2 + g + 1 - GSLOTS)
                    pool.sem_inc(pool_step, 1)
                for p in range(PT):
                    pool.indirect_dma_start(
                        gath[s][:, p, :], None, corner_maps[par].rearrange("y x c -> (y x) c"),
                        bass.IndirectOffsetOnAxis(idx[par][:, g, p:p + 1], 0)).then_inc(gathered[s], 16)

            def body(i, par):
                for s in stored:
                    pool.wait_ge(s, i * STORES + STORES)
                    pool.sem_inc(pool_step, 1)
                pool.wait_ge(idx_ready, i + 1)
                pool.sem_inc(pool_step, 1)
                for g in range(S2):
                    gather(i, par, g)

            body(0, 0)
            with pool.Fori(0, PAIRS // 2 - 1) as half:
                body(half * 2 + 1, 1)
                body(half * 2 + 2, 0)
            body(PAIRS - 1, 1)

        @block.tensor
        def _(pe):
            mm = nc.tensor.matmul

            def transpose(dst, src):
                return nc.tensor.transpose(dst, src, id_sb[:, :])

            def chunk(n, k):
                pe.wait_ge(img_loaded[k % 2], n * (8 * CHUNKS) + 16 * (k // 2 + 1))
                for g in range(GROUPS + 1):
                    u = (GROUPS + 1) * k + g
                    if past(n, XA_USES, u):
                        pe.wait_ge(xa_emptied, n * XA_USES + u)
                    if g < GROUPS:
                        for r in range(4):
                            y = 4 * g + r
                            last = transpose(xa[:, r * 128:(r + 1) * 128], img[k % 2][:, y * W:(y + 1) * W])
                    else:
                        for q in range(CROWS // DS):
                            qy = k * (CROWS // DS) + q
                            y0 = QUERY_ROW[qy] - k * CROWS
                            for j in range(2):
                                for r in range(2):
                                    last = mm(xa[j * C:(j + 1) * C, q * QR:(q + 1) * QR],
                                              rows[k % 2][:, j, 1 + y0 + r, :],
                                              interp_sb[:, (2 * qy + r) * QR:(2 * qy + r + 1) * QR],
                                              start=(r == 0), stop=(r == 1))
                    last.then_inc(xa_filled, 1)
                    yield

            def queries(n):
                u = XA_USES - 5
                for t0, nt in QO:
                    pe.wait_ge(xa_emptied, n * XA_USES + u)
                    for t in range(nt):
                        last = mm(xa[:, t * 160:(t + 1) * 160], qfT[:, (t0 + t) * 128:(t0 + t + 1) * 128],
                                  wqo[:, :], start=True, stop=True)
                    last.then_inc(xa_filled, 1)
                    u += 1
                    yield
                yield
                yield
                yield
                pe.wait_ge(h_ready, n + 1)
                for j in range(2):
                    last = transpose(xa[:, j * 128:(j + 1) * 128],
                                     os_[:, j * TILES:(j + 1) * TILES, :].rearrange("p t c -> p (t c)"))
                last.then_inc(xa_filled, 1)
                yield
                pe.wait_ge(xa_emptied, n * XA_USES + XA_USES - 1)
                for j in range(2):
                    last = mm(xa[:, j * 128:(j + 1) * 128], hT[:, j * 128:(j + 1) * 128], wo2bd[:, :], start=True, stop=True)
                last.then_inc(xa_filled, 1)

            def sample_T(i, g, gated):
                pe.wait_ge(summed, i * S2 + g + 1)
                if gated and past(i, 2 * S2, 2 * (g - S2) + 2):
                    pe.wait_ge(x_taken, i * (2 * S2) + 2 * (g - S2) + 2)
                if past(i, S2, g):
                    pe.wait_ge(sT_taken, i * S2 + g)
                for q in range(4):
                    last = transpose(st[:, q * 128:(q + 1) * 128], samp[g % 2][:, q * 128:(q + 1) * 128])
                last.then_inc(sT_filled, 1)

            def sample_k(i, g):
                pe.wait_ge(sT_taken, i * S2 + g + 1)
                if past(i, S2, g):
                    pe.wait_ge(k_used, i * S2 + g)
                for q in range(4):
                    last = mm(kp[:, q * 128:(q + 1) * 128], sampT[g % 2][:, q * 128:(q + 1) * 128],
                              wkv[:, 0:128], start=True, stop=True)
                last.then_inc(k_filled, 1)

            def sample_v(i, g):
                if past(i, S2, g):
                    pe.wait_ge(v_copied, i * S2 + g)
                for q in range(4):
                    last = mm(vp[:, q * 128:(q + 1) * 128], sampT[g % 2][:, q * 128:(q + 1) * 128],
                              wkv[:, 128:256], start=True, stop=True)
                last.then_inc(v_filled, 1)

            def attention(i, j):
                f0 = i * (2 * CB_USES) + j * CB_USES
                yield
                yield
                yield
                yield
                pe.wait_ge(xn_ready, i * 2 + j + 1)
                if past(i, 2 * CB_USES, j * CB_USES):
                    pe.wait_ge(cb_emptied, f0)
                for q in range(4):
                    last = transpose(cb[:, q * 128:(q + 1) * 128], xn[:, 2 * q:2 * q + 2, :].rearrange("p t c -> p (t c)"))
                last.then_inc(cb_filled, 1)
                yield
                yield
                for h in range(2):
                    pe.wait_ge(cb_emptied, f0 + 1 + h)
                    mm(cb[:, :], wqkv[0:C, HID:2 * HID], xnT[0:C, h * 512:(h + 1) * 512],
                       start=True, stop=True).then_inc(cb_filled, 1)
                    yield
                for h in range(2):
                    pe.wait_ge(cb_emptied, f0 + 3 + h)
                    for t in range(4 * h, 4 * h + 4):
                        last = mm(cb[:, (t % 4) * HID:(t % 4 + 1) * HID], xnT[:, t * 128:(t + 1) * 128], wqkv[:, 0:HID],
                                  start=True, stop=True)
                    last.then_inc(cb_filled, 1)
                    yield
                pe.wait_ge(d33_ready, i * 2 + j + 1)
                pe.wait_ge(cb_emptied, f0 + 5)
                mm(cb[0:33, 0:128], d33[:, :], id_sb[:, :], start=True, stop=True).then_inc(cb_filled, 1)
                yield
                for u in range(4):
                    pe.wait_ge(cb_emptied, f0 + 6 + u)
                    for t in range(2 * u, 2 * u + 2):
                        last = mm(cb[:, (t % 2) * 256:(t % 2 + 1) * 256], xnT[:, t * 128:(t + 1) * 128],
                                  wqkv[:, HID:3 * HID], start=True, stop=True)
                    last.then_inc(cb_filled, 1)
                    yield
                pe.wait_ge(qn_ready, i * 2 + j + 1)
                for h in range(2):
                    pe.wait_ge(cb_emptied, f0 + 10 + h)
                    for q in range(4):
                        t = 4 * h + q
                        last = transpose(cb[:, q * 128:(q + 1) * 128],
                                         qs[:, t * HEADS:(t + 1) * HEADS, :].rearrange("p h d -> p (h d)"))
                    last.then_inc(cb_filled, 1)
                    yield
                yield
                pe.wait_ge(cb_emptied, f0 + 12)
                for t in range(TILES):
                    mm(cb[:, 0:HID + 1], ek[:, t, :], va[:, t, :], start=(t == 0), stop=False)
                mm(cb[:, 0:HID + 1], emem[:, :], mvT[:, :], start=False, stop=True).then_inc(cb_filled, 1)
                yield
                yield
                pe.wait_ge(cb_emptied, f0 + 13)
                transpose(cb[:, 0:128], cmT[:, :]).then_inc(cb_filled, 1)
                yield
                pe.wait_ge(cb_emptied, f0 + 14)
                mm(cb[:, 0:C], cm[:, :], wout[:, :], start=True, stop=True).then_inc(cb_filled, 1)
                yield
                pe.wait_ge(cb_emptied, f0 + 15)
                for t in range(TILES):
                    last = mm(cb[:, t * C:(t + 1) * C], qnT[:, t * 128:(t + 1) * 128], ms[:, :], start=True, stop=True)
                last.then_inc(cb_filled, 1)
                yield
                yield
                yield
                yield
                yield
                yield
                yield
                yield
                pe.wait_ge(x2_ready, i * 2 + j + 1)
                pe.wait_ge(cb_emptied, f0 + 16)
                for q in range(4):
                    last = transpose(cb[:, q * 128:(q + 1) * 128],
                                     x2[j][:, 2 * q:2 * q + 2, :].rearrange("p t c -> p (t c)"))
                last.then_inc(cb_filled, 1)
                yield
                pe.wait_ge(cb_emptied, f0 + 17)
                for t in range(TILES):
                    last = mm(cb[:, t * E:(t + 1) * E], xnT[:, t * 128:(t + 1) * 128], gate_aug[:, :], start=True, stop=True)
                last.then_inc(cb_filled, 1)
                yield
                yield
                yield
                yield
                pe.wait_ge(gates_ready, i * 2 + j + 1)
                pe.wait_ge(cb_emptied, f0 + 18)
                transpose(cb[:, 0:128], gates[j][:, :, :].rearrange("p t e -> p (t e)")).then_inc(cb_filled, 1)

            def inputs_T(n, h):
                pe.wait_ge(xg_ready, n * 2 + h + 1)
                if past(n, 2, h):
                    pe.wait_ge(x_taken, n * 2 + h)
                for q in range(4):
                    last = transpose(st[:, q * 128:(q + 1) * 128],
                                     xg[:, 8 * h + 2 * q:8 * h + 2 * q + 2, :].rearrange("p e c -> p (e c)"))
                last.then_inc(x_filled, 1)

            def up(i, g, h):
                pe.wait_ge(x_taken, i * (2 * S2) + 2 * g + h + 1)
                if past(i, 4 * S2, 4 * g + 2 * h):
                    pe.wait_ge(h_relu, i * (4 * S2) + 4 * g + 2 * h)
                for n in range(4):
                    for a in range(2):
                        half = slice(a * C, (a + 1) * C)
                        last = mm(hb[a][:, n * F:(n + 1) * F], w1[half, 4 * h + n, :], xgT[half, 4 * h + n, :],
                                  start=True, stop=True)
                last.then_inc(h_filled, 1)

            def down(i, g, h):
                pe.wait_ge(h_relu, i * (4 * S2) + 4 * g + 2 * h + 2)
                if h == 0:
                    if past(i, S2, g):
                        pe.wait_ge(y_taken, i * S2 + g)
                for n in range(4):
                    for a in range(2):
                        e = 8 * h + 2 * n + a
                        last = mm(yb[a * C:(a + 1) * C, 0:128], w2[:, e * C:(e + 1) * C], hid[a][:, n, :],
                                  start=(h == 0 and n == 0), stop=(h == 1 and n == 3))
                last.then_inc(h_used, 1)

            def output(i, g):
                j, t = g // TILES, g % TILES
                pe.wait_ge(yT_taken, i * S2 + g + 1)
                if t == 0:
                    pe.wait_ge(cb_emptied, i * (2 * CB_USES) + (j + 1) * CB_USES)
                mm(yb[:, 128:128 + C], gT[j][:, :], b2bd[:, t * C:(t + 1) * C], start=True, stop=False)
                mm(yb[:, 128:128 + C], yT[:, :], id2[:, :], start=False, stop=True).then_inc(y_filled, 1)

            def body(i, first=False, second=False, maps=True, last=False):
                for g in range(S2):
                    if g == 0:
                        attn = iter(())
                    if g == 1:
                        attn = iter(()) if first else attention(i - 1, 1)
                    if g == TILES + 1:
                        attn = iter(()) if last else attention(i, 0)
                    if g == TILES:
                        side = queries(i + 1) if maps else iter(())
                    if g < TILES:
                        side = chunk(i + 1, g) if maps else iter(())
                    gated = not last or g < S2 - 1
                    gated = gated and (not first or g == S2 - 1)

                    if not last:
                        sample_T(i, g, not first)
                    if g < TILES:
                        next(side, None)
                    next(attn, None)
                    if not first:
                        up(i - 1, g, 0)
                    next(attn, None)
                    if g:
                        if not first:
                            output(i - 1, g - 1)
                    elif not (first or second):
                        output(i - 2, S2 - 1)
                    next(side, None)
                    if not last:
                        sample_k(i, g)
                    next(attn, None)
                    if gated:
                        inputs_T(i * S2 + (g + 1 - S2), 0)
                    next(attn, None)
                    if not first:
                        down(i - 1, g, 0)
                    if g < TILES:
                        next(side, None)
                    if not first:
                        up(i - 1, g, 1)
                    if not last:
                        sample_v(i, g)
                    next(attn, None)
                    next(side, None)
                    if gated:
                        inputs_T(i * S2 + (g + 1 - S2), 1)
                    if not first:
                        down(i - 1, g, 1)
                    next(attn, None)
                    if g < TILES:
                        next(side, None)
                    if g % TILES == TILES - 1:
                        for _ in attn:
                            pass
                        for _ in side:
                            pass

            pe.wait_ge(consts_in, NCONST_INC)
            pe.wait_ge(consts_ready, 2)
            for k in range(CHUNKS):
                for _ in chunk(0, k):
                    pass
            for _ in queries(0):
                pass
            body(0, first=True)
            body(1, second=True)
            with pe.Fori(2, PAIRS - 1) as i:
                body(i)
            body(PAIRS - 1, maps=False)
            body(PAIRS, maps=False, last=True)
            output(PAIRS - 1, S2 - 1)

        @block.scalar
        def _(act):
            chain = [0]

            def link(ins):
                chain[0] += 1
                ins.then_inc(act_chain, 1)
                act.wait_ge(act_chain, chain[0])

            def copy(dst, src):
                return nc.scalar.activation(dst, src, ACT.Copy)

            def square(dst, src):
                return nc.scalar.activation(dst, src, ACT.Square)

            def chunk(n, k):
                for g in range(GROUPS + 1):
                    u = (GROUPS + 1) * k + g
                    if g == 0:
                        if past(n, STORES, 32 * (k // 2)):
                            act.wait_ge(stored[k % 2], n * STORES + 32 * (k // 2))
                        if k:
                            act.wait_ge(xa_emptied, n * XA_USES + (GROUPS + 1) * k - 1)
                            copy(rows[k % 2][:, :, 0, :], rows[(k + 1) % 2][:, :, CROWS, :]).then_inc(seam_copied, 1)
                    act.wait_ge(xa_filled, n * XA_USES + u + 1)
                    if g < GROUPS:
                        copy(rows[k % 2][:, :, 1 + 4 * g:5 + 4 * g, :].rearrange("p j r c -> p r j c"),
                             xa[:, :].rearrange("p (r j c) -> p r j c", r=4, j=2)).then_inc(xa_emptied, 1)
                    else:
                        copy(qfT[:, k * QCOLS:(k + 1) * QCOLS], xa[:, 0:QCOLS]).then_inc(xa_emptied, 1)
                    yield

            def rsqrt_seed(src, tmp, dst, scale):
                link(nc.scalar.activation(tmp, src, ACT.Ln, scale=scale))
                return nc.scalar.activation(dst, tmp, ACT.Exp, scale=-0.5)

            def queries(n, par):
                u = XA_USES - 5
                if past(n, S2, -S2):
                    act.wait_ge(k_used, n * S2 - S2)
                for t0, nt in QO:
                    act.wait_ge(xa_filled, n * XA_USES + u + 1)
                    two = xa[:, 0:nt * 160].rearrange("p (t c) -> p t c", c=160)
                    nc.scalar.activation(q_sb[par][:, :, t0:t0 + nt, :].rearrange("p j t c -> p t j c"),
                                         two[:, :, 0:2 * C].rearrange("p t (j c) -> p t j c", j=2),
                                         ACT.Copy, scale=float(DH) ** -0.5)
                    copy(o1[:, :, :].rearrange("p (j t) c -> p t j c", j=2)[:, t0:t0 + nt, :, :],
                         two[:, :, 2 * C:160].rearrange("p t (j c) -> p t j c", j=2)).then_inc(xa_emptied, 1)
                    u += 1
                    yield
                act.wait_ge(o1_sum, n + 1)
                square(os_[:, :, :], oc[:, :, :]).then_inc(o1_sq, 1)
                yield
                act.wait_ge(o1_var, n + 1)
                rsqrt_seed(st16[:, 2, :], st16[:, 3, :], st16[:, 4, :], 1.0).then_inc(o1_seed, 1)
                yield
                act.wait_ge(gelu_in, n + 1)
                nc.scalar.activation(os_[:, :, :], os_[:, :, :], ACT.Exp,
                                     scale=-2.0 * math.sqrt(2.0 / math.pi)).then_inc(gelu_exp, 1)
                yield
                act.wait_ge(xa_filled, n * XA_USES + XA_USES - 1)
                copy(hT[:, :], xa[:, 0:256]).then_inc(xa_emptied, 1)
                yield
                act.wait_ge(xa_filled, n * XA_USES + XA_USES)
                nc.scalar.activation(px[:, :, :].rearrange("p n a -> p (n a)"), xa[:, 0:256],
                                     ACT.Copy, scale=4.0).then_inc(xa_emptied, 1)

            def sample_T(i, g):
                act.wait_ge(sT_filled, i * S2 + g + 1)
                if past(i, S2, g - 1):
                    act.wait_ge(v_filled, i * S2 + g - 1)
                copy(sampT[g % 2][:, :], st[:, :]).then_inc(sT_taken, 1)

            def sample_v(i, g):
                act.wait_ge(v_filled, i * S2 + g + 1)
                if past(i, 4, g // 4 - 1):
                    act.wait_ge(av_read, i * 4 + g // 4 - 1)
                copy(v_sb[(g // 4) % 2][:, g % 4, :], vp[:, :]).then_inc(v_copied, 1)

            def softmax_exp(i, q):
                act.wait_ge(score_ready, i * 4 + q + 1)
                nc.scalar.activation(sc[:, :, :, :], sc[:, :, :, :], ACT.Exp).then_inc(score_exp, 1)

            def attention(i, j):
                f0 = i * (2 * CB_USES) + j * CB_USES
                n3 = i * 6 + 3 * j
                yield
                act.wait_ge(cen_ready, n3 + 1)
                square(sq[:, :, :], cen[:, :, :]).then_inc(sq_done, 1)
                yield
                act.wait_ge(var_ready, n3 + 1)
                rsqrt_seed(st8[:, 0, :, :], st8[:, 1, :, :], st8[:, 2, :, :], LN_SCALE).then_inc(seed_ready, 1)
                yield
                yield
                act.wait_ge(cb_filled, f0 + 1)
                for par in range(2):
                    last = copy(xnT[0:C, :].rearrange("c (q a n) -> c q a n", a=2, n=128)[:, :, par, :],
                                cb[par * C:(par + 1) * C, :].rearrange("c (q n) -> c q n", n=128))
                last.then_inc(cb_emptied, 1)
                yield
                yield
                for h in range(2):
                    act.wait_ge(cb_filled, f0 + 2 + h)
                    copy(ek[:, 4 * h:4 * h + 4, :].rearrange("p t c -> p (t c)"), cb[:, :]).then_inc(cb_emptied, 1)
                    yield
                for h in range(2):
                    act.wait_ge(cb_filled, f0 + 4 + h)
                    copy(qs[:, h * 4 * HEADS:(h + 1) * 4 * HEADS, :].rearrange("p n d -> p (n d)"),
                         cb[:, :]).then_inc(cb_emptied, 1)
                    yield
                act.wait_ge(cb_filled, f0 + 6)
                nc.scalar.activation(emem[:, :], cb[0:MEM, 0:128], ACT.Exp)
                copy(wqkv[C:C + 1, HID:2 * HID], cb[32:33, 0:128]).then_inc(cb_emptied, 1)
                yield
                for u in range(4):
                    act.wait_ge(cb_filled, f0 + 7 + u)
                    two = cb[:, :].rearrange("p (t a c) -> p t a c", a=2, c=HID)
                    nc.scalar.activation(ek[:, 2 * u:2 * u + 2, :], two[:, :, 0, :], ACT.Exp)
                    copy(va[:, 2 * u:2 * u + 2, 0:HID], two[:, :, 1, :]).then_inc(cb_emptied, 1)
                    if u == 0:
                        act.wait_ge(qmax_done, i * 2 + j + 1)
                        nc.scalar.activation(qs[:, :, :], qs[:, :, :], ACT.Exp).then_inc(eq_done, 1)
                    yield
                for h in range(2):
                    act.wait_ge(cb_filled, f0 + 11 + h)
                    copy(qnT[:, h * 512:(h + 1) * 512], cb[:, :]).then_inc(cb_emptied, 1)
                    yield
                yield
                yield
                yield
                act.wait_ge(cb_filled, f0 + 14)
                nc.scalar.activation(cm[:, :], cb[:, 0:128], ACT.Copy, scale=float(HD) ** -0.5).then_inc(cb_emptied, 1)
                yield
                act.wait_ge(cb_filled, f0 + 15)
                copy(ms[:, :], cb[:, 0:C]).then_inc(cb_emptied, 1)
                yield
                yield
                act.wait_ge(cen_ready, n3 + 2)
                square(sq[:, :, :], cen[:, :, :]).then_inc(sq_done, 1)
                yield
                act.wait_ge(var_ready, n3 + 2)
                rsqrt_seed(st8[:, 3, 0, :], st8[:, 4, 0, :], st8[:, 5, 0, :], LN_SCALE).then_inc(seed_ready, 1)
                yield
                yield
                act.wait_ge(cen_ready, n3 + 3)
                square(sq[:, :, :], cen[:, :, :]).then_inc(sq_done, 1)
                yield
                act.wait_ge(var_ready, n3 + 3)
                rsqrt_seed(st8[:, 3, 1, :], st8[:, 4, 1, :], st8[:, 5, 1, :], LN_SCALE).then_inc(seed_ready, 1)
                yield
                yield
                yield
                act.wait_ge(cb_filled, f0 + 17)
                for par in range(2):
                    last = copy(xnT[0:C, :].rearrange("c (q a n) -> c q a n", a=2, n=128)[:, :, par, :],
                                cb[par * C:(par + 1) * C, :].rearrange("c (q n) -> c q n", n=128))
                last.then_inc(cb_emptied, 1)
                act.wait_ge(x2_ready, i * 2 + j + 1)
                copy(x2one[j][:, :, 0:C - 1], x2[j][:, :, 0:C - 1]).then_inc(x2one_ready, 1)
                yield
                act.wait_ge(cb_filled, f0 + 18)
                copy(lg[:, 2, :, :].rearrange("p t e -> p (t e)"), cb[:, 0:TILES * E]).then_inc(cb_emptied, 1)
                yield
                yield
                act.wait_ge(top_exp_in, i * 2 + j + 1)
                nc.scalar.activation(tk[:, 5, :], tk[:, 4, :], ACT.Exp).then_inc(top_exp, 1)
                yield
                yield
                act.wait_ge(cb_filled, f0 + 19)
                copy(gT[j][:, :], cb[:, 0:128]).then_inc(cb_emptied, 1)

            def inputs_T(n, h):
                act.wait_ge(x_filled, n * 2 + h + 1)
                copy(xgT[:, 4 * h:4 * h + 4, :].rearrange("p e n -> p (e n)"), st[:, :]).then_inc(x_taken, 1)

            def relu(i, g, h, a):
                if a == 0:
                    act.wait_ge(h_filled, i * (2 * S2) + 2 * g + h + 1)
                    if past(i, 2 * S2, 2 * g + h):
                        act.wait_ge(h_used, i * (2 * S2) + 2 * g + h)
                nc.scalar.activation(hid[a][:, :, :].rearrange("p n f -> p (n f)"), hb[a][:, :],
                                     ACT.Relu).then_inc(h_relu, 1)

            def outputs_T(i, g):
                act.wait_ge(h_used, i * (2 * S2) + 2 * g + 2)
                copy(yT[:, :], yb[:, 0:128]).then_inc(yT_taken, 1)

            def output(i, g):
                act.wait_ge(y_filled, i * S2 + g + 1)
                if g % TILES == 0:
                    if past(i, 2, g // TILES):
                        act.wait_ge(y_read, i * 2 + g // TILES)
                copy(moe[:, g % TILES, :], yb[:, 128:128 + C]).then_inc(y_taken, 1)

            def finish(i, j):
                yield
                yield
                act.wait_ge(f_cen, i * 2 + j + 1)
                square(fsq[:, :, :], outb[:, :, :]).then_inc(f_sq, 1)
                yield
                act.wait_ge(f_var, i * 2 + j + 1)
                rsqrt_seed(fst[:, 2, :], fst[:, 3, :], fst[:, 4, :], LN_SCALE).then_inc(f_seed, 1)

            def body(i, par, first=False, second=False, maps=True, last=False):
                for g in range(S2):
                    if g == 0:
                        attn = iter(())
                        fin = iter(()) if first or second else finish(i - 2, 1)
                    if g == 1:
                        attn = iter(()) if first else attention(i - 1, 1)
                    if g == TILES + 1:
                        attn = iter(()) if last else attention(i, 0)
                    if g == TILES:
                        side = queries(i + 1, 1 - par) if maps else iter(())
                        fin = iter(()) if first else finish(i - 1, 0)
                    if g < TILES:
                        side = chunk(i + 1, g) if maps else iter(())
                    gated = not last or g < S2 - 1
                    gated = gated and (not first or g == S2 - 1)

                    if not last:
                        sample_T(i, g)
                    done = (i - 1, g - 1) if g and not first else (i - 2, S2 - 1) if not (g or first or second) else None
                    if done:
                        outputs_T(*done)
                    if g < TILES:
                        next(side, None)
                    if g % 4 == 0:
                        if g and not last:
                            softmax_exp(i, g // 4 - 1)
                        if not g and not first:
                            softmax_exp(i - 1, 3)
                    next(attn, None)
                    if not first:
                        relu(i - 1, g, 0, 0)
                        relu(i - 1, g, 0, 1)
                    next(attn, None)
                    if done:
                        output(*done)
                    next(side, None)
                    next(attn, None)
                    if gated:
                        inputs_T(i * S2 + (g + 1 - S2), 0)
                    next(fin, None)
                    next(attn, None)
                    if g < TILES:
                        next(side, None)
                    if not first:
                        relu(i - 1, g, 1, 0)
                        relu(i - 1, g, 1, 1)
                    if not last:
                        sample_v(i, g)
                    next(attn, None)
                    next(side, None)
                    if gated:
                        inputs_T(i * S2 + (g + 1 - S2), 1)
                    next(fin, None)
                    next(attn, None)
                    if g < TILES:
                        next(side, None)
                    if g % TILES == TILES - 1:
                        for spread in (attn, side, fin):
                            for _ in spread:
                                pass
                act.sem_clear(act_chain)
                chain[0] = 0

            nc.scalar.preload_act_table_set("natural_log_exp_and_others")
            for k in range(CHUNKS):
                for _ in chunk(0, k):
                    pass
            for _ in queries(0, 0):
                pass
            body(0, 0, first=True)
            body(1, 1, second=True)
            with act.Fori(0, (PAIRS - 4) // 2) as half:
                body(half * 2 + 2, 0)
                body(half * 2 + 3, 1)
            body(PAIRS - 2, 0)
            body(PAIRS - 1, 1, maps=False)
            body(PAIRS, 0, maps=False, last=True)
            outputs_T(PAIRS - 1, S2 - 1)
            output(PAIRS - 1, S2 - 1)
            for _ in finish(PAIRS - 1, 1):
                pass

        @block.vector
        def _(dve):
            V = nc.vector
            chain = [0]
            END = "end of a step"

            def mark(ins):
                chain[0] += 1
                ins.then_inc(dve_chain, 1)
                return chain[0]

            def link(ins):
                last = mark(ins)
                yield
                dve.wait_ge(dve_chain, last)

            def step(*streams):
                streams = list(streams)
                while streams:
                    streams = [one for one in streams if next(one, END) is not END]

            def tt(out_, a, b, op):
                return V.tensor_tensor(out_, a, b, op)

            def bc(ap, n):
                return ap.unsqueeze(2).to_broadcast([ap.shape[0], ap.shape[1], n])

            def bc_mid(ap, n):
                return ap.unsqueeze(1).to_broadcast([ap.shape[0], n, ap.shape[1]])

            def centre(src, cen_, s, n, done):
                yield from link(V.reduce_sum(s, src, AX))
                V.scalar_tensor_tensor(cen_, bc(s, n), -1.0 / n, src, ALU.mult, ALU.add).then_inc(done, 1)

            def newton(r, seed, h, u, scale):
                yield from link(V.tensor_scalar(r, seed, scale ** 0.5, None, ALU.mult))
                yield from link(tt(u, r, r, ALU.mult))
                yield from link(tt(u, u, h, ALU.mult))
                yield from link(V.scalar_tensor_tensor(r, u, 1.5, r, ALU.add, ALU.mult))

            def queries(n, par):
                yield END
                yield END
                dve.wait_ge(xa_emptied, n * XA_USES + XA_USES - 2)
                yield from link(tt(o1[:, :, :], o1[:, :, :], bc_mid(bo1_sb[:, :], S2), ALU.add))
                yield from centre(o1[:, :, :], oc[:, :, :], st16[:, 0, :], O1, o1_sum)
                yield END
                dve.wait_ge(o1_sq, n + 1)
                yield from link(V.reduce_sum(st16[:, 1, :], os_[:, :, :], AX))
                V.tensor_scalar(st16[:, 2, :], st16[:, 1, :], 1.0 / O1, EPS, ALU.mult, ALU.add).then_inc(o1_var, 1)
                yield
                dve.wait_ge(o1_var, n + 1)
                yield from link(V.tensor_scalar(st16[:, 0, :], st16[:, 2, :], -0.5, None, ALU.mult))
                yield END
                dve.wait_ge(o1_seed, n + 1)
                yield from newton(st16[:, 5, :], st16[:, 4, :], st16[:, 0, :], st16[:, 1, :], 1.0)
                yield from link(tt(oc[:, :, :], oc[:, :, :], bc(st16[:, 5, :], O1), ALU.mult))
                yield from link(tt(oc[:, :, :], oc[:, :, :], bc_mid(lng_sb[:, :], S2), ALU.mult))
                yield from link(tt(oc[:, :, :], oc[:, :, :], bc_mid(lnb_sb[:, :], S2), ALU.add))
                yield from link(tt(os_[:, :, :], oc[:, :, :], oc[:, :, :], ALU.mult))
                yield from link(V.tensor_scalar(os_[:, :, :], os_[:, :, :], 0.044715, 1.0, ALU.mult, ALU.add))
                tt(os_[:, :, :], os_[:, :, :], oc[:, :, :], ALU.mult).then_inc(gelu_in, 1)
                yield END
                dve.wait_ge(gelu_exp, n + 1)
                yield from link(V.tensor_scalar(os_[:, :, :], os_[:, :, :], 1.0, None, ALU.add))
                yield from link(V.reciprocal(os_[:, :, :], os_[:, :, :]))
                tt(os_[:, :, :], os_[:, :, :], oc[:, :, :], ALU.mult).then_inc(h_ready, 1)
                yield END
                yield END
                dve.wait_ge(xa_emptied, n * XA_USES + XA_USES)
                yield from link(tt(px[:, :, :].rearrange("p n a -> p (n a)"), px[:, :, :].rearrange("p n a -> p (n a)"),
                        base[:, :, :].rearrange("p g c -> p (g c)"), ALU.add))
                yield from link(V.tensor_scalar(px[:, :, :], px[:, :, :], 0.0, float(W - 1), ALU.max, ALU.min))
                yield from link(V.tensor_scalar(fl[:, :, :], px[:, :, :], -0.5, FLOOR, ALU.add, ALU.add))
                yield from link(V.tensor_scalar(fl[:, :, :], fl[:, :, :], FLOOR, None, ALU.subtract))
                yield from link(V.scalar_tensor_tensor(idxf[:, :, :].rearrange("p g s -> p (g s)"), fl[:, :, 1], float(W), fl[:, :, 0],
                                            ALU.mult, ALU.add))
                tt(idx[par][:, :, :], idxf[:, :, :], bc(gbase[:, :], PT), ALU.add).then_inc(idx_ready, 1)
                yield END
                yield from link(tt(wt[:, 1, :, :], px[:, :, :], fl[:, :, :], ALU.subtract))
                yield from link(V.tensor_scalar(wt[:, 0, :, :], wt[:, 1, :, :], -1.0, 1.0, ALU.mult, ALU.add))
                for a in range(2):
                    for b in range(2):
                        last = mark(tt(w4[par][:, :, a, b], wt[:, a, :, 0], wt[:, b, :, 1], ALU.mult))
                dve.wait_ge(dve_chain, last)

            def weigh(i, par, g):
                t = g % S2
                G = gath[g % GSLOTS]
                dve.wait_ge(gathered[g % GSLOTS], i * (16 * PT * S2 // GSLOTS) + 16 * PT * (g // GSLOTS + 1))
                for p in range(0, PT, 2):
                    Gc = G[:, p:p + 2, :].rearrange("p s (k c) -> p (s k) c", c=C)
                    wg = w4[par][:, t * PT + p:t * PT + p + 2, :, :].rearrange("p s a b -> p (s a b)")
                    tt(Gc, Gc, bc(wg, C), ALU.mult).then_inc(corners_weighed, 1)
                    yield

            def sum_corners(i, g):
                G = gath[g % GSLOTS]
                dve.wait_ge(corners_weighed, (i * S2 + g + 1) * (PT // 2))
                tt(G[:, :, 0:2 * C], G[:, :, 0:2 * C], G[:, :, 2 * C:4 * C], ALU.add).then_inc(columns_summed, 1)
                yield
                if past(i, S2, g - 1):
                    dve.wait_ge(sT_filled, i * S2 + g - 1)
                dve.wait_ge(columns_summed, i * S2 + g + 1)
                tt(samp[g % 2][:, :].rearrange("p (s c) -> p s c", c=C), G[:, :, 0:C], G[:, :, C:2 * C],
                   ALU.add).then_inc(summed, 1)

            def scores(i, par, g):
                dve.wait_ge(k_filled, i * S2 + g + 1)
                j, t = g // TILES, g % TILES
                tt(prod[:, :].rearrange("p (s c) -> p s c", c=C),
                   kp[:, :].rearrange("p (s c) -> p s c", c=C),
                   bc_mid(q_sb[par][:, j, t, :], PT), ALU.mult).then_inc(k_used, 1)
                yield
                dve.wait_ge(k_used, i * S2 + g + 1)
                yield from link(V.reduce_sum(sc[:, g % 4, :, :].rearrange("p s h -> p (s h)"),
                                  prod[:, :].rearrange("p (n d) -> p n d", d=DH), AX))

            def by_point(a):
                return a.rearrange("p t s h -> p t h s")

            def attend_max(i, q):
                yield from link(V.reduce_max(scm[:, :, 0, :], by_point(sc[:, :, :, :]), AX))
                tt(sc[:, :, :, :], sc[:, :, :, :], scm[:, :, 0, :].unsqueeze(2).to_broadcast([128, 4, PT, DH]),
                   ALU.subtract).then_inc(score_ready, 1)

            def attend(i, q):
                dve.wait_ge(score_exp, i * 4 + q + 1)
                yield from link(V.reduce_sum(scm[:, :, 1, :], by_point(sc[:, :, :, :]), AX))
                yield from link(V.reciprocal(scm[:, :, 0, :], scm[:, :, 1, :]))
                yield from link(tt(sc[:, :, :, :], sc[:, :, :, :], scm[:, :, 0, :].unsqueeze(2).to_broadcast([128, 4, PT, DH]), ALU.mult))
                dve.wait_ge(v_copied, i * S2 + 4 * (q + 1))
                v = v_sb[q % 2][:, :, :].rearrange("p t (n d) -> p (t n) d", d=DH)
                yield from link(tt(v, v, bc(sc[:, :, :, :].rearrange("p t s h -> p (t s h)"), DH), ALU.mult))
                V.reduce_sum(h0[q // 2][:, (q % 2) * 4:(q % 2) * 4 + 4, :],
                             v_sb[q % 2][:, :, :].rearrange("p t (s c) -> p t c s", s=PT), AX).then_inc(av_read, 1)

            def attention(i, j):
                hj, h1j = h0[j][:, :, :], h1[j][:, :, :]
                f0 = i * (2 * CB_USES) + j * CB_USES
                n3 = i * 6 + 3 * j
                dve.wait_ge(av_read, i * 4 + 2 * j + 2)
                yield from centre(hj, cen[:, :, :], st8[:, 6, 0, :], C, cen_ready)
                yield END
                dve.wait_ge(sq_done, n3 + 1)
                yield from link(V.reduce_sum(st8[:, 6, 1, :], sq[:, :, :], AX))
                yield from link(V.tensor_scalar(st8[:, 0, 0, :], st8[:, 6, 1, :], 1.0 / C, EPS, ALU.mult, ALU.add))
                yield from link(V.reciprocal(st8[:, 7, 0, :], st8[:, 0, 0, :]))
                yield from link(tt(st8[:, 7, 0, :], st8[:, 7, 0, :], st8[:, 6, 1, :], ALU.mult))
                V.tensor_scalar(st8[:, 0, 1, :], st8[:, 7, 0, :], 1e-24, None, ALU.max).then_inc(var_ready, 1)
                yield
                dve.wait_ge(var_ready, n3 + 1)
                yield from link(V.tensor_scalar(st8[:, 6, :, :], st8[:, 0, :, :], -0.5, None, ALU.mult))
                yield END
                dve.wait_ge(seed_ready, n3 + 1)
                yield from newton(st8[:, 3, :, :], st8[:, 2, :, :], st8[:, 6, :, :], st8[:, 7, :, :], LN_SCALE)
                yield from link(tt(xln[:, :, :], cen[:, :, :], bc(st8[:, 3, 0, :], C), ALU.mult))
                tt(xn[:, :, :], xln[:, :, :], bc(st8[:, 3, 1, :], C), ALU.mult).then_inc(xn_ready, 1)
                yield END
                yield END
                yield END
                yield END
                yield END
                dve.wait_ge(cb_emptied, f0 + 3)
                yield from link(V.reduce_max(mx[:, 0:1], ek[:, :, :].rearrange("p t c -> p (t c)"), AX))
                yield from link(tt(mx[:, 1:2], mx[:, 0:1], mkmax[:, :], ALU.max))
                V.tensor_scalar(d33[:, 0:MEM], mk_sb[:, :], mx[:, 1:2], None, ALU.subtract)
                V.tensor_scalar(d33[:, 32:33], mx[:, 1:2], -1.0, None, ALU.mult).then_inc(d33_ready, 1)
                yield END
                yield END
                dve.wait_ge(cb_emptied, f0 + 5)
                yield from link(V.reduce_max(qst[:, 0, :], qs[:, :, :], AX))
                tt(qs[:, :, :], qs[:, :, :], bc(qst[:, 0, :], HD), ALU.subtract).then_inc(qmax_done, 1)
                yield END
                yield END
                dve.wait_ge(eq_done, i * 2 + j + 1)
                yield from link(V.reduce_sum(qst[:, 1, :], qs[:, :, :], AX))
                yield from link(V.reciprocal(qst[:, 2, :], qst[:, 1, :]))
                tt(qs[:, :, :], qs[:, :, :], bc(qst[:, 2, :], HD), ALU.mult).then_inc(qn_ready, 1)
                yield END
                for _ in range(5):
                    yield END
                yield END
                dve.wait_ge(cb_filled, f0 + 13)
                yield from link(V.reciprocal(rs[:, 0:1], cb[:, HID:HID + 1]))
                yield from link(V.tensor_scalar(cmT[:, :], cb[:, 0:HID], rs[:, 0:1], None, ALU.mult))
                tt(cmT[:, :], cmT[:, :], mask_sb[:, :], ALU.mult).then_inc(cb_emptied, 1)
                yield END
                for _ in range(3):
                    yield END
                dve.wait_ge(cb_filled, f0 + 16)
                tt(cen[:, :, :], cb[:, :].rearrange("p (t c) -> p t c", c=C), bc_mid(bout[:, :], TILES),
                   ALU.add).then_inc(cb_emptied, 1)
                dve.wait_ge(cb_emptied, f0 + 16)
                tt(xln[:, :, :], xln[:, :, :], hj, ALU.add).then_inc(cen_ready, 1)
                yield END
                dve.wait_ge(sq_done, n3 + 2)
                yield from link(V.reduce_sum(st8[:, 6, 0, :], sq[:, :, :], AX))
                V.tensor_scalar(st8[:, 3, 0, :], st8[:, 6, 0, :], 1e-24, None, ALU.max).then_inc(var_ready, 1)
                yield
                dve.wait_ge(var_ready, n3 + 2)
                yield from link(V.tensor_scalar(st8[:, 7, 0, :], st8[:, 3, 0, :], -0.5, None, ALU.mult))
                yield END
                yield from link(tt(cen[:, :, :], cen[:, :, :], bc_mid(gout[:, :], TILES), ALU.mult))
                dve.wait_ge(seed_ready, n3 + 2)
                yield from newton(st8[:, 6, 1, :], st8[:, 5, 0, :], st8[:, 7, 0, :], st8[:, 7, 1, :], LN_SCALE)
                yield from link(tt(cen[:, :, :], cen[:, :, :], bc(st8[:, 6, 1, :], C), ALU.mult))
                yield from link(tt(h1j, cen[:, :, :], xln[:, :, :], ALU.add))
                yield from centre(h1j, cen[:, :, :], st8[:, 6, 0, :], C, cen_ready)
                yield END
                yield END
                dve.wait_ge(sq_done, n3 + 3)
                yield from link(V.reduce_sum(st8[:, 6, 1, :], sq[:, :, :], AX))
                V.tensor_scalar(st8[:, 3, 1, :], st8[:, 6, 1, :], 1.0 / C, EPS, ALU.mult, ALU.add).then_inc(var_ready, 1)
                yield
                dve.wait_ge(var_ready, n3 + 3)
                yield from link(V.tensor_scalar(st8[:, 7, 0, :], st8[:, 3, 1, :], -0.5, None, ALU.mult))
                yield END
                dve.wait_ge(seed_ready, n3 + 3)
                yield from newton(st8[:, 6, 1, :], st8[:, 5, 1, :], st8[:, 7, 0, :], st8[:, 7, 1, :], LN_SCALE)
                tt(x2[j][:, :, :], cen[:, :, :], bc(st8[:, 6, 1, :], C), ALU.mult).then_inc(x2_ready, 1)
                yield END
                yield END
                yield END
                yield END
                dve.wait_ge(cb_emptied, f0 + 18)
                desc = bc_mid(desc_sb[:, :], TILES)

                def best(src, onehot, val, key):
                    yield from link(V.reduce_max(val, src, AX))
                    yield from link(tt(lg[:, 0, :, :], src, bc(val, E), ALU.is_equal))
                    yield from link(tt(lg[:, 0, :, :], lg[:, 0, :, :], desc, ALU.mult))
                    yield from link(V.reduce_max(key, lg[:, 0, :, :], AX))
                    yield from link(tt(onehot, lg[:, 0, :, :], bc(key, E), ALU.is_equal))

                yield from best(lg[:, 2, :, :], lg[:, 1, :, :], tk[:, 0, :], tk[:, 1, :])
                yield from link(V.scalar_tensor_tensor(lg[:, 2, :, :], lg[:, 1, :, :], -BIG, lg[:, 2, :, :], ALU.mult, ALU.add))
                yield from best(lg[:, 2, :, :], lg[:, 3, :, :], tk[:, 2, :], tk[:, 3, :])
                tt(tk[:, 4, :], tk[:, 2, :], tk[:, 0, :], ALU.subtract).then_inc(top_exp_in, 1)
                yield END
                yield END
                dve.wait_ge(top_exp, i * 2 + j + 1)
                yield from link(V.tensor_scalar(tk[:, 6, :], tk[:, 5, :], 1.0, None, ALU.add))
                yield from link(V.reciprocal(tk[:, 6, :], tk[:, 6, :]))
                yield from link(tt(tk[:, 7, :], tk[:, 5, :], tk[:, 6, :], ALU.mult))
                yield from link(tt(lg[:, 1, :, :], lg[:, 1, :, :], bc(tk[:, 6, :], E), ALU.mult))
                yield from link(tt(lg[:, 3, :, :], lg[:, 3, :, :], bc(tk[:, 7, :], E), ALU.mult))
                tt(gates[j][:, :, :], lg[:, 1, :, :], lg[:, 3, :, :], ALU.add).then_inc(gates_ready, 1)
                yield
                dve.wait_ge(gates_ready, i * 2 + j + 1)
                yield END
                yield END

            def gate_inputs(i, g):
                j, t = (g % S2) // TILES, g % TILES
                n = i * S2 + g
                if t == 0:
                    dve.wait_ge(x2one_ready, i * 2 + g // TILES + 1)
                for h in range(2):
                    if past(i, 2 * S2, 2 * g + h - 1):
                        dve.wait_ge(x_filled, i * (2 * S2) + 2 * g + h - 1)
                    tt(xg[:, 8 * h:8 * h + 8, :], bc(gates[j][:, t, 8 * h:8 * h + 8], C), bc_mid(x2one[j][:, t, :], 8),
                       ALU.mult).then_inc(xg_ready, 1)
                    yield

            def finish(i, j):
                dve.wait_ge(y_taken, i * S2 + TILES * (j + 1))
                if past(i, 32, 16 * j):
                    dve.wait_ge(out_stored, i * 32 + 16 * j)
                tt(outb[:, :, :], x2[j][:, :, :], moe[:, :, :], ALU.add).then_inc(y_read, 1)
                yield END
                dve.wait_ge(y_read, i * 2 + j + 1)
                yield from centre(outb[:, :, :], outb[:, :, :], fst[:, 0, :], C, f_cen)
                yield END
                dve.wait_ge(f_sq, i * 2 + j + 1)
                yield from link(V.reduce_sum(fst[:, 1, :], fsq[:, :, :], AX))
                V.tensor_scalar(fst[:, 2, :], fst[:, 1, :], 1.0 / C, EPS, ALU.mult, ALU.add).then_inc(f_var, 1)
                yield
                dve.wait_ge(f_var, i * 2 + j + 1)
                yield from link(V.tensor_scalar(fst[:, 0, :], fst[:, 2, :], -0.5, None, ALU.mult))
                yield from link(tt(outb[:, :, :], outb[:, :, :], bc_mid(gamma[:, :], TILES), ALU.mult))
                yield END
                dve.wait_ge(f_seed, i * 2 + j + 1)
                yield from newton(fst[:, 5, :], fst[:, 4, :], fst[:, 0, :], fst[:, 1, :], LN_SCALE)
                yield from link(tt(outb[:, :, :], outb[:, :, :], bc(fst[:, 5, :], C), ALU.mult))
                yield END
                yield from link(tt(outb[:, :, :], outb[:, :, :], bc_mid(beta[:, :], TILES), ALU.add))
                tt(outb[:, :, :], outb[:, :, :], h1[j][:, :, :], ALU.add).then_inc(out_ready, 1)

            def body(i, par, first=False, second=False, maps=True, last=False):
                for g in range(S2):
                    if g == 0:
                        attn = iter(())
                        side = iter(())
                        fin = iter(()) if first or second else finish(i - 2, 1)
                    if g == 1:
                        attn = iter(()) if first else attention(i - 1, 1)
                    if g == TILES + 1:
                        attn = iter(()) if last else attention(i, 0)
                    if g == TILES:
                        side = queries(i + 1, 1 - par) if maps else iter(())
                        fin = iter(()) if first else finish(i - 1, 0)
                    gated = not last or g < S2 - 1
                    gated = gated and (not first or g == S2 - 1)
                    ahead = not last and (maps or g < S2 - 1)
                    npar = par if g < S2 - 1 else 1 - par

                    none = iter(())
                    samples = weigh(i, npar, g + 1) if ahead else none
                    step(gate_inputs(i - 1, g + 1) if gated else none, attn)
                    next(samples, None)
                    step(attn, samples)
                    step(attn)
                    samples = sum_corners(i, g + 1) if ahead else none
                    average = none
                    if g % 4 == 0:
                        if g and not last:
                            average = attend(i, g // 4 - 1)
                        if not g and not first:
                            average = attend(i - 1, 3)
                    step(side, fin, samples)
                    step(average, attn)
                    tile = scores(i, par, g) if not last else none
                    step(attn, tile)
                    tile = attend_max(i, g // 4) if g % 4 == 3 and not last else none
                    step(side, fin, attn, tile)
                    if g % TILES == TILES - 1:
                        for spread in (attn, side, fin):
                            for _ in spread:
                                pass
                if first:
                    dve.sem_inc(dve_step, 1)
                dve.sem_clear(dve_chain)
                chain[0] = 0

            def chained(ins):
                dve.wait_ge(dve_chain, mark(ins))

            for z in (wqo, wkv, wo2bd, b2bd, d33, wqkv):
                V.memset(z[:, :], 0.0)
            V.memset(ek[:, :, :], 0.0)
            V.memset(va[:, :, HID:HID + 1], 1.0)
            V.memset(mvT[:, HID:HID + 1], 1.0)
            V.memset(xnT[C:C + 1, :], 1.0)
            for j in range(2):
                V.memset(x2one[j][:, :, C - 1:C], 1.0)
                V.memset(gbase[:, j * TILES:(j + 1) * TILES], float(j * IMGROWS))
            chained(V.memset(lg[:, :, :, :], 0.0))
            V.memset(outb[:, :, :], 0.0).then_inc(consts_ready, 1)
            dve.wait_ge(consts_in, NCONST_INC)
            for h in range(3):
                chained(V.tensor_scalar(wqkv[0:C, h * HID:(h + 1) * HID], wqkv[0:C, h * HID:(h + 1) * HID],
                                     gpre[:, 0:1], float(C) ** 0.5, ALU.mult, ALU.mult))
            chained(tt(w1[:, :, :], w1[:, :, :], ek[:, :, :], ALU.subtract))
            chained(V.tensor_scalar(gout[:, :], gout[:, :], float(C) ** 0.5, None, ALU.mult))
            chained(V.reduce_max(mkmax[:, :], mk_sb[:, :], AX))
            chained(V.tensor_scalar(bo2_sb[:, :], bo2_sb[:, :], 4.0, None, ALU.mult))
            for g in range(S2):
                t = g % TILES
                chained(tt(base[:, g, :].rearrange("p (s a) -> p s a", a=2),
                        bo2_sb[:, :].rearrange("p (s a) -> p s a", a=2),
                        bc_mid(ref_sb[:, 2 * t:2 * t + 2], PT), ALU.add))
            V.memset(outb[:, :, :], 0.0).then_inc(consts_ready, 1)
            dve.wait_ge(consts_ready, 2)
            for stream in (queries(0, 0), weigh(0, 0, 0), sum_corners(0, 0)):
                for _ in stream:
                    pass
            body(0, 0, first=True)
            body(1, 1, second=True)
            with dve.Fori(0, (PAIRS - 4) // 2) as half:
                body(half * 2 + 2, 0)
                body(half * 2 + 3, 1)
            body(PAIRS - 2, 0)
            body(PAIRS - 1, 1, maps=False)
            body(PAIRS, 0, maps=False, last=True)
            for _ in finish(PAIRS - 1, 1):
                pass


POINT = np.linspace(-1.0, 1.0, QR, dtype=np.float32)
PIXEL = (POINT + np.float32(1)) * np.float32(0.5) * np.float32(W - 1)
QUERY_ROW = [int(min(math.floor(v), H - 2)) for v in PIXEL]
NCONST_INC = 16 * (5 + 8 + 16 + 8 + 6 + 8 + 2)


def shape_constants():
    frac = PIXEL - np.array(QUERY_ROW, np.float32)
    cols = np.zeros((W, QR), np.float32)
    for q in range(QR):
        cols[QUERY_ROW[q], q] = 1 - frac[q]
        cols[QUERY_ROW[q] + 1, q] = frac[q]
    interp = np.zeros((W, QR, 2, QR), np.float32)
    for q in range(QR):
        interp[:, q, 0] = cols * (1 - frac[q])
        interp[:, q, 1] = cols * frac[q]
    p = np.arange(128)
    ref = np.zeros((128, TILES, 2), np.float32)
    for t in range(TILES):
        ref[:, t, 0] = PIXEL[p % QR]
        ref[:, t, 1] = PIXEL[(128 // QR) * t + p // QR]
    return {
        "interp": interp.reshape(W, -1),
        "ref": ref.reshape(128, -1),
        "ident": np.eye(128, dtype=np.float32),
        "headmask": np.kron(np.eye(HEADS), np.ones((HD, HD))).astype(np.float32),
        "descend": np.broadcast_to(np.arange(E, 0, -1, dtype=np.float32), (128, E)).copy(),
    }


def kernel(**inputs):
    import concourse.bacc as bacc
    from concourse.bass_utils import run_bass_kernel_spmd

    a = {k: np.asarray(v) for k, v in inputs.items()}
    c = np.ascontiguousarray
    arrays = {"x": c(a["x"]).reshape(B * C, H * W)}
    arrays.update(shape_constants())
    arrays.update({
        "wqT": c(a["L0_tok_W_q"].T), "wkT": c(a["L0_tok_W_k"].T), "wvT": c(a["L0_tok_W_v"].T),
        "wo1": a["L0_tok_W_o1"], "bo1": a["L0_tok_b_o1"], "lng": a["L0_tok_ln_g"], "lnb": a["L0_tok_ln_b"],
        "wo2": a["L0_tok_W_o2"], "bo2": a["L0_tok_b_o2"],
        "wqkv": a["L0_attn_w_qkv"], "mk": c(a["L0_attn_mem_kv"][0]).reshape(HID, MEM),
        "mvT": c(a["L0_attn_mem_kv"][1].reshape(HID, MEM).T),
        "wout": a["L0_attn_w_out"], "bout": a["L0_attn_b_out"], "gout": a["L0_attn_g_out"], "gpre": a["L0_attn_g_pre"],
        "gatew": a["L0_ffn_gate_w"], "gateb": a["L0_ffn_gate_b"],
        "w1": c(a["L0_ffn_w1"].transpose(1, 0, 2)).reshape(C, E * F), "b1": c(a["L0_ffn_b1"]).reshape(E * F),
        "w2": c(a["L0_ffn_w2"].transpose(1, 0, 2)).reshape(F, E * C), "b2": a["L0_ffn_b2"],
        "gamma": a["L0_ffn_gamma"], "beta": a["L0_ffn_beta"],
    })
    nc = bacc.Bacc("TRN2", target_bir_lowering=False, num_devices=1)
    args = [nc.dram_tensor(f"{n}_dram", v.shape, mybir.dt.from_np(v.dtype), kind="ExternalInput").ap()
            for n, v in arrays.items()]
    corner_maps = [nc.dram_tensor(f"corner_map{b}", (2 * MAPROWS, W, 2 * C), FP32).ap() for b in range(2)]
    out = nc.dram_tensor("out_dram", (B, NQ, C), FP32, kind="ExternalOutput").ap()
    build(nc, *args, corner_maps, out)
    r = run_bass_kernel_spmd(nc, [{f"{n}_dram": c(v) for n, v in arrays.items()}], core_ids=[0])
    return r.results[0]["out_dram"]
```
